# Optimizing a Trainium2 kernel written in Bass

```python
import numpy as np
import jax
import jax.numpy as jnp

def _softmax(x, axis=-1):
    return jax.nn.softmax(x, axis=axis)

def _gelu(x):
    return jax.nn.gelu(x, approximate=True)

def _silu(x):
    return jax.nn.silu(x)

def _sigmoid(x):
    return jax.nn.sigmoid(x)

def _layernorm(x, axis=-1, eps=1e-05):
    m = jnp.mean(x, axis=axis, keepdims=True)
    v = jnp.var(x, axis=axis, keepdims=True)
    return (x - m) / jnp.sqrt(v + eps)

def _scatter_add(tgt, idx, src, axis=0):
    return tgt.at[idx].add(src)

def _segment_sum(src, seg, n):
    return jax.ops.segment_sum(src, seg, n)
kernel_name = 'mk_early_fusion_d1_tok_img768_r4_eb64e7'

def setup_inputs(seed: int=0):
    np.random.seed(seed)
    _w = jnp.asarray

    def _rec_inputs():
        import jax
        import jax.numpy as jnp
        _rk = jax.random.key(seed)
        x = -9.30917e-05 + 1.0002 * jax.random.normal(jax.random.fold_in(_rk, 1), (32, 3, 64, 64), jnp.float32)
        txt = -0.000192023 + 1.00029 * jax.random.normal(jax.random.fold_in(_rk, 2), (32, 128, 192), jnp.float32)
        return (x, txt)
    x, txt = _rec_inputs()

    def _L0_tok_setup():
        import jax, jax.numpy as jnp
        import numpy as np
        PATCH = 16
        EPS = 1e-05

        def _shift(x, pad_spec):
            l, r, t, b = pad_spec
            H, W = (x.shape[2], x.shape[3])
            xp = jnp.pad(x, ((0, 0), (0, 0), (max(t, 0), max(b, 0)), (max(l, 0), max(r, 0))))
            h0 = -t if t < 0 else 0
            w0 = -l if l < 0 else 0
            return xp[:, :, h0:h0 + H, w0:w0 + W]
        key = jax.random.key(seed)
        k1, k2 = jax.random.split(key)
        B, C, H, Wd = (32, 3, 224, 224)
        patch_dim = PATCH * PATCH * 5 * C
        dim = 192
        x = jax.random.normal(k1, (B, C, H, Wd), dtype=jnp.float32)
        ln_gamma = jnp.ones((patch_dim,), dtype=jnp.float32)
        ln_beta = jnp.zeros((patch_dim,), dtype=jnp.float32)
        W = jax.random.normal(k2, (patch_dim, dim), dtype=jnp.float32) * patch_dim ** (-0.5)
        b = jnp.zeros((dim,), dtype=jnp.float32)
        return {'x': x, 'ln_gamma': ln_gamma, 'ln_beta': ln_beta, 'W': W, 'b': b}
    _L0_tok_all = _L0_tok_setup()
    _L0_tok_in = {k: v for k, v in _L0_tok_all.items() if k in ('ln_gamma', 'ln_beta', 'W', 'b')}
    del _L0_tok_all

    def _L0_attn_setup():
        import math
        import jax, jax.numpy as jnp
        import numpy as np
        H, D_MODEL, D_K, D_V, SEQ, BATCH = (12, 192, 64, 64, 512, 4)
        key = jax.random.key(seed)
        k1, k2, k3, k4, k5 = jax.random.split(key, 5)
        s = math.sqrt(0.02)
        return {'residual': jax.random.normal(k1, (BATCH, SEQ, D_MODEL), dtype=jnp.float32), 'W_Q': jax.random.normal(k2, (H, D_MODEL, D_K), dtype=jnp.float32) * s, 'W_K': jax.random.normal(k3, (H, D_MODEL, D_K), dtype=jnp.float32) * s, 'W_V': jax.random.normal(k4, (H, D_MODEL, D_V), dtype=jnp.float32) * s, 'W_O': jax.random.normal(k5, (H * D_V, D_MODEL), dtype=jnp.float32) * s}
    _L0_attn_all = _L0_attn_setup()
    _L0_attn_in = {k: v for k, v in _L0_attn_all.items() if k in ('W_Q', 'W_K', 'W_V', 'W_O')}
    del _L0_attn_all

    def _L0_ffn_setup():
        import jax, jax.numpy as jnp
        import numpy as np
        B, S, D, H, E, K = (4, 512, 192, 768, 8, 2)
        CAP_FACTOR = 1.5

        def _moe_forward(x, Wr, w1, b1, w2, b2):
            Bz, Sz, Dz = x.shape
            Ez = Wr.shape[1]
            capacity = int(Bz * Sz / Ez * CAP_FACTOR)
            logits = x @ Wr
            probs = jax.nn.softmax(logits, axis=-1)
            topk_p, topk_i = jax.lax.top_k(probs, K)
            topk_p = topk_p / topk_p.sum(-1, keepdims=True)
            e_flat = topk_i.reshape(-1)
            p_flat = topk_p.reshape(-1)
            onehot = (e_flat[:, None] == jnp.arange(Ez)[None, :]).astype(x.dtype)
            counts_before = jnp.cumsum(onehot, axis=0) - onehot
            pos = jnp.take_along_axis(counts_before, e_flat[:, None], axis=1)[:, 0]
            keep = (pos < capacity).astype(x.dtype)
            cw = (onehot * (p_flat * keep)[:, None]).reshape(Bz, Sz, K, Ez).sum(2)
            hidden = jax.nn.gelu(jnp.einsum('bsd,edh->bseh', x, w1) + b1, approximate=False)
            expert_out = jnp.einsum('bseh,ehd->bsed', hidden, w2) + b2
            return jnp.einsum('bse,bsed->bsd', cw, expert_out)
        key = jax.random.key(seed)
        ks = jax.random.split(key, 6)
        x = jax.random.normal(ks[0], (B, S, D), jnp.float32)
        Wr = jax.random.normal(ks[1], (D, E), jnp.float32) * 0.01
        w1 = jax.random.normal(ks[2], (E, D, H), jnp.float32) * (1.0 / np.sqrt(D))
        b1 = jnp.zeros((E, H), jnp.float32)
        w2 = jax.random.normal(ks[3], (E, H, D), jnp.float32) * (1.0 / np.sqrt(H))
        b2 = jnp.zeros((E, D), jnp.float32)
        return {'x': x, 'Wr': Wr, 'w1': w1, 'b1': b1, 'w2': w2, 'b2': b2}
    _L0_ffn_all = _L0_ffn_setup()
    _L0_ffn_in = {k: v for k, v in _L0_ffn_all.items() if k in ('Wr', 'w1', 'b1', 'w2', 'b2')}
    del _L0_ffn_all
    return {'x': x, 'txt': txt, 'L0_tok_ln_gamma': _L0_tok_in['ln_gamma'], 'L0_tok_ln_beta': _L0_tok_in['ln_beta'], 'L0_tok_W': _L0_tok_in['W'], 'L0_tok_b': _L0_tok_in['b'], 'L0_attn_W_Q': _L0_attn_in['W_Q'], 'L0_attn_W_K': _L0_attn_in['W_K'], 'L0_attn_W_V': _L0_attn_in['W_V'], 'L0_attn_W_O': _L0_attn_in['W_O'], 'L0_ffn_Wr': _L0_ffn_in['Wr'], 'L0_ffn_w1': _L0_ffn_in['w1'], 'L0_ffn_b1': _L0_ffn_in['b1'], 'L0_ffn_w2': _L0_ffn_in['w2'], 'L0_ffn_b2': _L0_ffn_in['b2']}

def reference(x, txt, L0_tok_ln_gamma, L0_tok_ln_beta, L0_tok_W, L0_tok_b, L0_attn_W_Q, L0_attn_W_K, L0_attn_W_V, L0_attn_W_O, L0_ffn_Wr, L0_ffn_w1, L0_ffn_b1, L0_ffn_w2, L0_ffn_b2):
    import jax
    import jax.numpy as jnp

    def _L0_tok_ref(x, ln_gamma, ln_beta, W, b):
        import jax, jax.numpy as jnp
        import numpy as np
        PATCH = 16
        EPS = 1e-05

        def _shift(x, pad_spec):
            l, r, t, b = pad_spec
            H, W = (x.shape[2], x.shape[3])
            xp = jnp.pad(x, ((0, 0), (0, 0), (max(t, 0), max(b, 0)), (max(l, 0), max(r, 0))))
            h0 = -t if t < 0 else 0
            w0 = -l if l < 0 else 0
            return xp[:, :, h0:h0 + H, w0:w0 + W]
        shifts = [(1, -1, 0, 0), (-1, 1, 0, 0), (0, 0, 1, -1), (0, 0, -1, 1)]
        xs = jnp.concatenate([x] + [_shift(x, s) for s in shifts], axis=1)
        B, C5, H, Wd = xs.shape
        h, w = (H // PATCH, Wd // PATCH)
        t = xs.reshape(B, C5, h, PATCH, w, PATCH)
        t = t.transpose(0, 2, 4, 3, 5, 1)
        t = t.reshape(B, h * w, PATCH * PATCH * C5)
        mu = jnp.mean(t, axis=-1, keepdims=True)
        var = jnp.var(t, axis=-1, keepdims=True)
        tn = (t - mu) * jax.lax.rsqrt(var + EPS) * ln_gamma + ln_beta
        return jnp.einsum('bnp,pd->bnd', tn, W) + b

    def _L0_attn_ref(residual, W_Q, W_K, W_V, W_O):
        import math
        import jax, jax.numpy as jnp
        import numpy as np
        H, D_MODEL, D_K, D_V, SEQ, BATCH = (12, 192, 64, 64, 512, 4)
        B, S, _ = residual.shape
        Q = jnp.einsum('hmk,bsm->hbsk', W_Q, residual)
        K = jnp.einsum('hmk,bsm->hbsk', W_K, residual)
        V = jnp.einsum('hmv,bsm->hbsv', W_V, residual)
        QK = jnp.einsum('hbqk,hbsk->hbqs', Q, K)
        causal = jnp.triu(jnp.ones((S, S), dtype=bool), k=1)
        mask = jnp.where(causal, -jnp.inf, 0.0).astype(QK.dtype)
        soft = jax.nn.softmax((QK + mask) / math.sqrt(D_K), axis=-1)
        attn = jnp.einsum('hbqs,hbsv->hbqv', soft, V)
        multi_head = jnp.transpose(attn, (1, 2, 0, 3)).reshape(B, S, -1)
        return jnp.einsum('nd,bqn->bqd', W_O, multi_head)

    def _L0_ffn_ref(x, Wr, w1, b1, w2, b2):
        import jax, jax.numpy as jnp
        import numpy as np
        B, S, D, H, E, K = (4, 512, 192, 768, 8, 2)
        CAP_FACTOR = 1.5

        def _moe_forward(x, Wr, w1, b1, w2, b2):
            Bz, Sz, Dz = x.shape
            Ez = Wr.shape[1]
            capacity = int(Bz * Sz / Ez * CAP_FACTOR)
            logits = x @ Wr
            probs = jax.nn.softmax(logits, axis=-1)
            topk_p, topk_i = jax.lax.top_k(probs, K)
            topk_p = topk_p / topk_p.sum(-1, keepdims=True)
            e_flat = topk_i.reshape(-1)
            p_flat = topk_p.reshape(-1)
            onehot = (e_flat[:, None] == jnp.arange(Ez)[None, :]).astype(x.dtype)
            counts_before = jnp.cumsum(onehot, axis=0) - onehot
            pos = jnp.take_along_axis(counts_before, e_flat[:, None], axis=1)[:, 0]
            keep = (pos < capacity).astype(x.dtype)
            cw = (onehot * (p_flat * keep)[:, None]).reshape(Bz, Sz, K, Ez).sum(2)
            hidden = jax.nn.gelu(jnp.einsum('bsd,edh->bseh', x, w1) + b1, approximate=False)
            expert_out = jnp.einsum('bseh,ehd->bsed', hidden, w2) + b2
            return jnp.einsum('bse,bsed->bsd', cw, expert_out)
        return _moe_forward(x, Wr, w1, b1, w2, b2)
    h = _L0_tok_ref(x, L0_tok_ln_gamma, L0_tok_ln_beta, L0_tok_W, L0_tok_b)
    h = jnp.concatenate([h, txt], axis=1)
    h = h + _L0_attn_ref(_layernorm(h, axis=-1), L0_attn_W_Q, L0_attn_W_K, L0_attn_W_V, L0_attn_W_O)
    h = h + _L0_ffn_ref(_layernorm(h, axis=-1), L0_ffn_Wr, L0_ffn_w1, L0_ffn_b1, L0_ffn_w2, L0_ffn_b2)
    return h

_drawn_inputs = setup_inputs


def setup_inputs(seed=0):
    import zlib

    import numpy as np

    out = dict(_drawn_inputs(seed))
    spreads = {'L0_tok_ln_gamma': (1.0, 0.2),
     'L0_tok_ln_beta': (0.0, 0.1),
     'L0_tok_b': (0.0, 0.1),
     'L0_ffn_b1': (0.0, 0.8),
     'L0_ffn_b2': (0.0, 0.692)}
    factors = {}
    for name, (base, spread) in spreads.items():
        noise = np.random.default_rng([zlib.crc32(name.encode()), seed]).standard_normal(out[name].shape)
        drawn = base * np.exp(spread * noise) if base else spread * noise
        out[name] = jnp.asarray(drawn.astype(out[name].dtype))
    for name, factor in factors.items():
        out[name] = (out[name] * factor).astype(out[name].dtype)
    return out
```

```python
from contextlib import ExitStack

import concourse.bass as bass
from concourse import mybir

F32 = mybir.dt.float32
F16 = mybir.dt.float16
BF16 = mybir.dt.bfloat16
I32 = mybir.dt.int32
U32 = mybir.dt.uint32
ALU = mybir.AluOpType
ACT = mybir.ActivationFunctionType
X = mybir.AxisListType.X

P = 128
EPS = 1e-5
D = 192
NI, IT, TT = 32, 16, 128
SEQ = IT + TT
TOK = NI * SEQ
H, DH = 12, 64
HD = H * DH
NE, FF = 8, 768
CAP = int(TOK / NE * 1.5)
ROW = D + 2
XP = 18
WS = 64.0
QS = 8.0
RS = 1024.0
NPAIR_A = 2
NPAIR = NPAIR_A + NI // 2
UNITS = 8
KB = [[(0, 0, 128)], [(128, 0, 64), (0, 64, 64)], [(64, 0, 128)]]
BLK = [P] * (CAP // P) + ([CAP % P] if CAP % P else [])
NB = len(BLK)
FB = CAP // P
HALF = CAP // 2


def head_of(pos):
    g, r = divmod(pos, 3)
    return 6 * (g // 2) + g % 2 + 2 * r


def build(nc, x, txt, gam, bet, wemb, bemb, wq, wk, wv, wo, wr, w1, b1, w2, b2, out):
    himg_d = nc.dram_tensor("himg_d", (NI * IT, D), F32, kind="Internal").ap()
    vimg_d = nc.dram_tensor("vimg_d", (NI * IT, 2, HD), F16, kind="Internal").ap()
    xg_d = nc.dram_tensor("xg_d", (NE * CAP, ROW), I32, kind="Internal").ap()

    with ExitStack() as ctx:
        def sb(name, shape, dt, c=ctx):
            return c.enter_context(nc.sbuf_tensor(name, shape, dt))

        def sem(name):
            return ctx.enter_context(nc.semaphore(name))

        def ps(name, shape, dt):
            return ctx.enter_context(nc.psum_tensor(name, shape, dt))

        ident = sb("ident", [P, P], F16)
        identb = sb("identb", [P, P], BF16)
        maskt = sb("maskt", [P, 3, SEQ], BF16)
        maski = sb("maski", [P, 3, P], BF16)
        tri = sb("tri", [P, P], F16)
        ones = sb("ones", [P, P], F16)
        rowmask = sb("rowmask", [P, 8, P], F16)
        seli = sb("seli", [P, 8], F32)
        iota8 = sb("iota8", [P, NE], F32)
        zrow = sb("zrow", [P, NB, ROW], I32)
        zid = zrow[:, :, ROW - 1:ROW]
        halfc = sb("halfc", [P, 4], F32)
        wqkvh = sb("wqkvh", [P, 3, 3 * HD], F16)
        wqkvl = sb("wqkvl", [P, 2, 3 * HD], F16)
        woh = sb("woh", [P, 6, D], F16)
        wol = sb("wol", [P, 6, D], F16)
        wr32 = sb("wr32", [P, 3, NE], F32)
        wrh = sb("wrh", [P, 3, NE], F16)
        wrl = sb("wrl", [P, 2, NE], F16)
        b1t = sb("b1t", [P, NE * 6], F32)
        stage = sb("stage", [P, 2, 3 * FF + 6 * D], F32)

        pj = [ps(f"pj{i}", [P, 512], F32) for i in range(2)]
        sps = [ps(f"sps{i}", [P, 512], F32) for i in range(2)]
        ptp = [ps(f"ptp{i}", [P, 1024], F16) for i in range(2)]
        ops = ps("ops", [P, 512], F32)
        po = ps("po", [P, 512], F32)
        poh = po[:, :].bitcast(F16)
        pjh = [b[:, :].bitcast(F16) for b in pj]

        early = ExitStack()
        raw = sb("raw", [P, 3, XP, 64], F32, early)
        pad = sb("pad", [P, 3, XP, 66], F32, early)
        wst = sb("wst", [P, 2, 15, D], F32, early)
        wg = sb("wg", [P, 30, D], F32, early)
        weh = sb("weh", [P, 30, D], F16, early)
        wel = sb("wel", [P, 30, D], F16, early)
        b1r = sb("b1r", [NE * 6, P], F32, early)
        identf = sb("identf", [P, P], F32, early)
        gm = sb("gm", [P, 2, 15], F32, early)
        gm64 = sb("gm64", [P, 30], F32, early)
        bt = sb("bt", [P, 2, 15], F32, early)
        bb = sb("bb", [P, D], F32, early)
        cb = sb("cb", [P, D], F32, early)
        est = sb("est", [P, 4, 15, 6], F32, early)
        emv = sb("emv", [P, 4, 2], F32, early)
        eve = sb("eve", [P, 4], F32, early)
        ers = sb("ers", [P, 4], F32, early)
        nx = raw[:, :, :, :].rearrange("p c r w -> p (c r w)")[:, 0:9 * XP * 16].rearrange("p (s r c) -> p s r c", s=3, c=16)
        nxh = sb("nxh", [P, 2, 3, 3 * XP * 16], F16, early)
        nxl = sb("nxl", [P, 2, 3, 3 * XP * 16], F16, early)
        tte = sb("tte", [P, 60, P], F16, early)
        him = sb("him", [P, 4, D], F32, early)

        c_set = sem("c_set")
        ld_x = sem("ld_x")
        ld_we = sem("ld_we")
        ld_g = sem("ld_g")
        ld_w = [sem(f"ld_w{n}") for n in range(4)]
        sp_hi = sem("sp_hi")
        sp_lo = sem("sp_lo")
        ec = sem("ec")
        e_wg = sem("e_wg")
        e_wh = sem("e_wh")
        e_wl = sem("e_wl")
        e_beta = sem("e_beta")
        e_var = sem("e_var")
        e_rs = sem("e_rs")
        e_nx = sem("e_nx")
        e_hi = sem("e_hi")
        e_lo = sem("e_lo")
        e_tp = sem("e_tp")
        e_ta = sem("e_ta")
        e_td = sem("e_td")
        e_ps = sem("e_ps")
        e_him = sem("e_him")
        e_st = sem("e_st")
        pref = sem("pref")

        def load192(eng, dst, src, s):
            n = 0
            for b, parts in enumerate(KB):
                for r, p0, k in parts:
                    eng.dma_start(dst(b, p0, k), src(r, k)).then_inc(s, 16)
                    n += 1
            return n

        SPLITS = [(0, 0), (1, 1), (2, 0), (3, 1)]

        LDW = [16 * 6, 16 * 12, 16 * 6, 16 * (12 + 4)]

        def split_hi(a, n, what, place):
            a.wait_ge(ld_w[n], LDW[n])
            if what < 3:
                a.activation(wqkvh[:, what, 0:HD], stage[:, place, 0:HD], ACT.Copy, scale=QS)
                a.activation(wqkvh[:, what, HD:3 * HD], stage[:, place, HD:3 * HD], ACT.Copy, scale=WS).then_inc(sp_hi, 1)
            else:
                a.activation(wrh[:, :, :], wr32[:, :, :], ACT.Copy, scale=RS)
                a.activation(woh[:, :, :], stage[:, place, 0:6 * D].rearrange("p (c n) -> p c n", n=D),
                             ACT.Copy, scale=WS).then_inc(sp_hi, 1)

        def split_lo(v, n, what, place):
            v.wait_ge(ld_w[n], LDW[n])
            v.wait_ge(sp_hi, n + 1)
            if what < 2:
                v.scalar_tensor_tensor(wqkvl[:, what, 0:HD], stage[:, place, 0:HD], QS, wqkvh[:, what, 0:HD],
                                       ALU.mult, ALU.subtract)
                v.scalar_tensor_tensor(wqkvl[:, what, HD:3 * HD], stage[:, place, HD:3 * HD], WS,
                                       wqkvh[:, what, HD:3 * HD], ALU.mult, ALU.subtract).then_inc(sp_lo, 1)
            elif what == 3:
                v.scalar_tensor_tensor(wrl[:, :, :], wr32[:, 0:2, :], RS, wrh[:, 0:2, :], ALU.mult, ALU.subtract)
                v.scalar_tensor_tensor(wol[:, :, :], stage[:, place, 0:6 * D].rearrange("p (c n) -> p c n", n=D), WS,
                                       woh[:, :, :], ALU.mult, ALU.subtract).then_inc(sp_lo, 1)

        def evac_t(eng, w, odd):
            for q in range(odd, 8, 2):
                n = min(8, 60 - 8 * q)
                eng.wait_ge(e_tp, 8 * w + q + 1)
                if w and q == odd:
                    eng.wait_ge(e_ps, w)
                dst = tte[:, 8 * q:8 * q + n, :]
                src = ptp[odd][:, 0:n * P].rearrange("p (n q) -> p n q", n=n)
                if odd:
                    eng.tensor_copy(dst, src).then_inc(e_td, 1)
                else:
                    eng.activation(dst, src, ACT.Copy).then_inc(e_ta, 1)

        OFF = [(1, 1), (1, 0), (1, 2), (0, 1), (2, 1)]

        with nc.Block() as block:
            @block.sync
            def _(sp):
                xr = raw[:, :, :, :]
                sp.wait_ge(ec, 2)
                v = x.rearrange("b c h w -> b c (h w)")
                for hy in range(4):
                    a, b = max(16 * hy - 1, 0), min(16 * hy + 17, 64)
                    d0 = a - (16 * hy - 1)
                    sp.dma_start(xr[hy:P:4].rearrange("p c r w -> p c (r w)")[:, :, d0 * 64:(d0 + b - a) * 64],
                                 v[:, :, a * 64:b * 64]).then_inc(ld_x, 16)
                sp.dma_start(gm[:, :, :], gam.rearrange("(a q f) -> q a f", a=2, q=P)).then_inc(ld_g, 16)
                sp.dma_start(bt[:, :, :], bet.rearrange("(a q f) -> q a f", a=2, q=P)).then_inc(ld_g, 16)
                sp.dma_start(bb[:, :], bemb.rearrange("(o n) -> o n", o=1).broadcast_to((P, D))).then_inc(ld_g, 16)
                sp.dma_start(b1r[:, :], b1.rearrange("e (c p) -> (e c) p", p=P)).then_inc(ld_g, 16)
                wv_ = wemb.rearrange("(a q f) n -> q a (f n)", a=2, q=P)
                for a in range(2):
                    sp.dma_start(wst[:, a, :, :].rearrange("q f n -> q (f n)"), wv_[:, a, :]).then_inc(ld_we, 16)
                for lot, (what, place) in enumerate(SPLITS):
                    if what < 3:
                        if what == 2:
                            sp.wait_ge(sp_hi, 1)
                            sp.wait_ge(sp_lo, 1)
                        for r, p0, k in KB[what]:
                            for n, w in ((0, wq), (1, wk)):
                                sp.dma_start(stage[p0:p0 + k, place, n * HD:(n + 1) * HD].rearrange("p (h d) -> p h d", h=H),
                                             w[:, r:r + k, :].rearrange("h m d -> m h d")).then_inc(ld_w[lot], 16)
                            for g in range(4):
                                h0 = head_of(3 * g)
                                sp.dma_start(stage[p0:p0 + k, place, 2 * HD + g * D:2 * HD + (g + 1) * D]
                                             .rearrange("p (r d) -> p r d", r=3),
                                             wv[h0:h0 + 5:2, r:r + k, :].rearrange("h m d -> m h d")).then_inc(ld_w[lot], 16)
                    else:
                        sp.wait_ge(sp_hi, 2)
                        sp.wait_ge(sp_lo, 2)
                        for pos in range(H):
                            p0, h = 64 * (pos % 2), head_of(pos)
                            sp.dma_start(stage[p0:p0 + 64, 1, pos // 2 * D:(pos // 2 + 1) * D],
                                         wo[h * DH:(h + 1) * DH, :]).then_inc(ld_w[lot], 16)
                        load192(sp, lambda b, p0, k: wr32[p0:p0 + k, b, :], lambda r, k: wr[r:r + k, :], ld_w[lot])
                hv = himg_d.rearrange("(p w) n -> p w n", w=4)
                sp.wait_ge(e_him, 4)
                sp.dma_start(hv, him[:, :, :]).then_inc(e_st, 16)
                sp.wait_ge(e_st, 16)

            @block.gpsimd
            def _(g):
                g.memset(ident[:, :], 0.0).then_inc(c_set, 1)
                g.memset(identb[:, :], 0.0).then_inc(c_set, 1)
                g.memset(maskt[:, :, :], 0.0).then_inc(c_set, 1)
                g.memset(maski[:, :, :], 0.0).then_inc(c_set, 1)
                g.memset(tri[:, :], 1.0).then_inc(c_set, 1)
                g.memset(ones[:, :], 1.0).then_inc(c_set, 1)
                g.memset(rowmask[:, :, :], 1.0).then_inc(c_set, 1)
                g.memset(seli[:, :], 1.0).then_inc(c_set, 1)
                g.memset(zrow[:, :, :], 0).then_inc(c_set, 1)
                g.memset(halfc[:, :], -0.5).then_inc(c_set, 1)
                g.memset(identf[:, :], 0.0).then_inc(c_set, 1)
                g.wait_ge(c_set, 11)
                for m in (ident, identb, identf):
                    g.affine_select(out=m[:, :], in_=m[:, :], compare_op=ALU.not_equal, fill=1.0, base=0,
                                    pattern=[[-1, P]], channel_multiplier=1).then_inc(c_set, 1)
                g.affine_select(out=maskt[:, :, :], in_=maskt[:, :, :], compare_op=ALU.is_ge, fill=-1e30, base=IT,
                                pattern=[[0, 3], [-1, SEQ]], channel_multiplier=1).then_inc(c_set, 1)
                g.affine_select(out=maski[:, :, :], in_=maski[:, :, :], compare_op=ALU.is_ge, fill=-1e30, base=0,
                                pattern=[[0, 3], [-1, P]], channel_multiplier=1).then_inc(c_set, 1)
                g.affine_select(out=tri[:, :], in_=tri[:, :], compare_op=ALU.is_gt, fill=0.0, base=0,
                                pattern=[[1, P]], channel_multiplier=-1).then_inc(c_set, 1)
                g.affine_select(out=rowmask[:, :, :], in_=rowmask[:, :, :], compare_op=ALU.is_gt, fill=0.0, base=IT,
                                pattern=[[IT, 8], [0, P]], channel_multiplier=-1).then_inc(c_set, 1)
                g.affine_select(out=seli[:, :], in_=seli[:, :], compare_op=ALU.is_gt, fill=0.0, base=IT,
                                pattern=[[IT, 8]], channel_multiplier=-1).then_inc(c_set, 1)
                g.iota(iota8[:, :], pattern=[[1, NE]], base=0, channel_multiplier=0,
                       allow_small_or_imprecise_dtypes=True).then_inc(c_set, 1)
                g.iota(zid, pattern=[[P, NB], [1, 1]], base=TOK, channel_multiplier=1).then_inc(c_set, 1)
                g.wait_ge(c_set, 21)
                g.affine_select(out=seli[:, :], in_=seli[:, :], compare_op=ALU.is_ge, fill=0.0, base=0,
                                pattern=[[-IT, 8]], channel_multiplier=1).then_inc(c_set, 1)
                for j in range(8):
                    g.affine_select(out=maski[:, :, j * IT:(j + 1) * IT], in_=maski[:, :, j * IT:(j + 1) * IT],
                                    compare_op=ALU.is_gt, fill=-1e30, base=(j + 1) * IT,
                                    pattern=[[0, 3], [0, IT]], channel_multiplier=-1).then_inc(c_set, 1)
                for e in range(NE):
                    g.dma_start(xg_d[e * CAP:e * CAP + FB * P, :].rearrange("(b p) n -> p b n", p=P), zrow[:, 0:FB, :]).then_inc(pref, 16)
                    g.dma_start(xg_d[e * CAP + FB * P:(e + 1) * CAP, :], zrow[0:CAP - FB * P, FB, :]).then_inc(pref, 16)
                zf = zrow[:, :, 0:D].bitcast(F32)
                g.dma_start(out[TOK:TOK + FB * P, :].rearrange("(b p) n -> p b n", p=P), zf[:, 0:FB, :]).then_inc(pref, 16)
                g.dma_start(out[TOK + FB * P:TOK + CAP, :], zf[0:CAP - FB * P, FB, :]).then_inc(pref, 16)
                g.wait_ge(ld_g, 64)
                g.wait_ge(ld_we, 32)
                g.tensor_scalar(gm64[:, :], gm[:, :, :].rearrange("p a f -> p (a f)"), WS, None, ALU.mult).then_inc(e_wg, 1)
                g.wait_ge(e_wg, 1)
                for a in range(2):
                    g.tensor_tensor(wg[:, 15 * a:15 * a + 15, :], wst[:, a, :, :],
                                    gm64[:, 15 * a:15 * a + 15].unsqueeze(2).broadcast_to((P, 15, D)), ALU.mult).then_inc(e_wg, 1)
                g.wait_ge(e_var, 1)
                g.tensor_tensor(ers[:, :], eve[:, :], halfc[:, :], ALU.pow).then_inc(e_rs, 1)
                for w in range(4):
                    g.wait_ge(e_nx, w + 1)
                    g.wait_ge(e_hi, w + 1)
                    if w >= 2:
                        g.wait_ge(e_tp, 8 * (w - 1))
                    g.tensor_tensor(nxl[:, w % 2], nx[:, :, :, :].rearrange("p s r c -> p s (r c)"), nxh[:, w % 2], ALU.subtract).then_inc(e_lo, 1)
                g.wait_ge(pref, 16 * (2 * NE + 2))

            @block.scalar
            def _(a):
                for n, (what, place) in enumerate(SPLITS[:2]):
                    split_hi(a, n, what, place)
                for h in range(2):
                    a.wait_ge(e_wg, 2 + h)
                    a.activation(weh[:, 15 * h:15 * h + 15, :], wg[:, 15 * h:15 * h + 15, :], ACT.Copy).then_inc(e_wh, 1)
                for w in range(4):
                    a.wait_ge(e_nx, w + 1)
                    if w >= 2:
                        a.wait_ge(e_tp, 8 * (w - 1))
                    a.activation(nxh[:, w % 2], nx[:, :, :, :].rearrange("p s r c -> p s (r c)"), ACT.Copy).then_inc(e_hi, 1)
                    if w >= 1:
                        evac_t(a, w - 1, 0)
                    if w < 2:
                        split_hi(a, 2 + w, *SPLITS[2 + w])
                evac_t(a, 3, 0)

            @block.vector
            def _(v):
                v.memset(raw[:, :, 0, :], 0.0).then_inc(ec, 1)
                v.memset(raw[:, :, XP - 1, :], 0.0).then_inc(ec, 1)
                v.memset(pad[:, :, :, :], 0.0).then_inc(ec, 1)
                v.wait_ge(ec, 3)
                v.wait_ge(ld_x, 64)
                v.tensor_copy(pad[:, :, :, 1:65], raw[:, :, :, :]).then_inc(ec, 1)
                v.wait_ge(ec, 4)
                for w in range(4):
                    for s, (r0, c0) in enumerate(OFF):
                        for c in range(3):
                            last = v.bn_stats(est[:, w, 3 * s + c, :],
                                              pad[:, c, r0:r0 + 16, c0 + 16 * w:c0 + 16 * w + 16])
                    last.then_inc(ec, 1)
                v.wait_ge(ec, 8)
                for w in range(4):
                    v.bn_aggr(emv[:, w, :], est[:, w, :, :].rearrange("p a b -> p (a b)")).then_inc(ec, 1)
                v.wait_ge(ec, 12)
                v.tensor_scalar(eve[:, :], emv[:, :, 1], EPS, None, ALU.add).then_inc(e_var, 1)
                split_lo(v, 0, *SPLITS[0])
                split_lo(v, 1, *SPLITS[1])
                for h in range(2):
                    v.wait_ge(e_wh, h + 1)
                    v.tensor_tensor(wel[:, 15 * h:15 * h + 15, :], wg[:, 15 * h:15 * h + 15, :],
                                    weh[:, 15 * h:15 * h + 15, :], ALU.subtract).then_inc(e_wl, 1)
                v.wait_ge(e_beta, 1)
                v.tensor_tensor(cb[:, :], po[:, 0:D], bb[:, :], ALU.add).then_inc(ec, 1)
                v.wait_ge(e_beta, 2)
                v.tensor_copy(b1t[:, :], pj[0][:, 0:NE * 6])
                v.wait_ge(e_rs, 1)

                def window(w):
                    if w:
                        v.wait_ge(e_lo, w)
                        v.wait_ge(e_hi, w)
                    rows = pad[:, :, :, 16 * w:16 * w + 16].rearrange("p c r w -> p (c r) w")
                    shifted = bass.AP(tensor=rows.tensor, offset=rows.offset, ap=[rows.ap[0], [1, 3], rows.ap[1], rows.ap[2]])
                    v.tensor_scalar(nx[:, :, :, :], shifted, emv[:, w, 0:1], ers[:, w:w + 1],
                                    ALU.subtract, ALU.mult).then_inc(e_nx, 1)

                window(0)
                window(1)
                for w in range(4):
                    evac_t(v, w, 1)
                    if w < 2:
                        window(w + 2)
                    if w == 1:
                        split_lo(v, 3, *SPLITS[3])
                    v.wait_ge(e_ps, w + 1)
                    v.wait_ge(ec, 13)
                    v.scalar_tensor_tensor(him[:, w, :], ops[:, 0:D], 1.0 / WS, cb[:, :], ALU.mult, ALU.add).then_inc(e_him, 1)

            @block.tensor
            def _(pe):
                pe.wait_ge(ld_we, 32)
                pe.wait_ge(ld_g, 64)
                for n in range(30):
                    mm = pe.matmul(po[:, 0:D], bt[:, n // 15, n % 15:n % 15 + 1].broadcast_to((P, P)), wst[:, n // 15, n % 15, :],
                                   start=n == 0, stop=n == 29)
                mm.then_inc(e_beta, 1)
                pe.wait_ge(c_set, 30)
                pe.transpose(pj[0][:, 0:NE * 6], b1r[:, :], identf[0:NE * 6, 0:NE * 6]).then_inc(e_beta, 1)
                for w in range(4):
                    pe.wait_ge(e_hi, w + 1)
                    for q in range(8):
                        if q == 4:
                            pe.wait_ge(e_lo, w + 1)
                        k = 4 * w + q // 2
                        if k:
                            pe.wait_ge(e_td if q % 2 else e_ta, k)
                        for n in range(8 * q, min(8 * q + 8, 60)):
                            src = (nxh, nxl)[n // 30]
                            a, f = divmod(n % 30, 15)
                            s, c = divmod(f, 3)
                            r0, c0 = OFF[s]
                            at0 = (c * XP + r0 + 8 * a) * 16
                            mm = pe.transpose(ptp[q % 2][:, (n % 8) * P:(n % 8 + 1) * P],
                                              src[:, w % 2, c0, at0:at0 + P], ident[:, :])
                            if n == 29:
                                pe.wait_ge(e_lo, w + 1)
                        mm.then_inc(e_tp, 1)
                    if w == 0:
                        pe.wait_ge(e_wl, 2)
                    else:
                        pe.wait_ge(e_him, w)
                    pe.wait_ge(e_td, 4 * w + 4)
                    pe.wait_ge(e_ta, 4 * w + 4)
                    for n in range(30):
                        pe.matmul(ops[:, 0:D], tte[:, n, :], weh[:, n, :], start=n == 0, stop=False)
                        pe.matmul(ops[:, 0:D], tte[:, n, :], wel[:, n, :], start=False, stop=False)
                        mm = pe.matmul(ops[:, 0:D], tte[:, 30 + n, :], weh[:, n, :], start=False, stop=n == 29)
                    mm.then_inc(e_ps, 1)
        early.close()

        att = ExitStack()
        hin = sb("hin", [P, 2, 2, D], F32, att)
        hres = sb("hres", [P, 2, 2, D], F32, att)
        bst = sb("bst", [P, 2, 6], F32, att)
        mv = sb("mv", [P, 2, 2], F32, att)
        rstd = sb("rstd", [P, 2], F32, att)
        xn = sb("xn", [P, 2, D], F32, att)
        x16 = sb("x16", [P, 2, 2, 2 * D], F16, att)
        xt = sb("xt", [P, 2, 3, 2 * P], F16, att)
        qk = sb("qk", [P, 2, 2, 6, 2, 2, SEQ], F16, att)
        kimg = sb("kimg", [P, 2, 6, NI * IT], F16, att)
        v16 = sb("v16", [P, 2, 2, 2, HD], F16, att)
        vi = sb("vi", [P, 2, 2, 2, 4, 3, DH], F16, att)
        nm = sb("nm", [P, 2, 3], F32, att)
        p32 = sb("p32", [P, 2, 3, SEQ], F32, att)
        ph = sb("ph", [P, 2, 3, P], F16, att)
        pl = sb("pl", [P, 2, 3, P], F16, att)
        pi = sb("pi", [P, 2, 4, 2, IT], F16, att)
        pt = sb("pt", [P, 2, 7, P], F16, att)
        rs = sb("rs", [P, 2, 4, 3], F32, att)
        ri = sb("ri", [P, 6], F32, att)
        a32 = sb("a32", [P, 2, 6, DH], F32, att)
        a16 = sb("a16", [P, 2, 2, 2, HD], F16, att)
        at = sb("at", [P, 2, 2, 6, P], F16, att)
        h1 = sb("h1", [P, 2, D], F32, att)
        bst2 = sb("bst2", [P, 2, 6], F32, att)
        mv2 = sb("mv2", [P, 2, 2], F32, att)
        rstd2 = sb("rstd2", [P, 2], F32, att)
        xn2 = sb("xn2", [P, 2, D], F32, att)
        x2 = sb("x2", [P, 2, 2 * D], F16, att)
        x2t = sb("x2t", [P, 3, 2 * P], F16, att)
        lg = sb("lg", [P, 2, NE], F32, att)
        mx = sb("mx", [P, 2, 8], F32, att)
        mi = sb("mi", [P, 2, 8], U32, att)
        dl = sb("dl", [P, 2, 8], F32, att)
        exr = sb("exr", [P, 2, 8], F32, att)
        sm = sb("sm", [P, 8], F32, att)
        pk = sb("pk", [P, 2, 2], F32, att)
        wk2 = sb("wk2", [P, 2, 2], F32, att)
        ix = sb("ix", [P, 2, 2], F32, att)
        oh = sb("oh", [P, 2, 2, NE], F32, att)
        ma = sb("ma", [P, 4, NE], F16, att)
        mb = sb("mb", [P, 4, NE], F16, att)
        pos = sb("pos", [P, 2, NE], F32, att)
        ohp = sb("ohp", [P, 2, 2, NE], F32, att)
        pk2 = sb("pk2", [P, 2, 2], F32, att)
        sl = sb("sl", [P, 2, 2], F32, att)
        ov = sb("ov", [P, 2, 2], F32, att)
        sli = sb("sli", [P, 2, 2], I32, att)
        rows = sb("rows", [P, 2, 2, ROW], I32, att)
        tid = sb("tid", [P, 2], F32, att)
        tb = sb("tb", [P, (NI + 1) * NE], F32, att)
        ximg = sb("ximg", [P, 4, 2 * D], F16, att)
        wimg = sb("wimg", [P, 4, 2], F32, att)
        iximg = sb("iximg", [P, 4, 2], F32, att)
        ohimg = sb("ohimg", [P, 4, 2, NE], F32, att)
        mimg = sb("mimg", [P, 4, NE], F16, att)
        ipre = sb("ipre", [P, NI * NE], F32, att)
        cimg = sb("cimg", [P, 4, NE], F32, att)
        tidi = sb("tidi", [P, 4], F32, att)
        ppos = sb("ppos", [P, 4], F32, att)
        ppi = sb("ppi", [P, 8], F32, att)
        posa = sb("posa", [P, 4, NE], F32, att)
        ohpa = sb("ohpa", [P, 4, 2, NE], F32, att)
        pka = sb("pka", [P, 4, 2], F32, att)
        sla = sb("sla", [P, 4, 2], F32, att)
        ova = sb("ova", [P, 4, 2], F32, att)
        slia = sb("slia", [P, 4, 2], I32, att)
        selt = sb("selt", [P, 4, NE, 8], F32, att)

        names = """hin_ld hres_ld stat lnv rst xna xnh x16r xtp xte pjd pjh pjl sd mxd nmr exd phd phi pli pll ptd pta ptv pvd
            rid ond ash asl atp ate wod h1d st2 l2v l2r l2n l2h l2l x2p x2e rtd dld erd mhd cud sld rwd dsp outd vil vst
            kcp kic viz init chain pchain icp""".split()
        S = {n: sem(n) for n in names}

        def isb(p):
            return not isinstance(p, int) or p >= NPAIR_A

        def wait(eng, name, v):
            if isinstance(v, int) and v <= 0:
                return
            eng.wait_ge(S[name], v)
            if eng is nc.sync and not isinstance(v, int):
                fixed(eng)

        def fixed(eng):
            eng.nop(nofuse=True)

        class Chain:
            def __init__(self, name):
                self.name, self.n = name, 0

            def done(self, ins):
                ins.then_inc(S[self.name], 1)
                self.n = self.n + 1
                return ins

            def here(self, eng):
                eng.wait_ge(S[self.name], self.n)

        SLOTS = 11
        PROJ_AT = {0: 0, 1: 1, 2: 2, 3: 3, 4: 4, 5: 5, 6: 6, 7: 7, 8: 8, 9: 9, 10: 10}
        LAG_T, LAG_V = 2, 3

        def unit(u):
            return u // 4, u % 4

        def step_pe(pe, s, par, pro, attn, post):
            pp, pa, pq = s, s - 1, s - 2
            qpar, apar = par, 1 - par

            def item(k):
                if k == 0:
                    wait(pe, "x16r", pp + 1)
                    wait(pe, "pjl", 10 * pp)
                    for j in range(2):
                        for b in range(3):
                            mm = pe.transpose(pjh[0][:, (3 * j + b) * P:(3 * j + b + 1) * P],
                                              x16[:, qpar, j, b * P:(b + 1) * P], ident[:, :])
                    mm.then_inc(S["xtp"], 1)
                elif k < 7:
                    m, bank = k - 1, pj[k % 2]
                    wait(pe, "xte", pp + 1)
                    if k >= 3:
                        wait(pe, "pjl", 10 * pp + k - 2)
                    for t in range(2):
                        c = t * HD + m * P
                        for n, (w, b, e) in enumerate(TERMS):
                            mm = pe.matmul(bank[:, t * 256:(t + 1) * 256], (wqkvh, wqkvl)[w][:, b, c:c + P],
                                           xt[:, qpar, e, :], start=n == 0, stop=n == 4)
                    mm.then_inc(S["pjd"], 1)
                else:
                    j, hf = divmod(k - 7, 2)
                    bank = pj[k % 2]
                    wait(pe, "pjl", 10 * pp + k - 2)
                    c = 2 * HD + hf * 384
                    for n, (w, b, e) in enumerate(TERMS):
                        mm = pe.matmul(bank[:, 0:384], xt[:, qpar, e, j * P:(j + 1) * P],
                                       (wqkvh, wqkvl)[w][:, b, c:c + 384], start=n == 0, stop=n == 4)
                    mm.then_inc(S["pjd"], 1)

            for k in range(SLOTS):
                if attn and k < UNITS:
                    j, g = unit(k)
                    bank = sps[k % 2]
                    if k == 0:
                        wait(pe, "pjl", 10 * pa + 10)
                        if isb(pa):
                            wait(pe, "kic", 2 * (pa - 2) + 2)
                    wait(pe, "exd", 8 * pa + k - 1)
                    lo, n = (0, SEQ) if isb(pa) else (IT, P)
                    bk = bank[:, 0:3 * SEQ].rearrange("p (r c) -> p r c", r=3)[:, :, lo:SEQ]
                    pe.matmul(bk, identb[:, :], (maskt if isb(pa) else maski)[:, :, :], start=True, stop=False)
                    r0 = 64 * (g % 2)
                    for r in range(3):
                        m = 3 * (g // 2) + r
                        q = [qk[r0:r0 + 64, apar, z, m, 0, j, IT:SEQ] for z in range(2)]
                        kk = [qk[r0:r0 + 64, apar, z, m, 1, j, lo:SEQ] for z in range(2)]
                        o = bank[:, r * SEQ + lo:(r + 1) * SEQ]
                        pe.matmul(o, q[0], kk[0], start=False, stop=False)
                        pe.matmul(o, q[0], kk[1], start=False, stop=False)
                        mm = pe.matmul(o, q[1], kk[0], start=False, stop=r == 2)
                    mm.then_inc(S["sd"], 1)
                if pro and k in PROJ_AT:
                    item(PROJ_AT[k])
                if attn and LAG_T <= k < LAG_T + UNITS:
                    u = k - LAG_T
                    bank = ptp[u % 2]
                    wait(pe, "pll", 8 * pa + u + 1)
                    wait(pe, "ptv" if u % 2 else "pta", 4 * pa + u // 2)
                    for r in range(3):
                        pe.transpose(bank[:, r * P:(r + 1) * P], ph[:, u % 2, r, :], ident[:, :])
                        mm = pe.transpose(bank[:, (3 + r) * P:(4 + r) * P], pl[:, u % 2, r, :], ident[:, :])
                    if isb(pa):
                        mm = pe.transpose(bank[:, 6 * P:7 * P], pi[:, u % 2, :, :, :].rearrange("p r t c -> p (r t c)"),
                                          ident[:, :])
                    mm.then_inc(S["ptd"], 1)
                if post:
                    post_pe(pe, k, pq, 1 - apar)
                if attn and LAG_V <= k:
                    u = k - LAG_V
                    j, g = unit(u)
                    wait(pe, "ptv" if u % 2 else "pta", 4 * pa + u // 2 + 1)
                    if u % 2 == 0:
                        wait(pe, "ond", 4 * pa + u // 2)
                    if u == 0 and isb(pa):
                        wait(pe, "vil", 16 * 12 * (pa - 1))
                    z = u % 2 * 192
                    if isb(pa):
                        for w in range(2):
                            mm = pe.matmul(ops[:, z:z + 192], pt[:, u % 2, 6, :],
                                           vi[:, apar, j, w, g, :, :].rearrange("p r d -> p (r d)"), start=w == 0, stop=False)
                    for r in range(3):
                        o = ops[:, z + r * DH:z + (r + 1) * DH]
                        c = g * 192 + r * DH
                        st = not isb(pa)
                        pe.matmul(o, pt[:, u % 2, r, :], v16[:, apar, j, 0, c:c + DH], start=st, stop=False)
                        pe.matmul(o, pt[:, u % 2, r, :], v16[:, apar, j, 1, c:c + DH], start=False, stop=False)
                        mm = pe.matmul(o, pt[:, u % 2, 3 + r, :], v16[:, apar, j, 0, c:c + DH], start=False,
                                       stop=st or r == 2)
                    mm.then_inc(S["pvd"], 1)

        TERMS = [(0, 0, 0), (0, 1, 1), (0, 2, 2), (1, 0, 0), (1, 1, 1)]

        def post_pe(pe, k, p, par):
            if k < 4:
                j, z = divmod(k, 2)
                wait(pe, *(("sld", p) if k == 0 else ("ate", 4 * p + k)))
                wait(pe, "asl", 4 * p + 2 * j + 2)
                for c in range(6):
                    mm = pe.transpose(poh[:, c * P:(c + 1) * P], a16[:, par, j, z, c * P:(c + 1) * P], ident[:, :])
                mm.then_inc(S["atp"], 1)
            if k == 4:
                wait(pe, "ate", 4 * p + 4)
                for j in range(2):
                    n = 0
                    for c in range(6):
                        for z, w in ((0, woh), (0, wol), (1, woh)):
                            mm = pe.matmul(po[:, j * D:(j + 1) * D], at[:, j, z, c, :], w[:, c, :], start=n == 0, stop=n == 17)
                            n += 1
                mm.then_inc(S["wod"], 1)
            if k == 6:
                wait(pe, "h1d", p + 1)
                wait(pe, "l2l", p + 1)
                for j in range(2):
                    for b in range(3):
                        mm = pe.transpose(poh[:, (3 * j + b) * P:(3 * j + b + 1) * P], x2[:, j, b * P:(b + 1) * P], ident[:, :])
                mm.then_inc(S["x2p"], 1)
            if k == 8:
                wait(pe, "x2e", p + 1)
                for j in range(2):
                    for n, (w, b, e) in enumerate(TERMS):
                        mm = pe.matmul(po[:, j * NE:(j + 1) * NE], x2t[:, e, j * P:(j + 1) * P], (wrh, wrl)[w][:, b, :],
                                       start=n == 0, stop=n == 4)
                mm.then_inc(S["rtd"], 1)
            if k == 10:
                wait(pe, "mhd", p + 1)
                if isb(p):
                    pe.matmul(po[:, 0:32], tri[:, :], ma[:, :, :].rearrange("p a e -> p (a e)"), start=True, stop=False)
                    mm = pe.matmul(po[:, 0:32], ones[:, :], mb[:, :, :].rearrange("p a e -> p (a e)"), start=False, stop=True)
                elif p == 0:
                    mm = pe.matmul(po[:, 0:NE], ident[:, :], mimg[:, 0, :], start=True, stop=True)
                else:
                    im = mimg[:, :, :].rearrange("p t e -> p (t e)")
                    pe.matmul(po[:, 0:32], tri[:, :], im, start=True, stop=True)
                    for q in range(8):
                        mm = pe.matmul(po[:, 32 * (q + 1):32 * (q + 2)], rowmask[:, q, :], im, start=True, stop=True)
                mm.then_inc(S["cud"], 1)

        def step_dve(v, ch, s, par, pre, pro, attn, post, last):
            pp, pa, pq = s, s - 1, s - 2
            apar = 1 - par

            def norm(b):
                j, hb = divmod(b, 2)
                wait(v, "pvd", 8 * pa + 2 * b + 2)
                wait(v, "exd", 8 * pa + 2 * b + 2)
                wait(v, "asl", 4 * pa + b - 1)
                wait(v, "ond", 4 * pa + b)
                v.reciprocal(ri[:, :], rs[:, j, 2 * hb:2 * hb + 2, :].rearrange("p g r -> p (g r)")).then_inc(S["rid"], 1)
                wait(v, "rid", 4 * pa + b + 1)
                v.tensor_tensor(a32[:, b % 2, :, :], ops[:, 0:384].rearrange("p (h d) -> p h d", h=6),
                                ri[:, :].unsqueeze(2).broadcast_to((P, 6, DH)), ALU.mult).then_inc(S["ond"], 1)

            for k in range(SLOTS + 1):
                if attn and k >= 5 and k % 2 == 1:
                    norm((k - 5) // 2)
                if k == SLOTS:
                    break
                if attn and k < UNITS:
                    wait(v, "sd", 8 * pa + k + 1)
                    wait(v, "exd", 8 * pa + k - 1)
                    lo = 0 if isb(pa) else IT
                    v.tensor_reduce(nm[:, k % 2, :], sps[k % 2][:, 0:3 * SEQ].rearrange("p (r c) -> p r c", r=3)[:, :, lo:SEQ],
                                    X, ALU.max, negate=True).then_inc(S["mxd"], 1)
                if pro and k >= 1:
                    n = k - 1
                    wait(v, "pjh", 10 * pp + n + 1)
                    bank = pj[k % 2]
                    if k < 7:
                        v.scalar_tensor_tensor(qk[:, par, 1, n, :, :, IT:SEQ], bank[:, :].rearrange("p (t j c) -> p t j c", t=2, j=2),
                                               1.0 / WS, qk[:, par, 0, n, :, :, IT:SEQ], ALU.mult, ALU.subtract).then_inc(S["pjl"], 1)
                    else:
                        j, hf = divmod(k - 7, 2)
                        v.scalar_tensor_tensor(v16[:, par, j, 1, hf * 384:(hf + 1) * 384], bank[:, 0:384], 1.0 / WS,
                                               v16[:, par, j, 0, hf * 384:(hf + 1) * 384], ALU.mult, ALU.subtract).then_inc(S["pjl"], 1)
                if attn and 1 <= k <= UNITS:
                    u = k - 1
                    wait(v, "exd", 8 * pa + u + 1)
                    wait(v, "ptd", 8 * pa + u - 1)
                    v.tensor_copy(ph[:, u % 2, :, :], p32[:, u % 2, :, IT:SEQ]).then_inc(S["phd"], 1)
                    if isb(pa):
                        v.tensor_copy(pi[:, u % 2, 0:3, 0, :], p32[:, u % 2, :, 0:IT]).then_inc(S["phi"], 1)
                if attn and LAG_T <= k < LAG_T + UNITS and k % 2 == 1:
                    u = k - LAG_T
                    wait(v, "ptd", 8 * pa + u + 1)
                    wait(v, "pvd", 8 * pa + u - 1)
                    evac_pt(v.tensor_copy, pa, u).then_inc(S["ptv"], 1)
                if pre and k == 2:
                    p = s + 1
                    wait(v, "hin_ld", 16 * (p + 1))
                    wait(v, "xna", 2 * p)
                    for j in range(2):
                        ch.done(v.bn_stats(bst[:, j, :], hin[:, (par + 1) % 2, j, :]))
                    ch.here(v)
                    fixed(v)
                    for j in range(2):
                        v.bn_aggr(mv[:, j, :], bst[:, j, :]).then_inc(S["stat"], 1)
                if post:
                    post_dve(v, ch, k, pq)

        def evac_pt(f, pa, u):
            n = 7 if isb(pa) else 6
            return f(pt[:, u % 2, 0:n, :], ptp[u % 2][:, 0:n * P].rearrange("p (n c) -> p n c", n=n))

        def post_dve(v, ch, k, p):
            B = isb(p)
            if k == 4:
                wait(v, "wod", p + 1)
                wait(v, "hres_ld", 16 * (p + 1))
                wait(v, "outd", 32 * p)
                wait(v, "l2n", 2 * p)
                v.scalar_tensor_tensor(h1[:, :, :], po[:, 0:2 * D].rearrange("p (j n) -> p j n", j=2), 1.0 / WS, hres[:, p_par(p), :, :],
                                       ALU.mult, ALU.add).then_inc(S["h1d"], 1)
                wait(v, "h1d", p + 1)
                for j in range(2):
                    ch.done(v.bn_stats(bst2[:, j, :], h1[:, j, :]))
                ch.here(v)
                fixed(v)
                for j in range(2):
                    v.bn_aggr(mv2[:, j, :], bst2[:, j, :]).then_inc(S["st2"], 1)
            if k == 8:
                wait(v, "rtd", p + 1)
                wait(v, "erd", p)
                ch.done(v.tensor_scalar(lg[:, :, :], po[:, 0:2 * NE].rearrange("p (j e) -> p j e", j=2), 1.0 / RS, None, ALU.mult))
                ch.here(v)
                fixed(v)
                for j in range(2):
                    ch.done(v.max(mx[:, j, :], lg[:, j, :]))
                ch.here(v)
                fixed(v)
                for j in range(2):
                    ch.done(v.max_index(mi[:, j, :], mx[:, j, :], lg[:, j, :]))
                v.tensor_tensor(dl[:, :, :], mx[:, :, :], mx[:, :, 0:1].broadcast_to((P, 2, 8)), ALU.subtract).then_inc(S["dld"], 1)
                ch.here(v)
                t0 = 2 * p if not B else None
                oht = oh[:, :, :, :] if B else ohimg[:, t0:t0 + 2, :, :]
                ixt = ix[:, :, :] if B else iximg[:, t0:t0 + 2, :]
                ch.done(v.tensor_copy(ixt, mi[:, :, 0:2]))
                ch.here(v)
                ch.done(v.tensor_tensor(oht, iota8[:, :].unsqueeze(1).unsqueeze(1).broadcast_to((P, 2, 2, NE)),
                                        ixt.unsqueeze(3).broadcast_to((P, 2, 2, NE)), ALU.is_equal))
                ch.here(v)
                if B:
                    wait(v, "cud", p)
                    ch.done(v.tensor_tensor(ma[:, 0:2, :], oht[:, :, 0, :], oht[:, :, 1, :], ALU.add))
                    ch.here(v)
                    ch.done(v.tensor_copy(mb[:, 1:3, :], ma[:, 0:1, :].broadcast_to((P, 2, NE))))
                    v.tensor_tensor(mb[:, 3, :], ma[:, 0, :], ma[:, 1, :], ALU.add).then_inc(S["mhd"], 1)
                    ch.here(v)
                else:
                    v.tensor_tensor(mimg[:, t0:t0 + 2, :], oht[:, :, 0, :], oht[:, :, 1, :], ALU.add).then_inc(S["mhd"], 1)
            if k == 9:
                wait(v, "erd", p + 1)
                ch.done(v.tensor_reduce(sm[:, 0:2], exr[:, :, :], X, ALU.add))
                ch.here(v)
                ch.done(v.reciprocal(sm[:, 2:4], sm[:, 0:2]))
                ch.here(v)
                ch.done(v.tensor_tensor(pk[:, :, :], exr[:, :, 0:2], sm[:, 2:4].unsqueeze(2).broadcast_to((P, 2, 2)), ALU.mult))
                ch.here(v)
                ch.done(v.tensor_reduce(sm[:, 4:6], pk[:, :, :], X, ALU.add))
                ch.here(v)
                ch.done(v.reciprocal(sm[:, 6:8], sm[:, 4:6]))
                ch.here(v)
                if B:
                    wait(v, "rwd", p)
                wt = wk2[:, :, :] if B else wimg[:, 2 * p:2 * p + 2, :]
                ch.done(v.tensor_tensor(wt, pk[:, :, :], sm[:, 6:8].unsqueeze(2).broadcast_to((P, 2, 2)), ALU.mult))
            if k == 10:
                wait(v, "cud", p + 1)
                if B:
                    b0 = 2 * (p - 2)
                    cur = tb[:, bass.ds(b0 * NE, NE)].unsqueeze(1).broadcast_to((P, 2, NE))
                    c4 = po[:, 0:32].rearrange("p (a e) -> p a e", a=4)
                    ch.done(v.tensor_tensor(pos[:, :, :], c4[:, 0:2, :], cur, ALU.add))
                    ch.done(v.tensor_tensor(tb[:, bass.ds((b0 + 1) * NE, 2 * NE)].rearrange("p (a e) -> p a e", a=2), c4[:, 2:4, :], cur, ALU.add))
                    ch.here(v)
                    ch.done(v.tensor_tensor(pos[:, :, :], pos[:, :, :],
                                            ipre[:, bass.ds(b0 * NE, 2 * NE)].rearrange("p (a e) -> p a e", a=2), ALU.add))
                    ch.here(v)
                    slots(v, ch, ohp[:, :, :, :], oh[:, :, :, :], pos[:, :, :], pk2[:, :, :], sl[:, :, :], ov[:, :, :],
                          ix[:, :, :], sli[:, :, :], 2, "sld", p)
                elif p == 0:
                    v.tensor_copy(cimg[:, 0, :], po[:, 0:NE]).then_inc(S["sld"], 1)
                else:
                    lp = po[:, 32:288].rearrange("p (j t e) -> p t j e", j=8, t=4)
                    ip = ipre[:, :].rearrange("p (t j e) -> p t j e", t=4, j=8)
                    wait(v, "sld", 1)
                    ch.done(v.tensor_copy(ip, lp))
                    ch.done(v.tensor_copy(cimg[:, :, :], po[:, 0:32].rearrange("p (t e) -> p t e", t=4)))
                    for t in range(1, 4):
                        tot = ipre[:, (8 * t - 1) * NE:8 * t * NE]
                        ch.here(v)
                        ch.done(v.tensor_tensor(cimg[:, t, :], cimg[:, t, :], tot, ALU.add))
                        ch.done(v.tensor_tensor(ip[:, t], ip[:, t], tot.unsqueeze(1).broadcast_to((P, 8, NE)), ALU.add))
                    ch.here(v)
                    v.tensor_scalar(ppos[:, :], ppos[:, :], 1.0, None, ALU.mult).then_inc(S["sld"], 1)

        def slots(v, ch, ohp_, oh_, pos_, pk_, sl_, ov_, ix_, sli_, n, name, p):
            ch.done(v.tensor_tensor(ohp_, oh_, pos_.unsqueeze(2).broadcast_to((P, n, 2, NE)), ALU.mult))
            ch.here(v)
            ch.done(v.tensor_reduce(pk_, ohp_, X, ALU.add))
            ch.here(v)
            ch.done(v.scalar_tensor_tensor(sl_, ix_, float(CAP), pk_, ALU.mult, ALU.add))
            ch.done(v.tensor_scalar(ov_, pk_, float(CAP), 65536.0, ALU.is_ge, ALU.mult))
            ch.here(v)
            if p is not None:
                wait(v, "dsp", 64 * (p - 2))
            v.tensor_tensor(sli_, sl_, ov_, ALU.add).then_inc(S[name], 1)

        def p_par(p):
            return PAR[0]

        PAR = [0]

        def step_act(a, s, par, pro, attn, post):
            pp, pa, pq = s, s - 1, s - 2
            for k in range(SLOTS):
                if attn and k < UNITS:
                    j, g = unit(k)
                    wait(a, "mxd", 8 * pa + k + 1)
                    wait(a, "pll", 8 * pa + k - 1)
                    if k % 2 == 0:
                        wait(a, "rid", 4 * (pa - 1) + k // 2 + 1)
                    lo = 0 if isb(pa) else IT
                    for r in range(3):
                        i = a.activation(p32[:, k % 2, r, lo:SEQ], sps[k % 2][:, r * SEQ + lo:(r + 1) * SEQ], ACT.Exp,
                                         bias=nm[:, k % 2, r:r + 1], accum_out=rs[:, j, g, r:r + 1])
                    i.then_inc(S["exd"], 1)
                if pro and k == 0:
                    wait(a, "xtp", pp + 1)
                    a.activation(xt[:, par, :, :].rearrange("p b (j c) -> p j b c", j=2),
                                 pjh[0][:, 0:6 * P].rearrange("p (j b c) -> p j b c", j=2, b=3), ACT.Copy).then_inc(S["xte"], 1)
                if pro and k >= 1:
                    n = k - 1
                    wait(a, "pjd", 10 * pp + n + 1)
                    bank = pj[k % 2]
                    if k == 1:
                        wait(a, "sd", 8 * (pp - 1))
                        if isinstance(pp, int) and 2 <= pp < 4:
                            wait(a, "kcp", pp - 1)
                            wait(a, "vst", 32 * (pp - 1))
                    if k == 7:
                        wait(a, "pvd", 8 * (pp - 1))
                    if k < 7:
                        a.activation(qk[:, par, 0, n, :, :, IT:SEQ], bank[:, :].rearrange("p (t j c) -> p t j c", t=2, j=2),
                                     ACT.Copy, scale=1.0 / WS).then_inc(S["pjh"], 1)
                    else:
                        j, hf = divmod(k - 7, 2)
                        a.activation(v16[:, par, j, 0, hf * 384:(hf + 1) * 384], bank[:, 0:384], ACT.Copy,
                                     scale=1.0 / WS).then_inc(S["pjh"], 1)
                if attn and LAG_T <= k < LAG_T + UNITS and k % 2 == 0:
                    u = k - LAG_T
                    wait(a, "ptd", 8 * pa + u + 1)
                    wait(a, "pvd", 8 * pa + u - 1)
                    evac_pt(lambda o, i: a.activation(o, i, ACT.Copy), pa, u).then_inc(S["pta"], 1)
                if post:
                    p = pq
                    if k < 4:
                        j, z = divmod(k, 2)
                        wait(a, "atp", 4 * p + k + 1)
                        a.activation(at[:, j, z, :, :], poh[:, 0:6 * P].rearrange("p (c q) -> p c q", c=6), ACT.Copy).then_inc(S["ate"], 1)
                    if k == 6:
                        wait(a, "x2p", p + 1)
                        a.activation(x2t[:, :, :].rearrange("p b (j c) -> p j b c", j=2),
                                     poh[:, 0:6 * P].rearrange("p (j b c) -> p j b c", j=2, b=3), ACT.Copy).then_inc(S["x2e"], 1)
                    if k == 8:
                        wait(a, "dld", p + 1)
                        a.activation(exr[:, :, :], dl[:, :, :], ACT.Exp).then_inc(S["erd"], 1)

        def layernorm(g, c, h_, mv_, rstd_, xn_, x16_, var, names, p, guard):
            wait(g, var, 2 * p + 2)
            fixed(g)
            c.done(g.tensor_scalar(rstd_, mv_[:, :, 1], EPS, None, ALU.add))
            c.here(g)
            c.done(g.tensor_tensor(rstd_, rstd_, halfc[:, 0:2], ALU.pow))
            c.here(g)
            fixed(g)
            for j in range(2):
                g.tensor_scalar(xn_[:, j, :], h_[:, j, :], mv_[:, j, 0:1], rstd_[:, j:j + 1], ALU.subtract, ALU.mult).then_inc(S[names[0]], 1)
            wait(g, names[0], 2 * p + 2)
            guard()
            fixed(g)
            c.done(g.tensor_copy(x16_[:, :, 0:D], xn_))
            c.here(g)
            g.tensor_tensor(x16_[:, :, D:2 * D], xn_, x16_[:, :, 0:D], ALU.subtract).then_inc(S[names[1]], 1)
            wait(g, names[1], p + 1)

        def step_pool(g, c, s, par, pre, pro, attn, post):
            pp, pa, pq = s, s - 1, s - 2
            apar = 1 - par

            def split_a(b):
                j, hb = divmod(b, 2)
                wait(g, "ond", 4 * pa + b + 1)
                if b == 0:
                    wait(g, "atp", 4 * (pa - 1))
                fixed(g)
                dst = [a16[:, apar, j, z, hb * 384:(hb + 1) * 384].rearrange("p (h d) -> p h d", h=6) for z in range(2)]
                g.tensor_copy(dst[0], a32[:, b % 2, :, :]).then_inc(S["ash"], 1)
                wait(g, "ash", 4 * pa + b + 1)
                g.tensor_tensor(dst[1], a32[:, b % 2, :, :], dst[0], ALU.subtract).then_inc(S["asl"], 1)

            for k in range(SLOTS + 1):
                if attn and k >= 5 and k % 2 == 1:
                    split_a((k - 5) // 2)
                if k == SLOTS:
                    break
                if pro and isb(pp) and k == 0:
                    wait(g, "sd", 8 * (pp - 1))
                    wait(g, "kcp", 2)
                    fixed(g)
                    for j in range(2):
                        g.tensor_copy(qk[:, par, :, :, 1, j, 0:IT],
                                      kimg[:, :, :, bass.ds((2 * (pp - 2) + j) * IT, IT)]).then_inc(S["kic"], 1)
                if attn and 1 <= k <= UNITS:
                    u = k - 1
                    wait(g, "phd", 8 * pa + u + 1)
                    if isb(pa):
                        wait(g, "phi", 8 * (pa - 2) + u + 1)
                        g.tensor_tensor(pi[:, u % 2, 0:3, 1, :], p32[:, u % 2, :, 0:IT], pi[:, u % 2, 0:3, 0, :], ALU.subtract).then_inc(S["pli"], 1)
                        wait(g, "pli", 8 * (pa - 2) + u + 1)
                    g.tensor_tensor(pl[:, u % 2, :, :], p32[:, u % 2, :, IT:SEQ], ph[:, u % 2, :, :], ALU.subtract).then_inc(S["pll"], 1)
                if pre and k == 3:
                    p = s + 1
                    layernorm(g, c, hin[:, (par + 1) % 2], mv, rstd[:, :], xn[:, :, :], x16[:, (par + 1) % 2], "stat",
                              ("xna", "x16r"), p, lambda: wait(g, "xtp", p - 1))
                if post and k == 5:
                    layernorm(g, c, h1, mv2, rstd2[:, :], xn2[:, :, :], x2, "st2", ("l2n", "l2l"), pq,
                              lambda: wait(g, "rwd", pq))
                if post and k == 6:
                    p = pq
                    if isb(p):
                        wait(g, "dsp", 64 * (p - 2))
                        fixed(g)
                        for kk in range(2):
                            c.done(g.tensor_copy(rows[:, :, kk, 0:D].bitcast(F16), x2[:, :, :]))
                    else:
                        g.tensor_copy(ximg[:, 2 * p:2 * p + 2, :], x2[:, :, :]).then_inc(S["rwd"], 1)
                        wait(g, "rwd", p + 1)
                if post and k == 10:
                    p = pq
                    if isb(p):
                        wait(g, "sld", p + 1)
                        fixed(g)
                        c.done(g.tensor_copy(rows[:, :, :, D].bitcast(F32), wk2[:, :, :]))
                        for kk in range(2):
                            c.done(g.tensor_copy(rows[:, :, kk, D + 1], tid[:, :]))
                        c.here(g)
                        fixed(g)
                        g.tensor_scalar(tid[:, :], tid[:, :], float(2 * SEQ), None, ALU.add).then_inc(S["rwd"], 1)
                        wait(g, "rwd", p + 1)
                        fixed(g)
                        for j in range(2):
                            for kk in range(2):
                                g.indirect_dma_start(xg_d, bass.IndirectOffsetOnAxis(ap=sli[:, j, kk:kk + 1], axis=0),
                                                     rows[:, j, kk, :], None, bounds_check=NE * CAP - 1,
                                                     oob_is_err=False).then_inc(S["dsp"], 16)
                if pro and not isb(pp) and k == 8:
                    wait(g, "pjl", 10 * pp + 6)
                    g.tensor_copy(kimg[:, :, :, 256 * pp:256 * (pp + 1)].rearrange("p z m (j c) -> p z m j c", j=2),
                                  qk[:, par, :, :, 1, :, IT:SEQ]).then_inc(S["kcp"], 1)

        def h_of(p):
            if isb(p):
                return txt[bass.ds(2 * (p - 2), 2)].rearrange("t p n -> p t n")
            return himg_d[256 * p:256 * (p + 1)].rearrange("(t p) n -> p t n", t=2)

        out_i = out[0:TOK, :].rearrange("(b s) n -> b s n", s=SEQ)

        def step_sp(sp, s, par, pre, pro, attn, post):
            pp, pa, pq = s, s - 1, s - 2
            if pre:
                p = s + 1
                wait(sp, "xna", 2 * (p - 1))
                wait(sp, "hin_ld", 16 * p)
                sp.dma_start(hin[:, (par + 1) % 2, :, :], h_of(p)).then_inc(S["hin_ld"], 16)
            if post:
                wait(sp, "h1d", pq - 1)
                wait(sp, "hres_ld", 16 * pq)
                sp.dma_start(hres[:, PAR[0], :, :], h_of(pq)).then_inc(S["hres_ld"], 16)
            if pro and isb(pp):
                wait(sp, "pvd", 8 * (pp - 1))
                wait(sp, "vil", 16 * 12 * (pp - 2))
                for j in range(2):
                    src = vimg_d[bass.ds((2 * (pp - 2) + j) * IT, IT)].rearrange("k z (g r d) -> k z g r d", g=4, r=3)
                    for r in range(3):
                        for t in range(2):
                            p0 = 32 * r + 16 * t
                            sp.dma_start(vi[p0:p0 + 16, par, j, :, :, r, :].rearrange("k z g d -> k (z g) d"),
                                         src[:, :, :, r, :].rearrange("k z g d -> k (z g) d")).then_inc(S["vil"], 16)
            if pro and not isb(pp):
                for j in range(2):
                    wait(sp, "pjl", 10 * pp + 8 + 2 * j)
                    r0 = 256 * pp + P * j
                    sp.dma_start(vimg_d[r0:r0 + P], v16[:, par, j, :, :]).then_inc(S["vst"], 16)
                if pp == 1:
                    sp.wait_ge(S["vst"], 64)
            if post:
                wait(sp, "h1d", pq + 1)
                for j in range(2):
                    if isb(pq):
                        dst = out_i[bass.ds(2 * (pq - 2) + j, 1), IT:SEQ, :].rearrange("o s n -> (o s) n")
                        sp.dma_start(dst, h1[:, j, :]).then_inc(S["outd"], 16)
                    else:
                        b0 = 8 * (2 * pq + j)
                        sp.dma_start(out_i[b0:b0 + 8, 0:IT, :], h1[:, j, :]).then_inc(S["outd"], 16)

        STEPS = range(-1, NPAIR + 2)
        LOOP0, LOOP1 = 5, NPAIR - 1

        def stages(s):
            return dict(pre=0 <= s + 1 < NPAIR, pro=0 <= s < NPAIR, attn=0 <= s - 1 < NPAIR, post=0 <= s - 2 < NPAIR)

        def run(eng, f, chain=None):
            for s in range(-1, LOOP0):
                n0 = chain.n if chain else 0
                PAR[0] = s % 2
                f(s, s % 2, stages(s))
            per = chain.n - n0 if chain else 0
            base = chain.n if chain else 0
            with eng.Fori(0, (LOOP1 - LOOP0) // 2) as i:
                for h in range(2):
                    if chain:
                        chain.n = (i * 2 + h) * per + base
                    PAR[0] = (LOOP0 + h) % 2
                    f(i * 2 + (LOOP0 + h), PAR[0], dict(pre=True, pro=True, attn=True, post=True))
            if chain:
                chain.n = base + per * (LOOP1 - LOOP0)
            for s in range(LOOP1, NPAIR + 2):
                PAR[0] = s % 2
                f(s, s % 2, stages(s))

        def finish_dve(v, ch):
            ch.done(v.tensor_tensor(selt[:, :, :, :], tb[:, 0:NI * NE].rearrange("p (t j e) -> p t e j", t=4, j=8),
                                    seli[:, :].unsqueeze(1).unsqueeze(1).broadcast_to((P, 4, NE, 8)), ALU.mult))
            ch.done(v.tensor_tensor(ppi[:, :], seli[:, :], iota8[:, :], ALU.mult))
            ch.here(v)
            ch.done(v.tensor_reduce(posa[:, :, :], selt[:, :, :, :], X, ALU.add))
            ch.done(v.tensor_reduce(pka[:, 0, 0:1], ppi[:, :], X, ALU.add))
            ch.here(v)
            ch.done(v.tensor_tensor(posa[:, :, :], posa[:, :, :], cimg[:, :, :], ALU.add))
            ch.done(v.scalar_tensor_tensor(tidi[:, :], pka[:, 0, 0:1].broadcast_to((P, 4)), float(SEQ - IT), ppos[:, :], ALU.mult, ALU.add))
            ch.here(v)
            slots(v, ch, ohpa[:, :, :, :], ohimg[:, :, :, :], posa[:, :, :], pka[:, :, :], sla[:, :, :], ova[:, :, :],
                  iximg[:, :, :], slia[:, :, :], 4, "init", None)

        def finish_pool(g, c):
            g.wait_ge(S["init"], 2)
            for t2 in range(2):
                g.wait_ge(S["dsp"], 64 * (NPAIR - NPAIR_A + t2))
                for kk in range(2):
                    c.done(g.tensor_copy(rows[:, :, kk, 0:D].bitcast(F16), ximg[:, 2 * t2:2 * t2 + 2, :]))
                    c.done(g.tensor_copy(rows[:, :, kk, D + 1], tidi[:, 2 * t2:2 * t2 + 2]))
                c.done(g.tensor_copy(rows[:, :, :, D].bitcast(F32), wimg[:, 2 * t2:2 * t2 + 2, :]))
                c.here(g)
                for j in range(2):
                    for kk in range(2):
                        g.indirect_dma_start(xg_d, bass.IndirectOffsetOnAxis(ap=slia[:, 2 * t2 + j, kk:kk + 1], axis=0),
                                             rows[:, j, kk, :], None, bounds_check=NE * CAP - 1,
                                             oob_is_err=False).then_inc(S["dsp"], 16)
            g.wait_ge(S["dsp"], 64 * (NPAIR - NPAIR_A + 2))

        with nc.Block() as block:
            @block.sync
            def _(sp):
                sp.wait_ge(S["init"], 1)
                run(sp, lambda s, par, st: step_sp(sp, s, par, **st))
                sp.wait_ge(S["outd"], 32 * NPAIR)

            @block.gpsimd
            def _(g):
                c = Chain("pchain")
                c.done(g.memset(vi[:, :, :, :, :, :, :], 0.0))
                c.done(g.memset(pi[:, :, :, :, :], 0.0))
                c.done(g.memset(tb[:, :], 0.0))
                c.done(g.memset(ma[:, :, :], 0.0))
                c.done(g.memset(mb[:, :, :], 0.0))
                c.done(g.iota(tid[:, :], pattern=[[SEQ, 2]], base=IT, channel_multiplier=1, allow_small_or_imprecise_dtypes=True))
                c.done(g.iota(ppos[:, :], pattern=[[8 * SEQ, 4]], base=0, channel_multiplier=1, allow_small_or_imprecise_dtypes=True))
                c.here(g)
                g.memset(ppi[:, :], 0.0).then_inc(S["init"], 1)
                run(g, lambda s, par, st: step_pool(g, c, s, par, **st), c)
                finish_pool(g, c)

            @block.scalar
            def _(a):
                run(a, lambda s, par, st: step_act(a, s, par, **{k: x for k, x in st.items() if k != "pre"}))

            @block.vector
            def _(v):
                ch = Chain("chain")
                v.wait_ge(S["init"], 1)
                run(v, lambda s, par, st: step_dve(v, ch, s, par, last=False, **st), ch)
                finish_dve(v, ch)

            @block.tensor
            def _(pe):
                run(pe, lambda s, par, st: step_pe(pe, s, par, **{k: x for k, x in st.items() if k != "pre"}))
        att.close()

        xg = sb("xg", [P, 2, NB, ROW], I32)
        xgt = sb("xgt", [P, 2, 3, CAP], F16)
        w1h = sb("w1h", [P, 2, 3, FF], F16)
        w1l = sb("w1l", [P, 2, 2, FF], F16)
        w2h = sb("w2h", [P, 2, 6, D], F16)
        w2l = sb("w2l", [P, 2, 6, D], F16)
        b2s = sb("b2s", [P, 2, D], F32)
        g32 = sb("g32", [P, 2, HALF], F32)
        h16 = sb("h16", [P, 2, 2, 6, CAP], F16)
        y1 = sb("y1", [P, 2, D], F32)
        y2 = sb("y2", [P, NB, D], F32)
        f1b = [pj[0], pj[1], ops]
        f2b = [po[:, :], ptp[0][:, :].bitcast(F32)]
        xtb = [b[:, :].bitcast(F16) for b in sps]
        names = "wld xld gtp gte whi wlo f1d gld hhd hld f2d y1d y2d add".split()
        S.update({n: sem("m_" + n) for n in names})
        NX = (NB + 1) // 2
        F2AT = {0: 0, 2: 1, 4: 2, 6: 3, 8: 4, 9: 5, 11: 6}

        def m_sp(sp, t, par, one, two):
            if not one:
                return
            wait(sp, "wld", 16 * 6 * t)
            wait(sp, "xld", 32 * t)
            wait(sp, "whi", t - 1)
            wait(sp, "wlo", t - 1)
            e = bass.ds(t, 1)
            for b, parts in enumerate(KB):
                for r, p0, k in parts:
                    sp.dma_start(stage[p0:p0 + k, par, b * FF:(b + 1) * FF], w1[e, r:r + k, :].rearrange("o r n -> (o r) n")).then_inc(S["wld"], 16)
            sp.dma_start(stage[:, par, 3 * FF:].rearrange("p (c n) -> p c n", n=D),
                         w2[e].rearrange("o (c p) n -> p (o c) n", p=P)).then_inc(S["wld"], 16)
            wait(sp, "y1d", NB * (t - 1))
            sp.dma_start(b2s[:, par, :], b2[e].broadcast_to((P, D))).then_inc(S["wld"], 16)
            wait(sp, "add", 16 * NB * (t - 1))
            sp.dma_start(xg[:, par, 0:FB, :], xg_d[bass.ds(t * CAP, FB * P), :].rearrange("(b p) n -> p b n", p=P)).then_inc(S["xld"], 16)
            sp.dma_start(xg[0:CAP - FB * P, par, FB, :], xg_d[bass.ds(t * CAP + FB * P, CAP - FB * P), :]).then_inc(S["xld"], 16)

        def m_pe(pe, t, par, one, two):
            if one:
                for q in range(NX):
                    if q == 0:
                        wait(pe, "xld", 32 * (t + 1))
                    wait(pe, "gte", NX * t + q - 1)
                    for b in range(2 * q, min(2 * q + 2, NB)):
                        for c in range(3):
                            o = xtb[q % 2][:, ((b % 2) * 3 + c) * P:((b % 2) * 3 + c) * P + BLK[b]]
                            mm = pe.transpose(o, xg[0:BLK[b], par, b, c * DH:(c + 1) * DH].bitcast(F16), ident[0:BLK[b], 0:BLK[b]])
                    mm.then_inc(S["gtp"], 1)
                wait(pe, "whi", t + 1)
                wait(pe, "wlo", t + 1)
            for q in range(12):
                if one:
                    m, hf = divmod(q, 2)
                    wait(pe, "gld", 12 * t + q - 2)
                    if q == 0:
                        wait(pe, "gte", NX * (t + 1))
                    for n, (w, b, e) in enumerate(TERMS):
                        mm = pe.matmul(f1b[q % 3][:, 0:HALF], (w1h, w1l)[w][:, par, b, m * P:(m + 1) * P],
                                       xgt[:, par, e, hf * HALF:(hf + 1) * HALF], start=n == 0, stop=n == 4)
                    mm.then_inc(S["f1d"], 1)
                if two and q in F2AT:
                    u, tt, pr = F2AT[q], t - 1, 1 - par
                    if u == 0:
                        wait(pe, "hld", 12 * (tt + 1))
                    wait(pe, "y1d", NB * tt + u - (1 if u else 0))
                    n = 0
                    for c in range(6):
                        for z, w in ((0, w2h), (0, w2l), (1, w2h)):
                            mm = pe.matmul(f2b[u % 2][0:BLK[u], 0:D], h16[:, pr, z, c, u * P:u * P + BLK[u]], w[:, pr, c, :],
                                           start=n == 0, stop=n == 17)
                            n += 1
                    mm.then_inc(S["f2d"], 1)

        def m_act(a, t, par, one, two):
            if one:
                wait(a, "wld", 16 * 6 * (t + 1))
                wait(a, "f1d", 12 * (t - 1))
                a.activation(w1h[:, par, :, :], stage[:, par, 0:3 * FF].rearrange("p (b n) -> p b n", b=3), ACT.Copy, scale=WS)
                wait(a, "f2d", NB * (t - 1))
                a.activation(w2h[:, par, :, :], stage[:, par, 3 * FF:].rearrange("p (c n) -> p c n", n=D), ACT.Copy,
                             scale=WS).then_inc(S["whi"], 1)
            for q in range(12):
                if one:
                    m, hf = divmod(q, 2)
                    wait(a, "f1d", 12 * t + q + 1)
                    wait(a, "hhd", 12 * t + q - 1)
                    wait(a, "hld", 12 * t + q - 1)
                    fixed(a)
                    a.activation(g32[:, q % 2, :], f1b[q % 3][:, 0:HALF], ACT.Gelu, bias=b1t[:, bass.ds(t * 6 + m, 1)],
                                 scale=1.0 / WS).then_inc(S["gld"], 1)
                if two and q in F2AT:
                    u, tt = F2AT[q], t - 1
                    n = BLK[u]
                    wait(a, "y1d", NB * tt + u + 1)
                    if u == 0:
                        wait(a, "add", 16 * NB * tt)
                    a.activation(y2[0:n, u, :], y1[0:n, u % 2, :], ACT.Copy,
                                 scale=xg[0:n, 1 - par, u, D:D + 1].bitcast(F32)).then_inc(S["y2d"], 1)

        def m_dve(v, t, par, one, two):
            if one:
                wait(v, "whi", t + 1)
                v.scalar_tensor_tensor(w1l[:, par, :, :], stage[:, par, 0:2 * FF].rearrange("p (b n) -> p b n", b=2), WS,
                                       w1h[:, par, 0:2, :], ALU.mult, ALU.subtract)
                v.scalar_tensor_tensor(w2l[:, par, :, :], stage[:, par, 3 * FF:].rearrange("p (c n) -> p c n", n=D), WS,
                                       w2h[:, par, :, :], ALU.mult, ALU.subtract).then_inc(S["wlo"], 1)
                for q in range(NX):
                    wait(v, "gtp", NX * t + q + 1)
                    for b in range(2 * q, min(2 * q + 2, NB)):
                        i = v.tensor_copy(xgt[:, par, :, b * P:b * P + BLK[b]],
                                          xtb[q % 2][:, (b % 2) * 3 * P:((b % 2) * 3 + 3) * P].rearrange("p (c n) -> p c n", c=3)[:, :, 0:BLK[b]])
                    i.then_inc(S["gte"], 1)
            for q in range(12):
                if one:
                    m, hf = divmod(q, 2)
                    wait(v, "hhd", 12 * t + q + 1)
                    c = slice(hf * HALF, (hf + 1) * HALF)
                    v.tensor_tensor(h16[:, par, 1, m, c], g32[:, q % 2, :], h16[:, par, 0, m, c], ALU.subtract).then_inc(S["hld"], 1)
                if two and q in F2AT:
                    u, tt = F2AT[q], t - 1
                    n = BLK[u]
                    wait(v, "f2d", NB * tt + u + 1)
                    wait(v, "y2d", NB * tt + u - (1 if u else 0))
                    v.scalar_tensor_tensor(y1[0:n, u % 2, :], f2b[u % 2][0:n, 0:D], 1.0 / WS, b2s[0:n, 1 - par, :], ALU.mult,
                                           ALU.add).then_inc(S["y1d"], 1)

        def m_pool(g, t, par, one, two):
            for q in range(12):
                if one:
                    m, hf = divmod(q, 2)
                    wait(g, "gld", 12 * t + q + 1)
                    wait(g, "f2d", NB * (t - 1))
                    fixed(g)
                    g.tensor_copy(h16[:, par, 0, m, hf * HALF:(hf + 1) * HALF], g32[:, q % 2, :]).then_inc(S["hhd"], 1)
                if two and q in F2AT:
                    u, tt = F2AT[q], t - 1
                    n = BLK[u]
                    wait(g, "y2d", NB * tt + u + 1)
                    if u == 0:
                        wait(g, "add", 16 * NB * tt)
                    fixed(g)
                    g.indirect_dma_start(out, bass.IndirectOffsetOnAxis(ap=xg[0:n, 1 - par, u, D + 1:ROW], axis=0),
                                         y2[0:n, u, :], None, compute_op=ALU.add).then_inc(S["add"], 16)

        def m_run(eng, f):
            f(eng, 0, 0, True, False)
            f(eng, 1, 1, True, True)
            with eng.Fori(1, NE // 2) as i:
                f(eng, i * 2, 0, True, True)
                f(eng, i * 2 + 1, 1, True, True)
            f(eng, NE, 0, False, True)

        with nc.Block() as block:
            @block.sync
            def _(sp):
                m_run(sp, m_sp)
                sp.wait_ge(S["add"], 16 * NB * NE)

            @block.gpsimd
            def _(g):
                m_run(g, m_pool)

            @block.scalar
            def _(a):
                m_run(a, m_act)

            @block.vector
            def _(v):
                m_run(v, m_dve)

            @block.tensor
            def _(pe):
                m_run(pe, m_pe)


INS = ["x", "txt", "L0_tok_ln_gamma", "L0_tok_ln_beta", "L0_tok_W", "L0_tok_b", "L0_attn_W_Q", "L0_attn_W_K", "L0_attn_W_V",
       "L0_attn_W_O", "L0_ffn_Wr", "L0_ffn_w1", "L0_ffn_b1", "L0_ffn_w2", "L0_ffn_b2"]


def kernel(**inputs):
    import numpy as np
    import concourse.bacc as bacc
    from concourse.bass_utils import run_bass_kernel_spmd

    nc = bacc.Bacc("TRN2", target_bir_lowering=False, num_devices=1)
    arrays, args = {}, []
    for name in INS:
        a = np.ascontiguousarray(inputs[name])
        arrays[f"in_{name}"] = a
        args.append(nc.dram_tensor(f"in_{name}", a.shape, mybir.dt.from_np(a.dtype), kind="ExternalInput").ap())
    out = nc.dram_tensor("out", (TOK + CAP, D), F32, kind="ExternalOutput").ap()
    build(nc, *args, out)
    r = run_bass_kernel_spmd(nc, [arrays], core_ids=[0])
    return r.results[0]["out"][:TOK].reshape(NI, SEQ, D)
```

```python
from contextlib import ExitStack

import concourse.bass as bass
from concourse import mybir

F32 = mybir.dt.float32
F16 = mybir.dt.float16
BF16 = mybir.dt.bfloat16
I32 = mybir.dt.int32
U32 = mybir.dt.uint32
ALU = mybir.AluOpType
ACT = mybir.ActivationFunctionType
X = mybir.AxisListType.X

P = 128
EPS = 1e-5
D = 192
NI, IT, TT = 32, 16, 128
SEQ = IT + TT
TOK = NI * SEQ
H, DH = 12, 64
HD = H * DH
NE, FF = 8, 768
CAP = int(TOK / NE * 1.5)
WC, EC, TC, ROW = D, D + 2, D + 3, D + 4
XP = 18
WS = 64.0
QS = 8.0
RS = 1024.0
NPAIR_A = 2
NPAIR = NPAIR_A + NI // 2
UNITS = 8
KB = [[(0, 0, 128)], [(128, 0, 64), (0, 64, 64)], [(64, 0, 128)]]
BLK = [P] * (CAP // P) + ([CAP % P] if CAP % P else [])
NB = len(BLK)
FB = CAP // P
HALF = CAP // 2


def head_of(pos):
    g, r = divmod(pos, 3)
    return 6 * (g // 2) + g % 2 + 2 * r


def build(nc, x, txt, gam, bet, wemb, bemb, wq, wk, wv, wo, wr, w1, b1, w2, b2, out):
    himg_d = nc.dram_tensor("himg_d", (NI * IT, D), F32, kind="Internal").ap()
    vimg_d = nc.dram_tensor("vimg_d", (NI * IT, 2, HD), F16, kind="Internal").ap()
    xg_d = nc.dram_tensor("xg_d", (NE * CAP, ROW), I32, kind="Internal").ap()

    with ExitStack() as ctx:
        def sb(name, shape, dt, c=ctx):
            return c.enter_context(nc.sbuf_tensor(name, shape, dt))

        def sem(name):
            return ctx.enter_context(nc.semaphore(name))

        def ps(name, shape, dt):
            return ctx.enter_context(nc.psum_tensor(name, shape, dt))

        ident = sb("ident", [P, P], F16)
        identb = sb("identb", [P, P], BF16)
        maskt = sb("maskt", [P, 3, SEQ], BF16)
        maski = sb("maski", [P, 3, P], BF16)
        tri = sb("tri", [P, P], F16)
        ones = sb("ones", [P, P], F16)
        rowmask = sb("rowmask", [P, 8, P], F16)
        seli = sb("seli", [P, 8], F32)
        iota8 = sb("iota8", [P, NE], F32)
        zrow = sb("zrow", [P, NB, ROW], I32)
        zid = zrow[:, :, ROW - 1:ROW]
        halfc = sb("halfc", [P, 4], F32)
        wqkvh = sb("wqkvh", [P, 3, 3 * HD], F16)
        wqkvl = sb("wqkvl", [P, 2, 3 * HD], F16)
        woh = sb("woh", [P, 6, D], F16)
        wol = sb("wol", [P, 6, D], F16)
        wr32 = sb("wr32", [P, 3, NE], F32)
        wrh = sb("wrh", [P, 3, NE], F16)
        wrl = sb("wrl", [P, 2, NE], F16)
        b1t = sb("b1t", [P, NE * 6], F32)
        stage = sb("stage", [P, 2, 3 * FF + 6 * D], F32)

        pj = [ps(f"pj{i}", [P, 512], F32) for i in range(2)]
        sps = [ps(f"sps{i}", [P, 512], F32) for i in range(2)]
        ptp = [ps(f"ptp{i}", [P, 1024], F16) for i in range(2)]
        ops = ps("ops", [P, 512], F32)
        po = ps("po", [P, 512], F32)
        poh = po[:, :].bitcast(F16)
        pjh = [b[:, :].bitcast(F16) for b in pj]

        early = ExitStack()
        raw = sb("raw", [P, 3, XP, 64], F32, early)
        pad = sb("pad", [P, 3, XP, 66], F32, early)
        wst = sb("wst", [P, 2, 15, D], F32, early)
        wg = sb("wg", [P, 30, D], F32, early)
        weh = sb("weh", [P, 30, D], F16, early)
        wel = sb("wel", [P, 30, D], F16, early)
        b1r = sb("b1r", [NE * 6, P], F32, early)
        identf = sb("identf", [P, P], F32, early)
        gm = sb("gm", [P, 2, 15], F32, early)
        gm64 = sb("gm64", [P, 30], F32, early)
        bt = sb("bt", [P, 2, 15], F32, early)
        bb = sb("bb", [P, D], F32, early)
        cb = sb("cb", [P, D], F32, early)
        est = sb("est", [P, 4, 15, 6], F32, early)
        emv = sb("emv", [P, 4, 2], F32, early)
        eve = sb("eve", [P, 4], F32, early)
        ers = sb("ers", [P, 4], F32, early)
        nx = raw[:, :, :, :].rearrange("p c r w -> p (c r w)")[:, 0:9 * XP * 16].rearrange("p (s r c) -> p s r c", s=3, c=16)
        nxh = sb("nxh", [P, 2, 3, 3 * XP * 16], F16, early)
        nxl = sb("nxl", [P, 2, 3, 3 * XP * 16], F16, early)
        tte = sb("tte", [P, 60, P], F16, early)
        him = sb("him", [P, 4, D], F32, early)

        c_set = sem("c_set")
        ld_x = sem("ld_x")
        ld_we = sem("ld_we")
        ld_g = sem("ld_g")
        ld_w = [sem(f"ld_w{n}") for n in range(4)]
        sp_hi = sem("sp_hi")
        sp_lo = sem("sp_lo")
        ec = sem("ec")
        e_wg = sem("e_wg")
        e_wh = sem("e_wh")
        e_wl = sem("e_wl")
        e_beta = sem("e_beta")
        e_var = sem("e_var")
        e_rs = sem("e_rs")
        e_nx = sem("e_nx")
        e_hi = sem("e_hi")
        e_lo = sem("e_lo")
        e_tp = sem("e_tp")
        e_ta = sem("e_ta")
        e_td = sem("e_td")
        e_ps = sem("e_ps")
        e_him = sem("e_him")
        e_st = sem("e_st")
        pref = sem("pref")

        def load192(eng, dst, src, s):
            n = 0
            for b, parts in enumerate(KB):
                for r, p0, k in parts:
                    eng.dma_start(dst(b, p0, k), src(r, k)).then_inc(s, 16)
                    n += 1
            return n

        SPLITS = [(0, 0), (1, 1), (2, 0), (3, 1)]

        LDW = [16 * 6, 16 * 12, 16 * 6, 16 * (12 + 4)]

        def split_hi(a, n, what, place):
            a.wait_ge(ld_w[n], LDW[n])
            if what < 3:
                a.activation(wqkvh[:, what, 0:HD], stage[:, place, 0:HD], ACT.Copy, scale=QS)
                a.activation(wqkvh[:, what, HD:3 * HD], stage[:, place, HD:3 * HD], ACT.Copy, scale=WS).then_inc(sp_hi, 1)
            else:
                a.activation(wrh[:, :, :], wr32[:, :, :], ACT.Copy, scale=RS)
                a.activation(woh[:, :, :], stage[:, place, 0:6 * D].rearrange("p (c n) -> p c n", n=D),
                             ACT.Copy, scale=WS).then_inc(sp_hi, 1)

        def split_lo(v, n, what, place):
            v.wait_ge(ld_w[n], LDW[n])
            v.wait_ge(sp_hi, n + 1)
            if what < 2:
                v.scalar_tensor_tensor(wqkvl[:, what, 0:HD], stage[:, place, 0:HD], QS, wqkvh[:, what, 0:HD],
                                       ALU.mult, ALU.subtract)
                v.scalar_tensor_tensor(wqkvl[:, what, HD:3 * HD], stage[:, place, HD:3 * HD], WS,
                                       wqkvh[:, what, HD:3 * HD], ALU.mult, ALU.subtract).then_inc(sp_lo, 1)
            elif what == 3:
                v.scalar_tensor_tensor(wrl[:, :, :], wr32[:, 0:2, :], RS, wrh[:, 0:2, :], ALU.mult, ALU.subtract)
                v.scalar_tensor_tensor(wol[:, :, :], stage[:, place, 0:6 * D].rearrange("p (c n) -> p c n", n=D), WS,
                                       woh[:, :, :], ALU.mult, ALU.subtract).then_inc(sp_lo, 1)

        def evac_t(eng, w, odd):
            for q in range(odd, 8, 2):
                n = min(8, 60 - 8 * q)
                eng.wait_ge(e_tp, 8 * w + q + 1)
                if w and q == odd:
                    eng.wait_ge(e_ps, w)
                dst = tte[:, 8 * q:8 * q + n, :]
                src = ptp[odd][:, 0:n * P].rearrange("p (n q) -> p n q", n=n)
                if odd:
                    eng.tensor_copy(dst, src).then_inc(e_td, 1)
                else:
                    eng.activation(dst, src, ACT.Copy).then_inc(e_ta, 1)

        OFF = [(1, 1), (1, 0), (1, 2), (0, 1), (2, 1)]

        with nc.Block() as block:
            @block.sync
            def _(sp):
                xr = raw[:, :, :, :]
                sp.wait_ge(ec, 2)
                v = x.rearrange("b c h w -> b c (h w)")
                for hy in range(4):
                    a, b = max(16 * hy - 1, 0), min(16 * hy + 17, 64)
                    d0 = a - (16 * hy - 1)
                    sp.dma_start(xr[hy:P:4].rearrange("p c r w -> p c (r w)")[:, :, d0 * 64:(d0 + b - a) * 64],
                                 v[:, :, a * 64:b * 64]).then_inc(ld_x, 16)
                sp.dma_start(gm[:, :, :], gam.rearrange("(a q f) -> q a f", a=2, q=P)).then_inc(ld_g, 16)
                sp.dma_start(bt[:, :, :], bet.rearrange("(a q f) -> q a f", a=2, q=P)).then_inc(ld_g, 16)
                sp.dma_start(bb[:, :], bemb.rearrange("(o n) -> o n", o=1).broadcast_to((P, D))).then_inc(ld_g, 16)
                sp.dma_start(b1r[:, :], b1.rearrange("e (c p) -> (e c) p", p=P)).then_inc(ld_g, 16)
                wv_ = wemb.rearrange("(a q f) n -> q a (f n)", a=2, q=P)
                for a in range(2):
                    sp.dma_start(wst[:, a, :, :].rearrange("q f n -> q (f n)"), wv_[:, a, :]).then_inc(ld_we, 16)
                for lot, (what, place) in enumerate(SPLITS):
                    if what < 3:
                        if what == 2:
                            sp.wait_ge(sp_hi, 1)
                            sp.wait_ge(sp_lo, 1)
                        for r, p0, k in KB[what]:
                            for n, w in ((0, wq), (1, wk)):
                                sp.dma_start(stage[p0:p0 + k, place, n * HD:(n + 1) * HD].rearrange("p (h d) -> p h d", h=H),
                                             w[:, r:r + k, :].rearrange("h m d -> m h d")).then_inc(ld_w[lot], 16)
                            for g in range(4):
                                h0 = head_of(3 * g)
                                sp.dma_start(stage[p0:p0 + k, place, 2 * HD + g * D:2 * HD + (g + 1) * D]
                                             .rearrange("p (r d) -> p r d", r=3),
                                             wv[h0:h0 + 5:2, r:r + k, :].rearrange("h m d -> m h d")).then_inc(ld_w[lot], 16)
                    else:
                        sp.wait_ge(sp_hi, 2)
                        sp.wait_ge(sp_lo, 2)
                        for pos in range(H):
                            p0, h = 64 * (pos % 2), head_of(pos)
                            sp.dma_start(stage[p0:p0 + 64, 1, pos // 2 * D:(pos // 2 + 1) * D],
                                         wo[h * DH:(h + 1) * DH, :]).then_inc(ld_w[lot], 16)
                        load192(sp, lambda b, p0, k: wr32[p0:p0 + k, b, :], lambda r, k: wr[r:r + k, :], ld_w[lot])
                hv = himg_d.rearrange("(p w) n -> p w n", w=4)
                sp.wait_ge(e_him, 4)
                sp.dma_start(hv, him[:, :, :]).then_inc(e_st, 16)
                sp.wait_ge(e_st, 16)

            @block.gpsimd
            def _(g):
                g.memset(ident[:, :], 0.0).then_inc(c_set, 1)
                g.memset(identb[:, :], 0.0).then_inc(c_set, 1)
                g.memset(maskt[:, :, :], 0.0).then_inc(c_set, 1)
                g.memset(maski[:, :, :], 0.0).then_inc(c_set, 1)
                g.memset(tri[:, :], 1.0).then_inc(c_set, 1)
                g.memset(ones[:, :], 1.0).then_inc(c_set, 1)
                g.memset(rowmask[:, :, :], 1.0).then_inc(c_set, 1)
                g.memset(seli[:, :], 1.0).then_inc(c_set, 1)
                g.memset(zrow[:, :, :], 0).then_inc(c_set, 1)
                g.memset(halfc[:, :], -0.5).then_inc(c_set, 1)
                g.memset(identf[:, :], 0.0).then_inc(c_set, 1)
                g.wait_ge(c_set, 11)
                for m in (ident, identb, identf):
                    g.affine_select(out=m[:, :], in_=m[:, :], compare_op=ALU.not_equal, fill=1.0, base=0,
                                    pattern=[[-1, P]], channel_multiplier=1).then_inc(c_set, 1)
                g.affine_select(out=maskt[:, :, :], in_=maskt[:, :, :], compare_op=ALU.is_ge, fill=-1e30, base=IT,
                                pattern=[[0, 3], [-1, SEQ]], channel_multiplier=1).then_inc(c_set, 1)
                g.affine_select(out=maski[:, :, :], in_=maski[:, :, :], compare_op=ALU.is_ge, fill=-1e30, base=0,
                                pattern=[[0, 3], [-1, P]], channel_multiplier=1).then_inc(c_set, 1)
                g.affine_select(out=tri[:, :], in_=tri[:, :], compare_op=ALU.is_gt, fill=0.0, base=0,
                                pattern=[[1, P]], channel_multiplier=-1).then_inc(c_set, 1)
                g.affine_select(out=rowmask[:, :, :], in_=rowmask[:, :, :], compare_op=ALU.is_gt, fill=0.0, base=IT,
                                pattern=[[IT, 8], [0, P]], channel_multiplier=-1).then_inc(c_set, 1)
                g.affine_select(out=seli[:, :], in_=seli[:, :], compare_op=ALU.is_gt, fill=0.0, base=IT,
                                pattern=[[IT, 8]], channel_multiplier=-1).then_inc(c_set, 1)
                g.iota(iota8[:, :], pattern=[[1, NE]], base=0, channel_multiplier=0,
                       allow_small_or_imprecise_dtypes=True).then_inc(c_set, 1)
                g.iota(zid, pattern=[[P, NB], [1, 1]], base=TOK, channel_multiplier=1).then_inc(c_set, 1)
                g.wait_ge(c_set, 21)
                g.affine_select(out=seli[:, :], in_=seli[:, :], compare_op=ALU.is_ge, fill=0.0, base=0,
                                pattern=[[-IT, 8]], channel_multiplier=1).then_inc(c_set, 1)
                for j in range(8):
                    g.affine_select(out=maski[:, :, j * IT:(j + 1) * IT], in_=maski[:, :, j * IT:(j + 1) * IT],
                                    compare_op=ALU.is_gt, fill=-1e30, base=(j + 1) * IT,
                                    pattern=[[0, 3], [0, IT]], channel_multiplier=-1).then_inc(c_set, 1)
                for e in range(NE):
                    g.dma_start(xg_d[e * CAP:e * CAP + FB * P, :].rearrange("(b p) n -> p b n", p=P), zrow[:, 0:FB, :]).then_inc(pref, 16)
                    g.dma_start(xg_d[e * CAP + FB * P:(e + 1) * CAP, :], zrow[0:CAP - FB * P, FB, :]).then_inc(pref, 16)
                zf = zrow[:, :, 0:D].bitcast(F32)
                g.dma_start(out[TOK:TOK + FB * P, :].rearrange("(b p) n -> p b n", p=P), zf[:, 0:FB, :]).then_inc(pref, 16)
                g.dma_start(out[TOK + FB * P:TOK + CAP, :], zf[0:CAP - FB * P, FB, :]).then_inc(pref, 16)
                g.wait_ge(ld_g, 64)
                g.wait_ge(ld_we, 32)
                g.tensor_scalar(gm64[:, :], gm[:, :, :].rearrange("p a f -> p (a f)"), WS, None, ALU.mult).then_inc(e_wg, 1)
                g.wait_ge(e_wg, 1)
                for a in range(2):
                    g.tensor_tensor(wg[:, 15 * a:15 * a + 15, :], wst[:, a, :, :],
                                    gm64[:, 15 * a:15 * a + 15].unsqueeze(2).broadcast_to((P, 15, D)), ALU.mult).then_inc(e_wg, 1)
                g.wait_ge(e_var, 1)
                g.tensor_tensor(ers[:, :], eve[:, :], halfc[:, :], ALU.pow).then_inc(e_rs, 1)
                for w in range(4):
                    g.wait_ge(e_nx, w + 1)
                    g.wait_ge(e_hi, w + 1)
                    if w >= 2:
                        g.wait_ge(e_tp, 8 * (w - 1))
                    g.tensor_tensor(nxl[:, w % 2], nx[:, :, :, :].rearrange("p s r c -> p s (r c)"), nxh[:, w % 2], ALU.subtract).then_inc(e_lo, 1)
                g.wait_ge(pref, 16 * (2 * NE + 2))

            @block.scalar
            def _(a):
                for n, (what, place) in enumerate(SPLITS[:2]):
                    split_hi(a, n, what, place)
                for h in range(2):
                    a.wait_ge(e_wg, 2 + h)
                    a.activation(weh[:, 15 * h:15 * h + 15, :], wg[:, 15 * h:15 * h + 15, :], ACT.Copy).then_inc(e_wh, 1)
                for w in range(4):
                    a.wait_ge(e_nx, w + 1)
                    if w >= 2:
                        a.wait_ge(e_tp, 8 * (w - 1))
                    a.activation(nxh[:, w % 2], nx[:, :, :, :].rearrange("p s r c -> p s (r c)"), ACT.Copy).then_inc(e_hi, 1)
                    if w >= 1:
                        evac_t(a, w - 1, 0)
                    if w < 2:
                        split_hi(a, 2 + w, *SPLITS[2 + w])
                evac_t(a, 3, 0)

            @block.vector
            def _(v):
                v.memset(raw[:, :, 0, :], 0.0).then_inc(ec, 1)
                v.memset(raw[:, :, XP - 1, :], 0.0).then_inc(ec, 1)
                v.memset(pad[:, :, :, :], 0.0).then_inc(ec, 1)
                v.wait_ge(ec, 3)
                v.wait_ge(ld_x, 64)
                v.tensor_copy(pad[:, :, :, 1:65], raw[:, :, :, :]).then_inc(ec, 1)
                v.wait_ge(ec, 4)
                for w in range(4):
                    for s, (r0, c0) in enumerate(OFF):
                        for c in range(3):
                            last = v.bn_stats(est[:, w, 3 * s + c, :],
                                              pad[:, c, r0:r0 + 16, c0 + 16 * w:c0 + 16 * w + 16])
                    last.then_inc(ec, 1)
                v.wait_ge(ec, 8)
                for w in range(4):
                    v.bn_aggr(emv[:, w, :], est[:, w, :, :].rearrange("p a b -> p (a b)")).then_inc(ec, 1)
                v.wait_ge(ec, 12)
                v.tensor_scalar(eve[:, :], emv[:, :, 1], EPS, None, ALU.add).then_inc(e_var, 1)
                split_lo(v, 0, *SPLITS[0])
                split_lo(v, 1, *SPLITS[1])
                for h in range(2):
                    v.wait_ge(e_wh, h + 1)
                    v.tensor_tensor(wel[:, 15 * h:15 * h + 15, :], wg[:, 15 * h:15 * h + 15, :],
                                    weh[:, 15 * h:15 * h + 15, :], ALU.subtract).then_inc(e_wl, 1)
                v.wait_ge(e_beta, 1)
                v.tensor_tensor(cb[:, :], po[:, 0:D], bb[:, :], ALU.add).then_inc(ec, 1)
                v.wait_ge(e_beta, 2)
                v.tensor_copy(b1t[:, :], pj[0][:, 0:NE * 6])
                v.wait_ge(e_rs, 1)

                def window(w):
                    if w:
                        v.wait_ge(e_lo, w)
                        v.wait_ge(e_hi, w)
                    rows = pad[:, :, :, 16 * w:16 * w + 16].rearrange("p c r w -> p (c r) w")
                    shifted = bass.AP(tensor=rows.tensor, offset=rows.offset, ap=[rows.ap[0], [1, 3], rows.ap[1], rows.ap[2]])
                    v.tensor_scalar(nx[:, :, :, :], shifted, emv[:, w, 0:1], ers[:, w:w + 1],
                                    ALU.subtract, ALU.mult).then_inc(e_nx, 1)

                window(0)
                window(1)
                for w in range(4):
                    evac_t(v, w, 1)
                    if w < 2:
                        window(w + 2)
                    if w == 1:
                        split_lo(v, 3, *SPLITS[3])
                    v.wait_ge(e_ps, w + 1)
                    v.wait_ge(ec, 13)
                    v.scalar_tensor_tensor(him[:, w, :], ops[:, 0:D], 1.0 / WS, cb[:, :], ALU.mult, ALU.add).then_inc(e_him, 1)

            @block.tensor
            def _(pe):
                pe.wait_ge(ld_we, 32)
                pe.wait_ge(ld_g, 64)
                for n in range(30):
                    mm = pe.matmul(po[:, 0:D], bt[:, n // 15, n % 15:n % 15 + 1].broadcast_to((P, P)), wst[:, n // 15, n % 15, :],
                                   start=n == 0, stop=n == 29)
                mm.then_inc(e_beta, 1)
                pe.wait_ge(c_set, 30)
                pe.transpose(pj[0][:, 0:NE * 6], b1r[:, :], identf[0:NE * 6, 0:NE * 6]).then_inc(e_beta, 1)
                for w in range(4):
                    pe.wait_ge(e_hi, w + 1)
                    for q in range(8):
                        if q == 4:
                            pe.wait_ge(e_lo, w + 1)
                        k = 4 * w + q // 2
                        if k:
                            pe.wait_ge(e_td if q % 2 else e_ta, k)
                        for n in range(8 * q, min(8 * q + 8, 60)):
                            src = (nxh, nxl)[n // 30]
                            a, f = divmod(n % 30, 15)
                            s, c = divmod(f, 3)
                            r0, c0 = OFF[s]
                            at0 = (c * XP + r0 + 8 * a) * 16
                            mm = pe.transpose(ptp[q % 2][:, (n % 8) * P:(n % 8 + 1) * P],
                                              src[:, w % 2, c0, at0:at0 + P], ident[:, :])
                            if n == 29:
                                pe.wait_ge(e_lo, w + 1)
                        mm.then_inc(e_tp, 1)
                    if w == 0:
                        pe.wait_ge(e_wl, 2)
                    else:
                        pe.wait_ge(e_him, w)
                    pe.wait_ge(e_td, 4 * w + 4)
                    pe.wait_ge(e_ta, 4 * w + 4)
                    for n in range(30):
                        pe.matmul(ops[:, 0:D], tte[:, n, :], weh[:, n, :], start=n == 0, stop=False)
                        pe.matmul(ops[:, 0:D], tte[:, n, :], wel[:, n, :], start=False, stop=False)
                        mm = pe.matmul(ops[:, 0:D], tte[:, 30 + n, :], weh[:, n, :], start=False, stop=n == 29)
                    mm.then_inc(e_ps, 1)
        early.close()

        att = ExitStack()
        hin = sb("hin", [P, 2, 2, D], F32, att)
        hres = sb("hres", [P, 2, 2, D], F32, att)
        bst = sb("bst", [P, 2, 6], F32, att)
        mv = sb("mv", [P, 2, 2], F32, att)
        rstd = sb("rstd", [P, 2], F32, att)
        xn = sb("xn", [P, 2, D], F32, att)
        x16 = sb("x16", [P, 2, 2, 2 * D], F16, att)
        xt = sb("xt", [P, 2, 3, 2 * P], F16, att)
        qk = sb("qk", [P, 2, 2, 6, 2, 2, SEQ], F16, att)
        kimg = sb("kimg", [P, 2, 6, NI * IT], F16, att)
        v16 = sb("v16", [P, 2, 2, 2, HD], F16, att)
        vi = sb("vi", [P, 2, 2, 2, 4, 3, DH], F16, att)
        nm = sb("nm", [P, 2, 3], F32, att)
        p32 = sb("p32", [P, 2, 3, SEQ], F32, att)
        ph = sb("ph", [P, 2, 3, P], F16, att)
        pl = sb("pl", [P, 2, 3, P], F16, att)
        pi = sb("pi", [P, 2, 4, 2, IT], F16, att)
        pt = sb("pt", [P, 2, 7, P], F16, att)
        rs = sb("rs", [P, 2, 4, 3], F32, att)
        ri = sb("ri", [P, 6], F32, att)
        a32 = sb("a32", [P, 2, 6, DH], F32, att)
        a16 = sb("a16", [P, 2, 2, 2, HD], F16, att)
        at = sb("at", [P, 2, 2, 6, P], F16, att)
        h1 = sb("h1", [P, 2, D], F32, att)
        bst2 = sb("bst2", [P, 2, 6], F32, att)
        mv2 = sb("mv2", [P, 2, 2], F32, att)
        rstd2 = sb("rstd2", [P, 2], F32, att)
        xn2 = sb("xn2", [P, 2, D], F32, att)
        x2t = sb("x2t", [P, 3, 2 * P], F16, att)
        lg = sb("lg", [P, 2, NE], F32, att)
        mx = sb("mx", [P, 2, 8], F32, att)
        mi = sb("mi", [P, 2, 8], U32, att)
        dl = sb("dl", [P, 2, 8], F32, att)
        exr = sb("exr", [P, 2, 8], F32, att)
        sm = sb("sm", [P, 8], F32, att)
        pk = sb("pk", [P, 2, 2], F32, att)
        ix = sb("ix", [P, 2, 2], F32, att)
        oh = sb("oh", [P, 2, 2, NE], F32, att)
        ma = sb("ma", [P, 4, NE], F16, att)
        mb = sb("mb", [P, 4, NE], F16, att)
        c4 = sb("c4", [P, 4 * NE], F32, att)
        pos = sb("pos", [P, 2, NE], F32, att)
        ohp = sb("ohp", [P, 2, 2, NE], F32, att)
        pk2 = sb("pk2", [P, 2, 2], F32, att)
        sl = sb("sl", [P, 2, 2], F32, att)
        ov = sb("ov", [P, 2, 2], F32, att)
        sli = sb("sli", [P, 2, 2], I32, att)
        rows = sb("rows", [P, 2, 2, ROW], I32, att)
        tid = sb("tid", [P, 2], F32, att)
        tb = sb("tb", [P, (NI + 1) * NE], F32, att)
        rimg = sb("rimg", [P, 4, ROW], I32, att)
        iximg = sb("iximg", [P, 4, 2], F32, att)
        ohimg = sb("ohimg", [P, 4, 2, NE], F32, att)
        mimg = sb("mimg", [P, 4, NE], F16, att)
        ipre = sb("ipre", [P, NI * NE], F32, att)
        cimg = sb("cimg", [P, 4, NE], F32, att)
        tidi = sb("tidi", [P, 4], F32, att)
        ppos = sb("ppos", [P, 4], F32, att)
        ppi = sb("ppi", [P, 8], F32, att)
        posa = sb("posa", [P, 4, NE], F32, att)
        ohpa = sb("ohpa", [P, 4, 2, NE], F32, att)
        pka = sb("pka", [P, 4, 2], F32, att)
        sla = sb("sla", [P, 4, 2], F32, att)
        ova = sb("ova", [P, 4, 2], F32, att)
        slia = sb("slia", [P, 4, 2], I32, att)
        selt = sb("selt", [P, 4, NE, 8], F32, att)

        names = """hin_ld hres_ld stat lnv rst xna xnh x16r xtp xte pjd pjh pjl sd mxd nmr exd phd phi pli pll ptd pta ptv pvd
            rid ond ash asl atp ate wod h1d st2 l2v l2r l2n l2h l2l x2p x2e rtd dld erd mhd cud cpd sld dsp outd vil vst
            kcp kic viz init chain pchain icp""".split()
        S = {n: sem(n) for n in names}

        def isb(p):
            return not isinstance(p, int) or p >= NPAIR_A

        def wait(eng, name, v):
            if isinstance(v, int) and v <= 0:
                return
            eng.wait_ge(S[name], v)
            if eng is nc.sync and not isinstance(v, int):
                fixed(eng)

        def fixed(eng):
            eng.nop(nofuse=True)

        class Chain:
            def __init__(self, name):
                self.name, self.n = name, 0

            def done(self, ins):
                ins.then_inc(S[self.name], 1)
                self.n = self.n + 1
                return ins

            def here(self, eng):
                eng.wait_ge(S[self.name], self.n)

        SLOTS = 11
        LAG_T, LAG_V = 2, 3

        def unit(u):
            return u // 4, u % 4

        def step_pe(pe, s, par, pre, pro, attn, post, place):
            pp, pa, pq = s, s - 1, s - 2
            qpar, apar = par, 1 - par

            def item(k):
                bank = pj[k % 2]
                if k == 0:
                    wait(pe, "xte", pp + 1)
                else:
                    wait(pe, "pjl", 10 * pp + k - 1)
                if k < 6:
                    for t in range(2):
                        c = t * HD + k * P
                        for n, (w, b, e) in enumerate(TERMS):
                            mm = pe.matmul(bank[:, t * 256:(t + 1) * 256], (wqkvh, wqkvl)[w][:, b, c:c + P],
                                           xt[:, qpar, e, :], start=n == 0, stop=n == 4)
                else:
                    j, hf = divmod(k - 6, 2)
                    c = 2 * HD + hf * 384
                    for n, (w, b, e) in enumerate(TERMS):
                        mm = pe.matmul(bank[:, 0:384], xt[:, qpar, e, j * P:(j + 1) * P],
                                       (wqkvh, wqkvl)[w][:, b, c:c + 384], start=n == 0, stop=n == 4)
                mm.then_inc(S["pjd"], 1)

            def transpose_x(p):
                wait(pe, "x16r", p + 1)
                wait(pe, "pjl", 10 * pp + 9)
                for j in range(2):
                    for b in range(3):
                        mm = pe.transpose(pjh[0][:, (3 * j + b) * P:(3 * j + b + 1) * P],
                                          x16[:, apar, j, b * P:(b + 1) * P], ident[:, :])
                mm.then_inc(S["xtp"], 1)

            for k in range(SLOTS):
                if attn and k < UNITS:
                    j, g = unit(k)
                    bank = sps[k % 2]
                    if k == 0:
                        wait(pe, "pjl", 10 * pa + 10)
                        if isb(pa):
                            wait(pe, "kic", 2 * (pa - 2) + 2)
                    wait(pe, "exd", 8 * pa + k - 1)
                    lo, n = (0, SEQ) if isb(pa) else (IT, P)
                    bk = bank[:, 0:3 * SEQ].rearrange("p (r c) -> p r c", r=3)[:, :, lo:SEQ]
                    pe.matmul(bk, identb[:, :], (maskt if isb(pa) else maski)[:, :, :], start=True, stop=False)
                    r0 = 64 * (g % 2)
                    for r in range(3):
                        m = 3 * (g // 2) + r
                        q = [qk[r0:r0 + 64, apar, z, m, 0, j, IT:SEQ] for z in range(2)]
                        kk = [qk[r0:r0 + 64, apar, z, m, 1, j, lo:SEQ] for z in range(2)]
                        o = bank[:, r * SEQ + lo:(r + 1) * SEQ]
                        pe.matmul(o, q[0], kk[0], start=False, stop=False)
                        pe.matmul(o, q[0], kk[1], start=False, stop=False)
                        mm = pe.matmul(o, q[1], kk[0], start=False, stop=r == 2)
                    mm.then_inc(S["sd"], 1)
                if pro and k < 10:
                    item(k)
                if pre and k == 10:
                    transpose_x(s + 1)
                if attn and LAG_T <= k < LAG_T + UNITS:
                    u = k - LAG_T
                    bank = ptp[u % 2]
                    wait(pe, "pll", 8 * pa + u + 1)
                    wait(pe, "ptv" if u % 2 else "pta", 4 * pa + u // 2)
                    for r in range(3):
                        pe.transpose(bank[:, r * P:(r + 1) * P], ph[:, u % 2, r, :], ident[:, :])
                        mm = pe.transpose(bank[:, (3 + r) * P:(4 + r) * P], pl[:, u % 2, r, :], ident[:, :])
                    if isb(pa):
                        mm = pe.transpose(bank[:, 6 * P:7 * P], pi[:, u % 2, :, :, :].rearrange("p r t c -> p (r t c)"),
                                          ident[:, :])
                    mm.then_inc(S["ptd"], 1)
                if post:
                    post_pe(pe, k, pq, 1 - apar)
                if attn and LAG_V <= k:
                    u = k - LAG_V
                    j, g = unit(u)
                    wait(pe, "ptv" if u % 2 else "pta", 4 * pa + u // 2 + 1)
                    if u % 2 == 0:
                        wait(pe, "ond", 4 * pa + u // 2)
                    if u == 0 and isb(pa):
                        wait(pe, "vil", 16 * 12 * (pa - 1))
                    z = u % 2 * 192
                    if isb(pa):
                        for w in range(2):
                            mm = pe.matmul(ops[:, z:z + 192], pt[:, u % 2, 6, :],
                                           vi[:, apar, j, w, g, :, :].rearrange("p r d -> p (r d)"), start=w == 0, stop=False)
                    for r in range(3):
                        o = ops[:, z + r * DH:z + (r + 1) * DH]
                        c = g * 192 + r * DH
                        st = not isb(pa)
                        pe.matmul(o, pt[:, u % 2, r, :], v16[:, apar, j, 0, c:c + DH], start=st, stop=False)
                        pe.matmul(o, pt[:, u % 2, r, :], v16[:, apar, j, 1, c:c + DH], start=False, stop=False)
                        mm = pe.matmul(o, pt[:, u % 2, 3 + r, :], v16[:, apar, j, 0, c:c + DH], start=False,
                                       stop=st or r == 2)
                    mm.then_inc(S["pvd"], 1)

        TERMS = [(0, 0, 0), (0, 1, 1), (0, 2, 2), (1, 0, 0), (1, 1, 1)]

        def post_pe(pe, k, p, par):
            if k < 4:
                j, z = divmod(k, 2)
                wait(pe, *(("cpd", p) if k == 0 else ("ate", 4 * p + k)))
                wait(pe, "asl", 4 * p + 2 * j + 2)
                for c in range(6):
                    mm = pe.transpose(poh[:, c * P:(c + 1) * P], a16[:, par, j, z, c * P:(c + 1) * P], ident[:, :])
                mm.then_inc(S["atp"], 1)
            if k == 4:
                wait(pe, "ate", 4 * p + 4)
                for j in range(2):
                    n = 0
                    for c in range(6):
                        for z, w in ((0, woh), (0, wol), (1, woh)):
                            mm = pe.matmul(po[:, j * D:(j + 1) * D], at[:, j, z, c, :], w[:, c, :], start=n == 0, stop=n == 17)
                            n += 1
                mm.then_inc(S["wod"], 1)
            if k == 7:
                wait(pe, "h1d", p + 1)
                wait(pe, "l2l", p + 1)
                for j in range(2):
                    for b in range(3):
                        mm = pe.transpose(poh[:, (3 * j + b) * P:(3 * j + b + 1) * P], x2_of(p)[:, j, b * P:(b + 1) * P], ident[:, :])
                mm.then_inc(S["x2p"], 1)
            if k == 8:
                wait(pe, "x2e", p + 1)
                for j in range(2):
                    for n, (w, b, e) in enumerate(TERMS):
                        mm = pe.matmul(po[:, j * NE:(j + 1) * NE], x2t[:, e, j * P:(j + 1) * P], (wrh, wrl)[w][:, b, :],
                                       start=n == 0, stop=n == 4)
                mm.then_inc(S["rtd"], 1)
            if k == 10:
                wait(pe, "mhd", p + 1)
                if isb(p):
                    pe.matmul(po[:, 0:32], tri[:, :], ma[:, :, :].rearrange("p a e -> p (a e)"), start=True, stop=False)
                    mm = pe.matmul(po[:, 0:32], ones[:, :], mb[:, :, :].rearrange("p a e -> p (a e)"), start=False, stop=True)
                elif p == 0:
                    mm = pe.matmul(po[:, 0:NE], ident[:, :], mimg[:, 0, :], start=True, stop=True)
                else:
                    im = mimg[:, :, :].rearrange("p t e -> p (t e)")
                    pe.matmul(po[:, 0:32], tri[:, :], im, start=True, stop=True)
                    for q in range(8):
                        mm = pe.matmul(po[:, 32 * (q + 1):32 * (q + 2)], rowmask[:, q, :], im, start=True, stop=True)
                mm.then_inc(S["cud"], 1)

        def step_dve(v, ch, s, par, pre, pro, attn, post, place):
            pp, pa, pq, pr = s, s - 1, s - 2, s - 3
            apar = 1 - par

            def norm(b):
                j, hb = divmod(b, 2)
                wait(v, "pvd", 8 * pa + 2 * b + 2)
                wait(v, "exd", 8 * pa + 2 * b + 2)
                wait(v, "asl", 4 * pa + b - 1)
                wait(v, "ond", 4 * pa + b)
                v.reciprocal(ri[:, :], rs[:, j, 2 * hb:2 * hb + 2, :].rearrange("p g r -> p (g r)")).then_inc(S["rid"], 1)
                wait(v, "rid", 4 * pa + b + 1)
                v.tensor_tensor(a32[:, b % 2, :, :], ops[:, 0:384].rearrange("p (h d) -> p h d", h=6),
                                ri[:, :].unsqueeze(2).broadcast_to((P, 6, DH)), ALU.mult).then_inc(S["ond"], 1)

            for k in range(SLOTS + 1):
                if attn and k < UNITS:
                    wait(v, "sd", 8 * pa + k + 1)
                    wait(v, "exd", 8 * pa + k - 1)
                    lo = 0 if isb(pa) else IT
                    v.tensor_reduce(nm[:, k % 2, :], sps[k % 2][:, 0:3 * SEQ].rearrange("p (r c) -> p r c", r=3)[:, :, lo:SEQ],
                                    X, ALU.max, negate=True).then_inc(S["mxd"], 1)
                if attn and 1 <= k <= UNITS:
                    u = k - 1
                    wait(v, "exd", 8 * pa + u + 1)
                    wait(v, "ptd", 8 * pa + u - 1)
                    v.tensor_copy(ph[:, u % 2, :, :], p32[:, u % 2, :, IT:SEQ]).then_inc(S["phd"], 1)
                    if isb(pa):
                        v.tensor_copy(pi[:, u % 2, 0:3, 0, :], p32[:, u % 2, :, 0:IT]).then_inc(S["phi"], 1)
                if attn and k >= 5 and k % 2 == 1:
                    norm((k - 5) // 2)
                if place and k == 0:
                    place_dve(v, ch, pr)
                if pro and k < 10:
                    n = k
                    wait(v, "pjh", 10 * pp + n + 1)
                    bank = pj[k % 2]
                    if k < 6:
                        v.scalar_tensor_tensor(qk[:, par, 1, n, :, :, IT:SEQ], bank[:, :].rearrange("p (t j c) -> p t j c", t=2, j=2),
                                               1.0 / WS, qk[:, par, 0, n, :, :, IT:SEQ], ALU.mult, ALU.subtract).then_inc(S["pjl"], 1)
                    else:
                        j, hf = divmod(k - 6, 2)
                        v.scalar_tensor_tensor(v16[:, par, j, 1, hf * 384:(hf + 1) * 384], bank[:, 0:384], 1.0 / WS,
                                               v16[:, par, j, 0, hf * 384:(hf + 1) * 384], ALU.mult, ALU.subtract).then_inc(S["pjl"], 1)
                if attn and LAG_T <= k < LAG_T + UNITS and k % 2 == 1:
                    u = k - LAG_T
                    wait(v, "ptd", 8 * pa + u + 1)
                    wait(v, "pvd", 8 * pa + u - 1)
                    evac_pt(v.tensor_copy, pa, u).then_inc(S["ptv"], 1)
                if pre and k == 2:
                    p = s + 1
                    wait(v, "hin_ld", 16 * (p + 1))
                    wait(v, "xna", 2 * p)
                    for j in range(2):
                        ch.done(v.bn_stats(bst[:, j, :], hin[:, (par + 1) % 2, j, :]))
                    ch.here(v)
                    fixed(v)
                    for j in range(2):
                        v.bn_aggr(mv[:, j, :], bst[:, j, :]).then_inc(S["stat"], 1)
                if pre and k == 4:
                    scaled(v, hin[:, (par + 1) % 2], mv, rstd, xn, s + 1, "rst", "x16r", "xna")
                if post and k < SLOTS:
                    post_dve(v, ch, k, pq)

        def evac_pt(f, pa, u):
            n = 7 if isb(pa) else 6
            return f(pt[:, u % 2, 0:n, :], ptp[u % 2][:, 0:n * P].rearrange("p (n c) -> p n c", n=n))

        def post_dve(v, ch, k, p):
            B = isb(p)
            if k == 4:
                wait(v, "wod", p + 1)
                wait(v, "hres_ld", 16 * (p + 1))
                wait(v, "outd", 32 * p)
                wait(v, "l2n", 2 * p)
                v.scalar_tensor_tensor(h1[:, :, :], po[:, 0:2 * D].rearrange("p (j n) -> p j n", j=2), 1.0 / WS, hres[:, p_par(p), :, :],
                                       ALU.mult, ALU.add).then_inc(S["h1d"], 1)
                wait(v, "h1d", p + 1)
                for j in range(2):
                    ch.done(v.bn_stats(bst2[:, j, :], h1[:, j, :]))
                ch.here(v)
                fixed(v)
                for j in range(2):
                    v.bn_aggr(mv2[:, j, :], bst2[:, j, :]).then_inc(S["st2"], 1)
            if k == 5:
                scaled(v, h1, mv2, rstd2, xn2, p, "l2r", "l2l", "l2n")
            if k == 8:
                wait(v, "rtd", p + 1)
                wait(v, "erd", p)
                ch.done(v.tensor_scalar(lg[:, :, :], po[:, 0:2 * NE].rearrange("p (j e) -> p j e", j=2), 1.0 / RS, None, ALU.mult))
                ch.here(v)
                fixed(v)
                for j in range(2):
                    ch.done(v.max(mx[:, j, :], lg[:, j, :]))
                ch.here(v)
                fixed(v)
                for j in range(2):
                    ch.done(v.max_index(mi[:, j, :], mx[:, j, :], lg[:, j, :]))
                v.tensor_tensor(dl[:, :, :], mx[:, :, :], mx[:, :, 0:1].broadcast_to((P, 2, 8)), ALU.subtract).then_inc(S["dld"], 1)
                ch.here(v)
                t0 = 2 * p if not B else None
                oht = oh[:, :, :, :] if B else ohimg[:, t0:t0 + 2, :, :]
                ixt = ix[:, :, :] if B else iximg[:, t0:t0 + 2, :]
                ch.done(v.tensor_copy(ixt, mi[:, :, 0:2]))
                ch.here(v)
                ch.done(v.tensor_tensor(oht, iota8[:, :].unsqueeze(1).unsqueeze(1).broadcast_to((P, 2, 2, NE)),
                                        ixt.unsqueeze(3).broadcast_to((P, 2, 2, NE)), ALU.is_equal))
                ch.here(v)
                if B:
                    wait(v, "cud", p)
                    ch.done(v.tensor_tensor(ma[:, 0:2, :], oht[:, :, 0, :], oht[:, :, 1, :], ALU.add))
                    ch.here(v)
                    ch.done(v.tensor_copy(mb[:, 1:3, :], ma[:, 0:1, :].broadcast_to((P, 2, NE))))
                    v.tensor_tensor(mb[:, 3, :], ma[:, 0, :], ma[:, 1, :], ALU.add).then_inc(S["mhd"], 1)
                    ch.here(v)
                else:
                    v.tensor_tensor(mimg[:, t0:t0 + 2, :], oht[:, :, 0, :], oht[:, :, 1, :], ALU.add).then_inc(S["mhd"], 1)
            if k == 9:
                wait(v, "erd", p + 1)
                ch.done(v.tensor_reduce(sm[:, 0:2], exr[:, :, :], X, ALU.add))
                ch.here(v)
                ch.done(v.reciprocal(sm[:, 2:4], sm[:, 0:2]))
                ch.here(v)
                ch.done(v.tensor_tensor(pk[:, :, :], exr[:, :, 0:2], sm[:, 2:4].unsqueeze(2).broadcast_to((P, 2, 2)), ALU.mult))
                ch.here(v)
                ch.done(v.tensor_reduce(sm[:, 4:6], pk[:, :, :], X, ALU.add))
                ch.here(v)
                ch.done(v.reciprocal(sm[:, 6:8], sm[:, 4:6]))
                ch.here(v)
                if B:
                    wait(v, "dsp", 64 * (p - 3))
                r_ = rows[:, PAR[0], :, :] if B else rimg[:, 2 * p:2 * p + 2, :]
                ch.done(v.tensor_tensor(r_[:, :, WC:WC + 2].bitcast(F32), pk[:, :, :], sm[:, 6:8].unsqueeze(2).broadcast_to((P, 2, 2)), ALU.mult))
                ch.done(v.tensor_copy(r_[:, :, EC].bitcast(F32), (ix[:, :, 0] if B else iximg[:, 2 * p:2 * p + 2, 0])))
                if B:
                    ch.done(v.tensor_copy(r_[:, :, TC], tid[:, :]))
                    ch.here(v)
                    ch.done(v.tensor_scalar(tid[:, :], tid[:, :], float(2 * SEQ), None, ALU.add))
            if k == 10:
                wait(v, "cud", p + 1)
                if B:
                    wait(v, "sld", p)
                    v.tensor_copy(c4[:, :], po[:, 0:32]).then_inc(S["cpd"], 1)
                elif p == 0:
                    v.tensor_copy(cimg[:, 0, :], po[:, 0:NE]).then_inc(S["cpd"], 1)
                else:
                    wait(v, "cpd", 1)
                    ch.done(v.tensor_copy(ipre[:, :].rearrange("p (t j e) -> p t j e", t=4, j=8),
                                          po[:, 32:288].rearrange("p (j t e) -> p t j e", j=8, t=4)))
                    ch.here(v)
                    v.tensor_copy(cimg[:, :, :], po[:, 0:32].rearrange("p (t e) -> p t e", t=4)).then_inc(S["cpd"], 1)

        def place_dve(v, ch, p):
            wait(v, "cpd", p + 1)
            if isb(p):
                b0 = 2 * (p - 2)
                cur = tb[:, bass.ds(b0 * NE, NE)].unsqueeze(1).broadcast_to((P, 2, NE))
                cc = c4[:, :].rearrange("p (a e) -> p a e", a=4)
                ch.done(v.tensor_tensor(pos[:, :, :], cc[:, 0:2, :], cur, ALU.add))
                ch.done(v.tensor_tensor(tb[:, bass.ds((b0 + 1) * NE, 2 * NE)].rearrange("p (a e) -> p a e", a=2), cc[:, 2:4, :], cur, ALU.add))
                ch.here(v)
                ch.done(v.tensor_tensor(pos[:, :, :], pos[:, :, :],
                                        ipre[:, bass.ds(b0 * NE, 2 * NE)].rearrange("p (a e) -> p a e", a=2), ALU.add))
                ch.here(v)
                slots(v, ch, ohp[:, :, :, :], oh[:, :, :, :], pos[:, :, :], pk2[:, :, :], sl[:, :, :], ov[:, :, :],
                      ix[:, :, :], sli[:, :, :], 2, "sld", p)
            elif p == 1:
                ip = ipre[:, :].rearrange("p (t j e) -> p t j e", t=4, j=8)
                for t in range(1, 4):
                    tot = ipre[:, (8 * t - 1) * NE:8 * t * NE]
                    ch.here(v)
                    ch.done(v.tensor_tensor(cimg[:, t, :], cimg[:, t, :], tot, ALU.add))
                    i = v.tensor_tensor(ip[:, t], ip[:, t], tot.unsqueeze(1).broadcast_to((P, 8, NE)), ALU.add)
                    if t < 3:
                        ch.done(i)
                    else:
                        i.then_inc(S["sld"], 2)

        def slots(v, ch, ohp_, oh_, pos_, pk_, sl_, ov_, ix_, sli_, n, name, p, also=lambda: None):
            ch.done(v.tensor_tensor(ohp_, oh_, pos_.unsqueeze(2).broadcast_to((P, n, 2, NE)), ALU.mult))
            ch.here(v)
            ch.done(v.tensor_reduce(pk_, ohp_, X, ALU.add))
            ch.here(v)
            ch.done(v.scalar_tensor_tensor(sl_, ix_, float(CAP), pk_, ALU.mult, ALU.add))
            ch.done(v.tensor_scalar(ov_, pk_, float(CAP), 65536.0, ALU.is_ge, ALU.mult))
            also()
            ch.here(v)
            if p is not None:
                wait(v, "dsp", 64 * (p - 2))
            v.tensor_tensor(sli_, sl_, ov_, ALU.add).then_inc(S[name], 1)

        def p_par(p):
            return PAR[0]

        PAR = [0]

        def step_act(a, s, par, pre, pro, attn, post, place):
            pp, pa, pq = s, s - 1, s - 2
            for k in range(SLOTS + 1):
                if attn and k < UNITS:
                    j, g = unit(k)
                    wait(a, "mxd", 8 * pa + k + 1)
                    wait(a, "pll", 8 * pa + k - 1)
                    if k % 2 == 0:
                        wait(a, "rid", 4 * (pa - 1) + k // 2 + 1)
                    lo = 0 if isb(pa) else IT
                    for r in range(3):
                        i = a.activation(p32[:, k % 2, r, lo:SEQ], sps[k % 2][:, r * SEQ + lo:(r + 1) * SEQ], ACT.Exp,
                                         bias=nm[:, k % 2, r:r + 1], accum_out=rs[:, j, g, r:r + 1])
                    i.then_inc(S["exd"], 1)
                if pre and k == 10:
                    wait(a, "xtp", s + 2)
                    a.activation(xt[:, 1 - par, :, :].rearrange("p b (j c) -> p j b c", j=2),
                                 pjh[0][:, 0:6 * P].rearrange("p (j b c) -> p j b c", j=2, b=3), ACT.Copy).then_inc(S["xte"], 1)
                if pro and k < 10:
                    n = k
                    wait(a, "pjd", 10 * pp + n + 1)
                    bank = pj[k % 2]
                    if k == 0:
                        wait(a, "sd", 8 * (pp - 1))
                        if isinstance(pp, int) and 2 <= pp < 4:
                            wait(a, "kcp", pp - 1)
                            wait(a, "vst", 32 * (pp - 1))
                    if k == 6:
                        wait(a, "pvd", 8 * (pp - 1))
                    if k < 6:
                        a.activation(qk[:, par, 0, n, :, :, IT:SEQ], bank[:, :].rearrange("p (t j c) -> p t j c", t=2, j=2),
                                     ACT.Copy, scale=1.0 / WS).then_inc(S["pjh"], 1)
                    else:
                        j, hf = divmod(k - 6, 2)
                        a.activation(v16[:, par, j, 0, hf * 384:(hf + 1) * 384], bank[:, 0:384], ACT.Copy,
                                     scale=1.0 / WS).then_inc(S["pjh"], 1)
                if attn and LAG_T <= k < LAG_T + UNITS and k % 2 == 0:
                    u = k - LAG_T
                    wait(a, "ptd", 8 * pa + u + 1)
                    wait(a, "pvd", 8 * pa + u - 1)
                    evac_pt(lambda o, i: a.activation(o, i, ACT.Copy), pa, u).then_inc(S["pta"], 1)
                if attn and k >= 5 and k % 2 == 1:
                    b = (k - 5) // 2
                    j, hb = divmod(b, 2)
                    wait(a, "ond", 4 * pa + b + 1)
                    if b == 0:
                        wait(a, "atp", 4 * (pa - 1))
                    a.activation(a16[:, 1 - par, j, 0, hb * 384:(hb + 1) * 384].rearrange("p (h d) -> p h d", h=6),
                                 a32[:, b % 2, :, :], ACT.Copy).then_inc(S["ash"], 1)
                if pre and k == 5:
                    wait(a, "xna", 2 * (s + 1) + 2)
                    wait(a, "xtp", s)
                    a.activation(x16[:, 1 - par, :, 0:D], xn[:, :, :], ACT.Copy).then_inc(S["xnh"], 1)
                if post:
                    p = pq
                    if k == 5:
                        wait(a, "l2n", 2 * p + 2)
                        if isb(p):
                            wait(a, "dsp", 64 * (p - 3))
                        a.activation(x2_of(p)[:, :, 0:D], xn2[:, :, :], ACT.Copy).then_inc(S["l2h"], 1)
                    if k < 4:
                        j, z = divmod(k, 2)
                        wait(a, "atp", 4 * p + k + 1)
                        a.activation(at[:, j, z, :, :], poh[:, 0:6 * P].rearrange("p (c q) -> p c q", c=6), ACT.Copy).then_inc(S["ate"], 1)
                    if k == 7:
                        wait(a, "x2p", p + 1)
                        a.activation(x2t[:, :, :].rearrange("p b (j c) -> p j b c", j=2),
                                     poh[:, 0:6 * P].rearrange("p (j b c) -> p j b c", j=2, b=3), ACT.Copy).then_inc(S["x2e"], 1)
                    if k == 8:
                        wait(a, "dld", p + 1)
                        a.activation(exr[:, :, :], dl[:, :, :], ACT.Exp).then_inc(S["erd"], 1)

        def inv_std(g, c, rstd_, mv_, var, name, p):
            wait(g, var, 2 * p + 2)
            fixed(g)
            c.done(g.tensor_scalar(rstd_, mv_[:, :, 1], EPS, None, ALU.add))
            c.here(g)
            g.tensor_tensor(rstd_, rstd_, halfc[:, 0:2], ALU.pow).then_inc(S[name], 1)

        def scaled(v, h_, mv_, rstd_, xn_, p, inv, split, name):
            wait(v, inv, p + 1)
            wait(v, split, p)
            fixed(v)
            for j in range(2):
                v.tensor_scalar(xn_[:, j, :], h_[:, j, :], mv_[:, j, 0:1], rstd_[:, j:j + 1], ALU.subtract, ALU.mult).then_inc(S[name], 1)

        def x2_of(p):
            return (rows[:, PAR[0], :, 0:D] if isb(p) else rimg[:, 2 * p:2 * p + 2, 0:D]).bitcast(F16)

        def step_pool(g, c, s, par, pre, pro, attn, post, place):
            pp, pa, pq, pr = s, s - 1, s - 2, s - 3
            apar = 1 - par

            def split_a(b):
                j, hb = divmod(b, 2)
                wait(g, "ash", 4 * pa + b + 1)
                dst = [a16[:, apar, j, z, hb * 384:(hb + 1) * 384].rearrange("p (h d) -> p h d", h=6) for z in range(2)]
                g.tensor_tensor(dst[1], a32[:, b % 2, :, :], dst[0], ALU.subtract).then_inc(S["asl"], 1)

            for k in range(SLOTS + 1):
                if pro and isb(pp) and k == 0:
                    wait(g, "sd", 8 * (pp - 1))
                    wait(g, "kcp", 2)
                    fixed(g)
                    for j in range(2):
                        g.tensor_copy(qk[:, par, :, :, 1, j, 0:IT],
                                      kimg[:, :, :, bass.ds((2 * (pp - 2) + j) * IT, IT)]).then_inc(S["kic"], 1)
                if attn and 1 <= k <= UNITS:
                    u = k - 1
                    wait(g, "phd", 8 * pa + u + 1)
                    if isb(pa):
                        wait(g, "phi", 8 * (pa - 2) + u + 1)
                        g.tensor_tensor(pi[:, u % 2, 0:3, 1, :], p32[:, u % 2, :, 0:IT], pi[:, u % 2, 0:3, 0, :], ALU.subtract).then_inc(S["pli"], 1)
                        wait(g, "pli", 8 * (pa - 2) + u + 1)
                    g.tensor_tensor(pl[:, u % 2, :, :], p32[:, u % 2, :, IT:SEQ], ph[:, u % 2, :, :], ALU.subtract).then_inc(S["pll"], 1)
                if place and isb(pr) and 1 <= k <= 4:
                    j, kk = divmod(k - 1, 2)
                    if k == 1:
                        wait(g, "sld", pr + 1)
                    fixed(g)
                    g.indirect_dma_start(xg_d, bass.IndirectOffsetOnAxis(ap=sli[:, j, kk:kk + 1], axis=0),
                                         rows[:, apar, j, :], None, bounds_check=NE * CAP - 1, oob_is_err=False).then_inc(S["dsp"], 16)
                if attn and k >= 5 and k % 2 == 1:
                    split_a((k - 5) // 2)
                if pre and k == 3:
                    inv_std(g, c, rstd[:, :], mv, "stat", "rst", s + 1)
                if pre and k == 6:
                    x_ = x16[:, (par + 1) % 2]
                    wait(g, "xnh", s + 2)
                    g.tensor_tensor(x_[:, :, D:2 * D], xn[:, :, :], x_[:, :, 0:D], ALU.subtract).then_inc(S["x16r"], 1)
                if post and k == 5:
                    inv_std(g, c, rstd2[:, :], mv2, "st2", "l2r", pq)
                if post and k == 6:
                    wait(g, "l2h", pq + 1)
                    x_ = x2_of(pq)
                    g.tensor_tensor(x_[:, :, D:2 * D], xn2[:, :, :], x_[:, :, 0:D], ALU.subtract).then_inc(S["l2l"], 1)
                if pro and not isb(pp) and k == 8:
                    wait(g, "pjl", 10 * pp + 6)
                    g.tensor_copy(kimg[:, :, :, 256 * pp:256 * (pp + 1)].rearrange("p z m (j c) -> p z m j c", j=2),
                                  qk[:, par, :, :, 1, :, IT:SEQ]).then_inc(S["kcp"], 1)

        def h_of(p):
            if isb(p):
                return txt[bass.ds(2 * (p - 2), 2)].rearrange("t p n -> p t n")
            return himg_d[256 * p:256 * (p + 1)].rearrange("(t p) n -> p t n", t=2)

        out_i = out[0:TOK, :].rearrange("(b s) n -> b s n", s=SEQ)

        def step_sp(sp, s, par, pre, pro, attn, post, place):
            pp, pa, pq = s, s - 1, s - 2
            if pre:
                p = s + 1
                wait(sp, "xna", 2 * (p - 1))
                wait(sp, "hin_ld", 16 * p)
                sp.dma_start(hin[:, (par + 1) % 2, :, :], h_of(p)).then_inc(S["hin_ld"], 16)
            if post:
                wait(sp, "h1d", pq - 1)
                wait(sp, "hres_ld", 16 * pq)
                sp.dma_start(hres[:, PAR[0], :, :], h_of(pq)).then_inc(S["hres_ld"], 16)
            if pro and isb(pp):
                wait(sp, "pvd", 8 * (pp - 1))
                wait(sp, "vil", 16 * 12 * (pp - 2))
                for j in range(2):
                    src = vimg_d[bass.ds((2 * (pp - 2) + j) * IT, IT)].rearrange("k z (g r d) -> k z g r d", g=4, r=3)
                    for r in range(3):
                        for t in range(2):
                            p0 = 32 * r + 16 * t
                            sp.dma_start(vi[p0:p0 + 16, par, j, :, :, r, :].rearrange("k z g d -> k (z g) d"),
                                         src[:, :, :, r, :].rearrange("k z g d -> k (z g) d")).then_inc(S["vil"], 16)
            if pro and not isb(pp):
                for j in range(2):
                    wait(sp, "pjl", 10 * pp + 8 + 2 * j)
                    r0 = 256 * pp + P * j
                    sp.dma_start(vimg_d[r0:r0 + P], v16[:, par, j, :, :]).then_inc(S["vst"], 16)
                if pp == 1:
                    sp.wait_ge(S["vst"], 64)
            if post:
                wait(sp, "h1d", pq + 1)
                for j in range(2):
                    if isb(pq):
                        dst = out_i[bass.ds(2 * (pq - 2) + j, 1), IT:SEQ, :].rearrange("o s n -> (o s) n")
                        sp.dma_start(dst, h1[:, j, :]).then_inc(S["outd"], 16)
                    else:
                        b0 = 8 * (2 * pq + j)
                        sp.dma_start(out_i[b0:b0 + 8, 0:IT, :], h1[:, j, :]).then_inc(S["outd"], 16)

        LOOP0, LOOP1 = 7, NPAIR - 1

        def stages(s):
            return dict(pre=0 <= s + 1 < NPAIR, pro=0 <= s < NPAIR, attn=0 <= s - 1 < NPAIR, post=0 <= s - 2 < NPAIR,
                        place=0 <= s - 3 < NPAIR)

        def run(eng, f, chain=None):
            for s in range(-1, LOOP0):
                n0 = chain.n if chain else 0
                PAR[0] = s % 2
                f(s, s % 2, stages(s))
            per = chain.n - n0 if chain else 0
            base = chain.n if chain else 0
            with eng.Fori(0, (LOOP1 - LOOP0) // 2) as i:
                for h in range(2):
                    if chain:
                        chain.n = (i * 2 + h) * per + base
                    PAR[0] = (LOOP0 + h) % 2
                    f(i * 2 + (LOOP0 + h), PAR[0], dict(pre=True, pro=True, attn=True, post=True, place=True))
            if chain:
                chain.n = base + per * (LOOP1 - LOOP0)
            for s in range(LOOP1, NPAIR + 3):
                PAR[0] = s % 2
                f(s, s % 2, stages(s))

        def finish_dve(v, ch):
            ch.done(v.tensor_tensor(selt[:, :, :, :], tb[:, 0:NI * NE].rearrange("p (t j e) -> p t e j", t=4, j=8),
                                    seli[:, :].unsqueeze(1).unsqueeze(1).broadcast_to((P, 4, NE, 8)), ALU.mult))
            ch.done(v.tensor_tensor(ppi[:, :], seli[:, :], iota8[:, :], ALU.mult))
            ch.here(v)
            ch.done(v.tensor_reduce(posa[:, :, :], selt[:, :, :, :], X, ALU.add))
            ch.done(v.tensor_reduce(pka[:, 0, 0:1], ppi[:, :], X, ALU.add))
            ch.here(v)
            ch.done(v.tensor_tensor(posa[:, :, :], posa[:, :, :], cimg[:, :, :], ALU.add))
            ch.done(v.scalar_tensor_tensor(tidi[:, :], pka[:, 0, 0:1].broadcast_to((P, 4)), float(SEQ - IT), ppos[:, :], ALU.mult, ALU.add))
            ch.here(v)
            slots(v, ch, ohpa[:, :, :, :], ohimg[:, :, :, :], posa[:, :, :], pka[:, :, :], sla[:, :, :], ova[:, :, :],
                  iximg[:, :, :], slia[:, :, :], 4, "init", None, lambda: ch.done(v.tensor_copy(rimg[:, :, TC], tidi[:, :])))

        def finish_pool(g, c):
            g.wait_ge(S["init"], 2)
            for t in range(4):
                for kk in range(2):
                    g.indirect_dma_start(xg_d, bass.IndirectOffsetOnAxis(ap=slia[:, t, kk:kk + 1], axis=0), rimg[:, t, :], None,
                                         bounds_check=NE * CAP - 1, oob_is_err=False).then_inc(S["dsp"], 16)
            g.wait_ge(S["dsp"], 64 * (NPAIR - NPAIR_A + 2))

        with nc.Block() as block:
            @block.sync
            def _(sp):
                sp.wait_ge(S["init"], 1)
                run(sp, lambda s, par, st: step_sp(sp, s, par, **st))
                sp.wait_ge(S["outd"], 32 * NPAIR)

            @block.gpsimd
            def _(g):
                c = Chain("pchain")
                c.done(g.memset(vi[:, :, :, :, :, :, :], 0.0))
                c.done(g.memset(pi[:, :, :, :, :], 0.0))
                c.done(g.memset(tb[:, :], 0.0))
                c.done(g.memset(ma[:, :, :], 0.0))
                c.done(g.memset(mb[:, :, :], 0.0))
                c.done(g.iota(tid[:, :], pattern=[[SEQ, 2]], base=IT, channel_multiplier=1, allow_small_or_imprecise_dtypes=True))
                c.done(g.iota(ppos[:, :], pattern=[[8 * SEQ, 4]], base=0, channel_multiplier=1, allow_small_or_imprecise_dtypes=True))
                c.here(g)
                g.memset(ppi[:, :], 0.0).then_inc(S["init"], 1)
                run(g, lambda s, par, st: step_pool(g, c, s, par, **st), c)
                finish_pool(g, c)

            @block.scalar
            def _(a):
                run(a, lambda s, par, st: step_act(a, s, par, **st))

            @block.vector
            def _(v):
                ch = Chain("chain")
                v.wait_ge(S["init"], 1)
                run(v, lambda s, par, st: step_dve(v, ch, s, par, **st), ch)
                finish_dve(v, ch)

            @block.tensor
            def _(pe):
                run(pe, lambda s, par, st: step_pe(pe, s, par, **st))
        att.close()

        xg = sb("xg", [P, 2, NB, ROW], I32)
        xgt = sb("xgt", [P, 2, 3, CAP], F16)
        wsel = sb("wsel", [P, 2, 3, NB], F32)
        tok = sb("tok", [P, 2, NB, 1], I32)
        w1h = sb("w1h", [P, 2, 3, FF], F16)
        w1l = sb("w1l", [P, 2, 2, FF], F16)
        w2h = sb("w2h", [P, 2, 6, D], F16)
        w2l = sb("w2l", [P, 2, 6, D], F16)
        b2s = sb("b2s", [P, 2, D], F32)
        g32 = sb("g32", [P, 2, HALF], F32)
        h16 = sb("h16", [P, 2, 2, 6, CAP], F16)
        y1 = sb("y1", [P, 2, D], F32)
        y2 = sb("y2", [P, NB, D], F32)
        f1b = [pj[0], pj[1], ops]
        f2b = [po[:, :], ptp[0][:, :].bitcast(F32)]
        xtb = [b[:, :].bitcast(F16) for b in sps]
        names = "mchain xgz w1d w2d b2d xld sel gtp gte w1hd w1ld w2hd w2ld f1d gld hhd hld f2d y1d y2d add".split()
        S.update({n: sem("m_" + n) for n in names})
        NX = (NB + 1) // 2
        NQ = 12
        F2AT = {0: 0, 2: 1, 4: 2, 6: 3, 8: 4, 9: 5, 11: 6}
        PREP0 = 7

        def m_sp(sp, t, par, prep, one, two):
            if prep:
                n, place = t + 1, 1 - par
                if not one:
                    wait(sp, "xgz", 1)
                wait(sp, "w1d", 16 * 4 * n)
                wait(sp, "w1ld", n - 1)
                e = bass.ds(n, 1)
                for b, parts in enumerate(KB):
                    for r, p0, k in parts:
                        sp.dma_start(stage[p0:p0 + k, place, b * FF:(b + 1) * FF], w1[e, r:r + k, :].rearrange("o r n -> (o r) n")).then_inc(S["w1d"], 16)
                wait(sp, "xld", 32 * n)
                wait(sp, "gtp", NX * (n - 1))
                wait(sp, "sel", 2 * (n - 1))
                sp.dma_start(xg[:, place, 0:FB, :], xg_d[bass.ds(n * CAP, FB * P), :].rearrange("(b p) n -> p b n", p=P)).then_inc(S["xld"], 16)
                sp.dma_start(xg[0:CAP - FB * P, place, FB, :], xg_d[bass.ds(n * CAP + FB * P, CAP - FB * P), :]).then_inc(S["xld"], 16)
                wait(sp, "w2d", 16 * n)
                wait(sp, "w2ld", n - 1)
                sp.dma_start(stage[:, place, 3 * FF:].rearrange("p (c n) -> p c n", n=D),
                             w2[e].rearrange("o (c p) n -> p (o c) n", p=P)).then_inc(S["w2d"], 16)
                wait(sp, "b2d", 16 * n)
                wait(sp, "y1d", NB * (n - 1))
                sp.dma_start(b2s[:, place, :], b2[e].broadcast_to((P, D))).then_inc(S["b2d"], 16)

        def m_pe(pe, t, par, prep, one, two):
            def rows_t(q):
                if q == 0:
                    wait(pe, "xld", 32 * (t + 2))
                wait(pe, "gte", NX * (t + 1) + q - 1)
                for b in range(2 * q, min(2 * q + 2, NB)):
                    for c in range(3):
                        o = xtb[q % 2][:, ((b % 2) * 3 + c) * P:((b % 2) * 3 + c) * P + BLK[b]]
                        mm = pe.transpose(o, xg[0:BLK[b], 1 - par, b, c * DH:(c + 1) * DH].bitcast(F16), ident[0:BLK[b], 0:BLK[b]])
                mm.then_inc(S["gtp"], 1)

            if one:
                wait(pe, "w1hd", t + 1)
                wait(pe, "w1ld", t + 1)
                wait(pe, "gte", NX * (t + 1))
            for q in range(NQ):
                if one:
                    m, hf = divmod(q, 2)
                    wait(pe, "gld", NQ * t + q - 2)
                    for n, (w, b, e) in enumerate(TERMS):
                        mm = pe.matmul(f1b[q % 3][:, 0:HALF], (w1h, w1l)[w][:, par, b, m * P:(m + 1) * P],
                                       xgt[:, par, e, hf * HALF:(hf + 1) * HALF], start=n == 0, stop=n == 4)
                    mm.then_inc(S["f1d"], 1)
                if two and q in F2AT:
                    u, tt, pr = F2AT[q], t - 1, 1 - par
                    if u == 0:
                        wait(pe, "hld", NQ * (tt + 1))
                        wait(pe, "w2hd", tt + 1)
                        wait(pe, "w2ld", tt + 1)
                    wait(pe, "y1d", NB * tt + u - (1 if u else 0))
                    n = 0
                    for c in range(6):
                        for z, w in ((0, w2h), (0, w2l), (1, w2h)):
                            mm = pe.matmul(f2b[u % 2][0:BLK[u], 0:D], h16[:, pr, z, c, u * P:u * P + BLK[u]], w[:, pr, c, :],
                                           start=n == 0, stop=n == 17)
                            n += 1
                    mm.then_inc(S["f2d"], 1)
                if prep and PREP0 <= q < PREP0 + NX:
                    rows_t(q - PREP0)

        def m_act(a, t, par, prep, one, two):
            def w1_hi():
                wait(a, "w1d", 16 * 4 * (t + 2))
                wait(a, "f1d", NQ * t)
                a.activation(w1h[:, 1 - par, :, :], stage[:, 1 - par, 0:3 * FF].rearrange("p (b n) -> p b n", b=3), ACT.Copy,
                             scale=WS).then_inc(S["w1hd"], 1)

            for q in range(NQ):
                if one:
                    m, hf = divmod(q, 2)
                    wait(a, "f1d", NQ * t + q + 1)
                    wait(a, "hld", NQ * t + q - 1)
                    fixed(a)
                    a.activation(g32[:, q % 2, :], f1b[q % 3][:, 0:HALF], ACT.Gelu, bias=b1t[:, bass.ds(t * 6 + m, 1)],
                                 scale=1.0 / WS).then_inc(S["gld"], 1)
                    if q == 0:
                        wait(a, "f2d", NB * (t - 1))
                    wait(a, "gld", NQ * t + q + 1)
                    a.activation(h16[:, par, 0, m, hf * HALF:(hf + 1) * HALF], g32[:, q % 2, :], ACT.Copy).then_inc(S["hhd"], 1)
                if one and q == 1:
                    wait(a, "w2d", 16 * (t + 1))
                    wait(a, "f2d", NB * (t - 1))
                    a.activation(w2h[:, par, :, :], stage[:, par, 3 * FF:].rearrange("p (c n) -> p c n", n=D), ACT.Copy,
                                 scale=WS).then_inc(S["w2hd"], 1)
                if prep and one and q == 3:
                    w1_hi()
                if two and q in F2AT:
                    u, tt = F2AT[q], t - 1
                    n = BLK[u]
                    wait(a, "y1d", NB * tt + u + 1)
                    if u == 0:
                        wait(a, "sel", 2 * (tt + 1))
                        wait(a, "add", 16 * NB * tt)
                    a.activation(y2[0:n, u, :], y1[0:n, u % 2, :], ACT.Copy, scale=wsel[0:n, 1 - par, 2, u:u + 1]).then_inc(S["y2d"], 1)
            if prep and not one:
                w1_hi()

        def m_dve(v, ch, t, par, prep, one, two):
            def w1_lo():
                wait(v, "w1hd", t + 2)
                v.scalar_tensor_tensor(w1l[:, 1 - par, :, :], stage[:, 1 - par, 0:2 * FF].rearrange("p (b n) -> p b n", b=2), WS,
                                       w1h[:, 1 - par, 0:2, :], ALU.mult, ALU.subtract).then_inc(S["w1ld"], 1)

            def rows_e(q):
                wait(v, "gtp", NX * (t + 1) + q + 1)
                for b in range(2 * q, min(2 * q + 2, NB)):
                    i = v.tensor_copy(xgt[:, 1 - par, :, b * P:b * P + BLK[b]],
                                      xtb[q % 2][:, (b % 2) * 3 * P:((b % 2) * 3 + 3) * P].rearrange("p (c n) -> p c n", c=3)[:, :, 0:BLK[b]])
                i.then_inc(S["gte"], 1)

            def choose():
                wait(v, "xld", 32 * (t + 1))
                wait(v, "add", 16 * NB * (t - 1))
                x_ = xg[:, par]
                wt = [x_[:, :, WC + z].bitcast(F32) for z in range(2)]
                fixed(v)
                for z, op in ((0, ALU.is_equal), (1, ALU.not_equal)):
                    ch.done(v.scalar_tensor_tensor(wsel[:, par, z, :], x_[:, :, EC].bitcast(F32), iota8[:, bass.ds(t, 1)],
                                                   wt[z], op, ALU.mult))
                v.tensor_copy(tok[:, par, :, 0], x_[:, :, TC]).then_inc(S["sel"], 1)
                ch.here(v)
                v.tensor_tensor(wsel[:, par, 2, :], wsel[:, par, 0, :], wsel[:, par, 1, :], ALU.add).then_inc(S["sel"], 1)

            if prep and not one:
                w1_lo()
                for q in range(NX):
                    rows_e(q)
            for q in range(NQ):
                if one:
                    m, hf = divmod(q, 2)
                    wait(v, "hhd", NQ * t + q + 1)
                    c = slice(hf * HALF, (hf + 1) * HALF)
                    v.tensor_tensor(h16[:, par, 1, m, c], g32[:, q % 2, :], h16[:, par, 0, m, c], ALU.subtract).then_inc(S["hld"], 1)
                if one and q == 1:
                    wait(v, "w2hd", t + 1)
                    v.scalar_tensor_tensor(w2l[:, par, :, :], stage[:, par, 3 * FF:].rearrange("p (c n) -> p c n", n=D), WS,
                                           w2h[:, par, :, :], ALU.mult, ALU.subtract).then_inc(S["w2ld"], 1)
                if prep and one and q == 3:
                    w1_lo()
                if one and q == 2:
                    choose()
                if two and q in F2AT:
                    u, tt = F2AT[q], t - 1
                    n = BLK[u]
                    wait(v, "f2d", NB * tt + u + 1)
                    wait(v, "y2d", NB * tt + u - (1 if u else 0))
                    if u == 0:
                        wait(v, "b2d", 16 * (tt + 1))
                    v.scalar_tensor_tensor(y1[0:n, u % 2, :], f2b[u % 2][0:n, 0:D], 1.0 / WS, b2s[0:n, 1 - par, :], ALU.mult,
                                           ALU.add).then_inc(S["y1d"], 1)
                if prep and one and PREP0 <= q < PREP0 + NX:
                    rows_e(q - PREP0)

        def m_pool(g, t, par, prep, one, two):
            if two:
                tt = t - 1
                for u, n in enumerate(BLK):
                    wait(g, "y2d", NB * tt + u + 1)
                    if u == 0:
                        wait(g, "sel", 2 * (tt + 1))
                        wait(g, "add", 16 * NB * tt)
                    fixed(g)
                    g.indirect_dma_start(out, bass.IndirectOffsetOnAxis(ap=tok[0:n, 1 - par, u, :], axis=0),
                                         y2[0:n, u, :], None, compute_op=ALU.add).then_inc(S["add"], 16)

        def steps(eng, f, chain=None):
            f(-1, 1, True, False, False)
            f(0, 0, True, True, False)
            base = chain.n if chain else 0
            per = base
            with eng.Fori(0, NE // 2 - 1) as i:
                for h in range(2):
                    if chain:
                        chain.n = (i * 2 + h) * per + base
                    f(i * 2 + (1 + h), 1 - h, True, True, True)
            if chain:
                chain.n = base + per * (NE - 2)
            f(NE - 1, 1, False, True, True)
            f(NE, 0, False, False, True)

        with nc.Block() as block:
            @block.sync
            def _(sp):
                steps(sp, lambda *a: m_sp(sp, *a))
                sp.wait_ge(S["add"], 16 * NB * NE)

            @block.gpsimd
            def _(g):
                steps(g, lambda *a: m_pool(g, *a))

            @block.scalar
            def _(a):
                steps(a, lambda *b: m_act(a, *b))

            @block.vector
            def _(v):
                v.memset(xg[:, :, FB, :], 0).then_inc(S["xgz"], 1)
                ch = Chain("mchain")
                steps(v, lambda *a: m_dve(v, ch, *a), ch)

            @block.tensor
            def _(pe):
                steps(pe, lambda *a: m_pe(pe, *a))


INS = ["x", "txt", "L0_tok_ln_gamma", "L0_tok_ln_beta", "L0_tok_W", "L0_tok_b", "L0_attn_W_Q", "L0_attn_W_K", "L0_attn_W_V",
       "L0_attn_W_O", "L0_ffn_Wr", "L0_ffn_w1", "L0_ffn_b1", "L0_ffn_w2", "L0_ffn_b2"]


def kernel(**inputs):
    import numpy as np
    import concourse.bacc as bacc
    from concourse.bass_utils import run_bass_kernel_spmd

    nc = bacc.Bacc("TRN2", target_bir_lowering=False, num_devices=1)
    arrays, args = {}, []
    for name in INS:
        a = np.ascontiguousarray(inputs[name])
        arrays[f"in_{name}"] = a
        args.append(nc.dram_tensor(f"in_{name}", a.shape, mybir.dt.from_np(a.dtype), kind="ExternalInput").ap())
    out = nc.dram_tensor("out", (TOK + CAP, D), F32, kind="ExternalOutput").ap()
    build(nc, *args, out)
    r = run_bass_kernel_spmd(nc, [arrays], core_ids=[0])
    return r.results[0]["out"][:TOK].reshape(NI, SEQ, D)
```

```python
from contextlib import ExitStack

import concourse.bass as bass
from concourse import mybir

F32 = mybir.dt.float32
F16 = mybir.dt.float16
BF16 = mybir.dt.bfloat16
I32 = mybir.dt.int32
U32 = mybir.dt.uint32
ALU = mybir.AluOpType
ACT = mybir.ActivationFunctionType
X = mybir.AxisListType.X

P = 128
EPS = 1e-5
D = 192
NI, IT, TT = 32, 16, 128
SEQ = IT + TT
TOK = NI * SEQ
H, DH = 12, 64
HD = H * DH
NE, FF = 8, 768
CAP = int(TOK / NE * 1.5)
WC, EC, TC, ROW = D, D + 2, D + 3, D + 4
XP = 18
WS = 64.0
QS = 8.0
RS = 1024.0
NPAIR_A = 2
NPAIR = NPAIR_A + NI // 2
UNITS = 8
KB = [[(0, 0, 128)], [(128, 0, 64), (0, 64, 64)], [(64, 0, 128)]]
BLK = [P] * (CAP // P) + ([CAP % P] if CAP % P else [])
NB = len(BLK)
FB = CAP // P
HALF = CAP // 2
NQ = 12


def head_of(pos):
    g, r = divmod(pos, 3)
    return 6 * (g // 2) + g % 2 + 2 * r


TERMS = [(0, 0, 0), (0, 1, 1), (0, 2, 2), (1, 0, 0), (1, 1, 1)]


def build(nc, x, txt, gam, bet, wemb, bemb, wq, wk, wv, wo, wr, w1, b1, w2, b2, out):
    himg_d = nc.dram_tensor("himg_d", (NI * IT, D), F32, kind="Internal").ap()
    vimg_d = nc.dram_tensor("vimg_d", (NI * IT, 2, HD), F16, kind="Internal").ap()
    xg_d = nc.dram_tensor("xg_d", (NE * CAP, ROW), I32, kind="Internal").ap()

    with ExitStack() as ctx:
        def sb(name, shape, dt, c=ctx):
            return c.enter_context(nc.sbuf_tensor(name, shape, dt))

        def sem(name):
            return ctx.enter_context(nc.semaphore(name))

        def ps(name, shape, dt):
            return ctx.enter_context(nc.psum_tensor(name, shape, dt))

        ident = sb("ident", [P, P], F16)
        identb = sb("identb", [P, P], BF16)
        maskt = sb("maskt", [P, 3, SEQ], BF16)
        maski = sb("maski", [P, 3, P], BF16)
        tri = sb("tri", [P, P], F16)
        ones = sb("ones", [P, P], F16)
        rowmask = sb("rowmask", [P, 8, P], F16)
        seli = sb("seli", [P, 8], F32)
        iota8 = sb("iota8", [P, NE], F32)
        zrow = sb("zrow", [P, NB, ROW], I32)
        zid = zrow[:, :, ROW - 1:ROW]
        halfc = sb("halfc", [P, 4], F32)
        wqkvh = sb("wqkvh", [P, 3, 3 * HD], F16)
        wqkvl = sb("wqkvl", [P, 2, 3 * HD], F16)
        woh = sb("woh", [P, 6, D], F16)
        wol = sb("wol", [P, 6, D], F16)
        wr32 = sb("wr32", [P, 3, NE], F32)
        wrh = sb("wrh", [P, 3, NE], F16)
        wrl = sb("wrl", [P, 2, NE], F16)
        b1t = sb("b1t", [P, NE * 6], F32)
        stage = sb("stage", [P, 2, 3 * FF + 6 * D], F32)

        pj = [ps(f"pj{i}", [P, 512], F32) for i in range(2)]
        sps = [ps(f"sps{i}", [P, 512], F32) for i in range(2)]
        ptp = [ps(f"ptp{i}", [P, 1024], F16) for i in range(2)]
        ops = ps("ops", [P, 512], F32)
        po = ps("po", [P, 512], F32)
        poh = po[:, :].bitcast(F16)
        pjh = [b[:, :].bitcast(F16) for b in pj]

        early = ExitStack()
        raw = sb("raw", [P, 3, XP, 64], F32, early)
        pad = sb("pad", [P, 3, XP, 66], F32, early)
        wst = sb("wst", [P, 2, 15, D], F32, early)
        wg = sb("wg", [P, 30, D], F32, early)
        weh = sb("weh", [P, 30, D], F16, early)
        wel = sb("wel", [P, 30, D], F16, early)
        b1r = sb("b1r", [NE * 6, P], F32, early)
        identf = sb("identf", [P, P], F32, early)
        gm = sb("gm", [P, 2, 15], F32, early)
        gm64 = sb("gm64", [P, 30], F32, early)
        bt = sb("bt", [P, 2, 15], F32, early)
        bb = sb("bb", [P, D], F32, early)
        cb = sb("cb", [P, D], F32, early)
        est = sb("est", [P, 4, 15, 6], F32, early)
        emv = sb("emv", [P, 4, 2], F32, early)
        eve = sb("eve", [P, 4], F32, early)
        eng = sb("eng", [P, 4], F32, early)
        enm = sb("enm", [P, 4], F32, early)
        ers = sb("ers", [P, 4], F32, early)
        nx = raw[:, :, :, :].rearrange("p c r w -> p (c r w)")[:, 0:9 * XP * 16].rearrange("p (s r c) -> p s r c", s=3, c=16)
        nxh = sb("nxh", [P, 2, 3, 3 * XP * 16], F16, early)
        nxl = sb("nxl", [P, 2, 3, 3 * XP * 16], F16, early)
        tte = sb("tte", [P, 60, P], F16, early)
        him = sb("him", [P, 4, D], F32, early)

        c_set = sem("c_set")
        ld_x = sem("ld_x")
        ld_gm = sem("ld_gm")
        ld_bt = sem("ld_bt")
        ld_we = [sem(f"ld_we{a}") for a in range(2)]
        ld_g = sem("ld_g")
        ld_w = [sem(f"ld_w{n}") for n in range(4)]
        sp_hi = sem("sp_hi")
        sp_lo = sem("sp_lo")
        ec = sem("ec")
        e_wg = sem("e_wg")
        e_wh = sem("e_wh")
        e_wl = sem("e_wl")
        e_beta = sem("e_beta")
        e_var = sem("e_var")
        e_cb = sem("e_cb")
        e_rs = sem("e_rs")
        e_nx = sem("e_nx")
        e_hi = sem("e_hi")
        e_lo = sem("e_lo")
        e_tp = sem("e_tp")
        e_ta = sem("e_ta")
        e_td = sem("e_td")
        e_mm = sem("e_mm")
        e_him = sem("e_him")
        e_st = sem("e_st")
        pref = sem("pref")

        def load192(eng, dst, src, s):
            n = 0
            for b, parts in enumerate(KB):
                for r, p0, k in parts:
                    eng.dma_start(dst(b, p0, k), src(r, k)).then_inc(s, 16)
                    n += 1
            return n

        SPLITS = [(0, 0), (1, 1), (2, 0), (3, 1)]

        LDW = [16 * 6, 16 * 12, 16 * 6, 16 * (12 + 4)]

        def split_hi(a, n, what, place):
            a.wait_ge(ld_w[n], LDW[n])
            if what < 3:
                a.activation(wqkvh[:, what, 0:HD], stage[:, place, 0:HD], ACT.Copy, scale=QS)
                a.activation(wqkvh[:, what, HD:3 * HD], stage[:, place, HD:3 * HD], ACT.Copy, scale=WS).then_inc(sp_hi, 1)
            else:
                a.activation(wrh[:, :, :], wr32[:, :, :], ACT.Copy, scale=RS)
                a.activation(woh[:, :, :], stage[:, place, 0:6 * D].rearrange("p (c n) -> p c n", n=D),
                             ACT.Copy, scale=WS).then_inc(sp_hi, 1)

        def split_lo(v, n, what, place):
            v.wait_ge(ld_w[n], LDW[n])
            v.wait_ge(sp_hi, n + 1)
            if what < 2:
                v.scalar_tensor_tensor(wqkvl[:, what, 0:HD], stage[:, place, 0:HD], QS, wqkvh[:, what, 0:HD],
                                       ALU.mult, ALU.subtract)
                v.scalar_tensor_tensor(wqkvl[:, what, HD:3 * HD], stage[:, place, HD:3 * HD], WS,
                                       wqkvh[:, what, HD:3 * HD], ALU.mult, ALU.subtract).then_inc(sp_lo, 1)
            elif what == 3:
                v.scalar_tensor_tensor(wrl[:, :, :], wr32[:, 0:2, :], RS, wrh[:, 0:2, :], ALU.mult, ALU.subtract)
                v.scalar_tensor_tensor(wol[:, :, :], stage[:, place, 0:6 * D].rearrange("p (c n) -> p c n", n=D), WS,
                                       woh[:, :, :], ALU.mult, ALU.subtract).then_inc(sp_lo, 1)

        TBANK = [ptp[0][:, :], ptp[1][:, :]] + [b[:, :].bitcast(F16) for b in sps]
        TSIZE = [8, 8, 8, 6]

        def evac_t(eng, w, z, odd):
            for q in range(odd, 4, 2):
                n = TSIZE[q]
                eng.wait_ge(e_tp, 8 * w + 4 * z + q + 1)
                if w and q == odd:
                    eng.wait_ge(e_mm, 2 * (w - 1) + z + 1)
                dst = tte[:, 30 * z + 8 * q:30 * z + 8 * q + n, :]
                src = TBANK[q][:, 0:n * P].rearrange("p (n q) -> p n q", n=n)
                if odd:
                    eng.tensor_copy(dst, src).then_inc(e_td, 1)
                else:
                    eng.activation(dst, src, ACT.Copy).then_inc(e_ta, 1)

        OFF = [(1, 1), (1, 0), (1, 2), (0, 1), (2, 1)]

        with nc.Block() as block:
            @block.sync
            def _(sp):
                xr = raw[:, :, :, :]
                sp.wait_ge(ec, 2)
                v = x.rearrange("b c h w -> b c (h w)")
                for hy in range(4):
                    a, b = max(16 * hy - 1, 0), min(16 * hy + 17, 64)
                    d0 = a - (16 * hy - 1)
                    sp.dma_start(xr[hy:P:4].rearrange("p c r w -> p c (r w)")[:, :, d0 * 64:(d0 + b - a) * 64],
                                 v[:, :, a * 64:b * 64]).then_inc(ld_x, 16)
                sp.dma_start(gm[:, :, :], gam.rearrange("(a q f) -> q a f", a=2, q=P)).then_inc(ld_gm, 16)
                sp.dma_start(bt[:, :, :], bet.rearrange("(a q f) -> q a f", a=2, q=P)).then_inc(ld_bt, 16)
                wv_ = wemb.rearrange("(a q f) n -> q a (f n)", a=2, q=P)
                for a in range(2):
                    sp.dma_start(wst[:, a, :, :].rearrange("q f n -> q (f n)"), wv_[:, a, :]).then_inc(ld_we[a], 16)
                sp.dma_start(bb[:, :], bemb.rearrange("(o n) -> o n", o=1).broadcast_to((P, D))).then_inc(ld_g, 16)
                sp.dma_start(b1r[:, :], b1.rearrange("e (c p) -> (e c) p", p=P)).then_inc(ld_g, 16)
                for lot, (what, place) in enumerate(SPLITS):
                    if what < 3:
                        if what == 2:
                            sp.wait_ge(sp_hi, 1)
                            sp.wait_ge(sp_lo, 1)
                        for r, p0, k in KB[what]:
                            for n, w in ((0, wq), (1, wk)):
                                sp.dma_start(stage[p0:p0 + k, place, n * HD:(n + 1) * HD].rearrange("p (h d) -> p h d", h=H),
                                             w[:, r:r + k, :].rearrange("h m d -> m h d")).then_inc(ld_w[lot], 16)
                            for g in range(4):
                                h0 = head_of(3 * g)
                                sp.dma_start(stage[p0:p0 + k, place, 2 * HD + g * D:2 * HD + (g + 1) * D]
                                             .rearrange("p (r d) -> p r d", r=3),
                                             wv[h0:h0 + 5:2, r:r + k, :].rearrange("h m d -> m h d")).then_inc(ld_w[lot], 16)
                    else:
                        sp.wait_ge(sp_hi, 2)
                        sp.wait_ge(sp_lo, 2)
                        for pos in range(H):
                            p0, h = 64 * (pos % 2), head_of(pos)
                            sp.dma_start(stage[p0:p0 + 64, 1, pos // 2 * D:(pos // 2 + 1) * D],
                                         wo[h * DH:(h + 1) * DH, :]).then_inc(ld_w[lot], 16)
                        load192(sp, lambda b, p0, k: wr32[p0:p0 + k, b, :], lambda r, k: wr[r:r + k, :], ld_w[lot])
                sp.wait_ge(c_set, 21)
                for e in range(NE):
                    sp.dma_start(xg_d[e * CAP:e * CAP + FB * P, :].rearrange("(b p) n -> p b n", p=P), zrow[:, 0:FB, :]).then_inc(pref, 16)
                    sp.dma_start(xg_d[e * CAP + FB * P:(e + 1) * CAP, :], zrow[0:CAP - FB * P, FB, :]).then_inc(pref, 16)
                zf = zrow[:, :, 0:D].bitcast(F32)
                sp.dma_start(out[TOK:TOK + FB * P, :].rearrange("(b p) n -> p b n", p=P), zf[:, 0:FB, :]).then_inc(pref, 16)
                sp.dma_start(out[TOK + FB * P:TOK + CAP, :], zf[0:CAP - FB * P, FB, :]).then_inc(pref, 16)
                hv = himg_d.rearrange("(p w) n -> p w n", w=4)
                sp.wait_ge(e_him, 4)
                sp.dma_start(hv, him[:, :, :]).then_inc(e_st, 16)
                sp.wait_ge(e_st, 16)
                sp.wait_ge(pref, 16 * (2 * NE + 2))

            @block.gpsimd
            def _(g):
                g.memset(ident[:, :], 0.0).then_inc(c_set, 1)
                g.memset(identb[:, :], 0.0).then_inc(c_set, 1)
                g.memset(maskt[:, :, :], 0.0).then_inc(c_set, 1)
                g.memset(maski[:, :, :], 0.0).then_inc(c_set, 1)
                g.memset(tri[:, :], 1.0).then_inc(c_set, 1)
                g.memset(ones[:, :], 1.0).then_inc(c_set, 1)
                g.memset(rowmask[:, :, :], 1.0).then_inc(c_set, 1)
                g.memset(seli[:, :], 1.0).then_inc(c_set, 1)
                g.memset(zrow[:, :, :], 0).then_inc(c_set, 1)
                g.memset(halfc[:, :], -0.5).then_inc(c_set, 1)
                g.memset(identf[:, :], 0.0).then_inc(c_set, 1)
                g.wait_ge(c_set, 11)
                for m in (ident, identb, identf):
                    g.affine_select(out=m[:, :], in_=m[:, :], compare_op=ALU.not_equal, fill=1.0, base=0,
                                    pattern=[[-1, P]], channel_multiplier=1).then_inc(c_set, 1)
                g.affine_select(out=maskt[:, :, :], in_=maskt[:, :, :], compare_op=ALU.is_ge, fill=-1e30, base=IT,
                                pattern=[[0, 3], [-1, SEQ]], channel_multiplier=1).then_inc(c_set, 1)
                g.affine_select(out=maski[:, :, :], in_=maski[:, :, :], compare_op=ALU.is_ge, fill=-1e30, base=0,
                                pattern=[[0, 3], [-1, P]], channel_multiplier=1).then_inc(c_set, 1)
                g.affine_select(out=tri[:, :], in_=tri[:, :], compare_op=ALU.is_gt, fill=0.0, base=0,
                                pattern=[[1, P]], channel_multiplier=-1).then_inc(c_set, 1)
                g.affine_select(out=rowmask[:, :, :], in_=rowmask[:, :, :], compare_op=ALU.is_gt, fill=0.0, base=IT,
                                pattern=[[IT, 8], [0, P]], channel_multiplier=-1).then_inc(c_set, 1)
                g.affine_select(out=seli[:, :], in_=seli[:, :], compare_op=ALU.is_gt, fill=0.0, base=IT,
                                pattern=[[IT, 8]], channel_multiplier=-1).then_inc(c_set, 1)
                g.iota(iota8[:, :], pattern=[[1, NE]], base=0, channel_multiplier=0,
                       allow_small_or_imprecise_dtypes=True).then_inc(c_set, 1)
                g.iota(zid, pattern=[[P, NB], [1, 1]], base=TOK, channel_multiplier=1).then_inc(c_set, 1)
                g.wait_ge(c_set, 21)
                g.affine_select(out=seli[:, :], in_=seli[:, :], compare_op=ALU.is_ge, fill=0.0, base=0,
                                pattern=[[-IT, 8]], channel_multiplier=1).then_inc(c_set, 1)
                for j in range(8):
                    g.affine_select(out=maski[:, :, j * IT:(j + 1) * IT], in_=maski[:, :, j * IT:(j + 1) * IT],
                                    compare_op=ALU.is_gt, fill=-1e30, base=(j + 1) * IT,
                                    pattern=[[0, 3], [0, IT]], channel_multiplier=-1).then_inc(c_set, 1)
                def weights(a):
                    if a == 0:
                        g.wait_ge(ld_gm, 16)
                        g.tensor_scalar(gm64[:, :], gm[:, :, :].rearrange("p a f -> p (a f)"), WS, None, ALU.mult).then_inc(e_wg, 1)
                        g.wait_ge(e_wg, 1)
                    g.wait_ge(ld_we[a], 16)
                    g.tensor_tensor(wg[:, 15 * a:15 * a + 15, :], wst[:, a, :, :],
                                    gm64[:, 15 * a:15 * a + 15].unsqueeze(2).broadcast_to((P, 15, D)), ALU.mult).then_inc(e_wg, 1)

                def scale(w):
                    g.wait_ge(e_var, w + 1)
                    g.tensor_tensor(ers[:, w:w + 1], eve[:, w:w + 1], halfc[:, 0:1], ALU.pow).then_inc(e_rs, 1)
                    g.wait_ge(e_rs, 2 * w + 1)
                    g.tensor_tensor(enm[:, w:w + 1], eng[:, w:w + 1], ers[:, w:w + 1], ALU.mult).then_inc(e_rs, 1)

                weights(0)
                scale(0)
                weights(1)
                for w in range(4):
                    g.wait_ge(e_nx, w + 1)
                    g.wait_ge(e_hi, w + 1)
                    if w >= 2:
                        g.wait_ge(e_tp, 8 * (w - 1))
                    g.tensor_tensor(nxl[:, w % 2], nx[:, :, :, :].rearrange("p s r c -> p s (r c)"), nxh[:, w % 2], ALU.subtract).then_inc(e_lo, 1)
                    if w < 3:
                        scale(w + 1)

            @block.scalar
            def _(a):
                def window(w):
                    if w:
                        a.wait_ge(e_lo, w)
                        a.wait_ge(e_hi, w)
                    a.wait_ge(e_rs, 2 * w + 2)
                    rows_ = pad[:, :, :, 16 * w:16 * w + 16].rearrange("p c r w -> p (c r) w")
                    shifted = bass.AP(tensor=rows_.tensor, offset=rows_.offset, ap=[rows_.ap[0], [1, 3], rows_.ap[1], rows_.ap[2]])
                    a.activation(nx[:, :, :, :], shifted, ACT.Identity, bias=enm[:, w:w + 1], scale=ers[:, w:w + 1]).then_inc(e_nx, 1)
                    if w >= 2:
                        a.wait_ge(e_tp, 8 * (w - 1))
                    a.activation(nxh[:, w % 2].rearrange("p s (r c) -> p s r c", c=16), shifted, ACT.Identity,
                                 bias=enm[:, w:w + 1], scale=ers[:, w:w + 1]).then_inc(e_hi, 1)

                def weights(h):
                    a.wait_ge(e_wg, 2 + h)
                    a.activation(weh[:, 15 * h:15 * h + 15, :], wg[:, 15 * h:15 * h + 15, :], ACT.Copy).then_inc(e_wh, 1)

                weights(0)
                window(0)
                weights(1)
                for w in range(4):
                    evac_t(a, w, 0, 0)
                    if w < 3:
                        window(w + 1)
                    evac_t(a, w, 1, 0)
                    split_hi(a, w, *SPLITS[w])

            @block.vector
            def _(v):
                v.memset(raw[:, :, 0, :], 0.0).then_inc(ec, 1)
                v.memset(raw[:, :, XP - 1, :], 0.0).then_inc(ec, 1)
                v.memset(pad[:, :, :, :], 0.0).then_inc(ec, 1)
                v.wait_ge(ec, 3)
                v.wait_ge(ld_x, 64)
                v.tensor_copy(pad[:, :, :, 1:65], raw[:, :, :, :]).then_inc(ec, 1)
                v.wait_ge(ec, 4)

                def stats(w):
                    for s, (r0, c0) in enumerate(OFF):
                        for c in range(3):
                            last = v.bn_stats(est[:, w, 3 * s + c, :],
                                              pad[:, c, r0:r0 + 16, c0 + 16 * w:c0 + 16 * w + 16])
                    last.then_inc(ec, 1)
                    v.wait_ge(ec, 5 + 2 * w)
                    v.bn_aggr(emv[:, w, :], est[:, w, :, :].rearrange("p a b -> p (a b)")).then_inc(ec, 1)
                    v.wait_ge(ec, 6 + 2 * w)
                    v.tensor_scalar(eng[:, w:w + 1], emv[:, w, 0:1], -1.0, None, ALU.mult)
                    v.tensor_scalar(eve[:, w:w + 1], emv[:, w, 1:2], EPS, None, ALU.add).then_inc(e_var, 1)

                def weights(h):
                    v.wait_ge(e_wh, h + 1)
                    v.tensor_tensor(wel[:, 15 * h:15 * h + 15, :], wg[:, 15 * h:15 * h + 15, :],
                                    weh[:, 15 * h:15 * h + 15, :], ALU.subtract).then_inc(e_wl, 1)

                def out_of_psum(w):
                    v.wait_ge(e_mm, 2 * w + 2)
                    v.wait_ge(e_cb, 1)
                    v.scalar_tensor_tensor(him[:, w, :], ops[:, 0:D], 1.0 / WS, cb[:, :], ALU.mult, ALU.add).then_inc(e_him, 1)

                stats(0)
                stats(1)
                weights(0)
                weights(1)
                for w in range(4):
                    evac_t(v, w, 0, 1)
                    if w:
                        out_of_psum(w - 1)
                    evac_t(v, w, 1, 1)
                    if w < 2:
                        stats(w + 2)
                    if w == 0:
                        v.wait_ge(e_beta, 1)
                        v.wait_ge(ld_g, 32)
                        v.tensor_tensor(cb[:, :], po[:, 0:D], bb[:, :], ALU.add).then_inc(e_cb, 1)
                        v.wait_ge(e_beta, 2)
                        v.tensor_copy(b1t[:, :], pj[0][:, 0:NE * 6])
                    split_lo(v, w, *SPLITS[w])
                out_of_psum(3)

            @block.tensor
            def _(pe):
                pe.wait_ge(ld_bt, 16)
                for n in range(30):
                    if n % 15 == 0:
                        pe.wait_ge(ld_we[n // 15], 16)
                    mm = pe.matmul(po[:, 0:D], bt[:, n // 15, n % 15:n % 15 + 1].broadcast_to((P, P)), wst[:, n // 15, n % 15, :],
                                   start=n == 0, stop=n == 29)
                mm.then_inc(e_beta, 1)

                def transposes(w, z):
                    pe.wait_ge((e_hi, e_lo)[z], w + 1)
                    for q in range(4):
                        k = 4 * w + 2 * z - 1 + q // 2
                        if w or z:
                            pe.wait_ge(e_td if q % 2 else e_ta, k)
                        for i in range(TSIZE[q]):
                            a, f = divmod(8 * q + i, 15)
                            s, c = divmod(f, 3)
                            r0, c0 = OFF[s]
                            at0 = (c * XP + r0 + 8 * a) * 16
                            mm = pe.transpose(TBANK[q][:, i * P:(i + 1) * P], (nxh, nxl)[z][:, w % 2, c0, at0:at0 + P], ident[:, :])
                        mm.then_inc(e_tp, 1)

                def products(w, z):
                    pe.wait_ge(e_ta, 4 * w + 2 * z + 2)
                    pe.wait_ge(e_td, 4 * w + 2 * z + 2)
                    if z == 0 and w:
                        pe.wait_ge(e_him, w)
                    for n in range(30):
                        mm = pe.matmul(ops[:, 0:D], tte[:, 30 * z + n, :], weh[:, n, :], start=z == 0 and n == 0, stop=z == 1 and n == 29)
                        if z == 0:
                            mm = pe.matmul(ops[:, 0:D], tte[:, n, :], wel[:, n, :], start=False, stop=False)
                    mm.then_inc(e_mm, 1)

                pe.wait_ge(c_set, 30)
                transposes(0, 0)
                transposes(0, 1)
                pe.wait_ge(ld_g, 32)
                pe.transpose(pj[0][:, 0:NE * 6], b1r[:, :], identf[0:NE * 6, 0:NE * 6]).then_inc(e_beta, 1)
                pe.wait_ge(e_wl, 2)
                for w in range(4):
                    products(w, 0)
                    if w < 3:
                        transposes(w + 1, 0)
                    products(w, 1)
                    if w < 3:
                        transposes(w + 1, 1)
        early.close()

        w1h = sb("w1h", [P, 2, 3, FF], F16)
        w1l = sb("w1l", [P, 2, 2, FF], F16)
        att = ExitStack()
        hin = sb("hin", [P, 2, 2, D], F32, att)
        hres = sb("hres", [P, 2, 2, D], F32, att)
        bst = sb("bst", [P, 2, 6], F32, att)
        mv = sb("mv", [P, 2, 2], F32, att)
        rstd = sb("rstd", [P, 2], F32, att)
        xn = sb("xn", [P, 2, D], F32, att)
        x16 = sb("x16", [P, 2, 2, 2 * D], F16, att)
        xt = sb("xt", [P, 2, 3, 2 * P], F16, att)
        qk = sb("qk", [P, 2, 2, 6, 2, 2, SEQ], F16, att)
        kimg = sb("kimg", [P, 2, 6, NI * IT], F16, att)
        v16 = sb("v16", [P, 2, 2, 2, HD], F16, att)
        vi = sb("vi", [P, 2, 2, 2, 4, 3, DH], F16, att)
        nm = sb("nm", [P, 2, 3], F32, att)
        p32 = sb("p32", [P, 2, 3, SEQ], F32, att)
        ph = sb("ph", [P, 2, 3, P], F16, att)
        pl = sb("pl", [P, 2, 3, P], F16, att)
        pi = sb("pi", [P, 2, 4, 2, IT], F16, att)
        pt = sb("pt", [P, 2, 7, P], F16, att)
        rs = sb("rs", [P, 2, 4, 3], F32, att)
        ri = sb("ri", [P, 6], F32, att)
        a32 = sb("a32", [P, 2, 6, DH], F32, att)
        a16 = sb("a16", [P, 2, 2, 2, HD], F16, att)
        at = sb("at", [P, 2, 2, 6, P], F16, att)
        h1 = sb("h1", [P, 2, D], F32, att)
        bst2 = sb("bst2", [P, 2, 6], F32, att)
        mv2 = sb("mv2", [P, 2, 2], F32, att)
        rstd2 = sb("rstd2", [P, 2], F32, att)
        xn2 = sb("xn2", [P, 2, D], F32, att)
        x2t = sb("x2t", [P, 3, 2 * P], F16, att)
        lg = sb("lg", [P, 2, NE], F32, att)
        mx = sb("mx", [P, 2, 8], F32, att)
        mi = sb("mi", [P, 2, 8], U32, att)
        dl = sb("dl", [P, 2, 8], F32, att)
        exr = sb("exr", [P, 2, 8], F32, att)
        sm = sb("sm", [P, 8], F32, att)
        pk = sb("pk", [P, 2, 2], F32, att)
        ix = sb("ix", [P, 2, 2], F32, att)
        oh = sb("oh", [P, 2, 2, NE], F32, att)
        ma = sb("ma", [P, 4, NE], F16, att)
        mb = sb("mb", [P, 4, NE], F16, att)
        c4 = sb("c4", [P, 4 * NE], F32, att)
        base = sb("base", [P, 2, NE], F32, att)
        pos = sb("pos", [P, 2, NE], F32, att)
        ohp = sb("ohp", [P, 2, 2, NE], F32, att)
        pk2 = sb("pk2", [P, 2, 2], F32, att)
        sl = sb("sl", [P, 2, 2], F32, att)
        ov = sb("ov", [P, 2, 2], F32, att)
        sli = sb("sli", [P, 2, 2], I32, att)
        rows = sb("rows", [P, 2, 2, ROW], I32, att)
        tid = sb("tid", [P, 2], F32, att)
        tb = sb("tb", [P, (NI + 1) * NE], F32, att)
        rimg = sb("rimg", [P, 4, ROW], I32, att)
        iximg = sb("iximg", [P, 4, 2], F32, att)
        ohimg = sb("ohimg", [P, 4, 2, NE], F32, att)
        mimg = sb("mimg", [P, 4, NE], F16, att)
        ipre = sb("ipre", [P, NI * NE], F32, att)
        cimg = sb("cimg", [P, 4, NE], F32, att)
        tidi = sb("tidi", [P, 4], F32, att)
        ppos = sb("ppos", [P, 4], F32, att)
        ppi = sb("ppi", [P, 8], F32, att)
        posa = sb("posa", [P, 4, NE], F32, att)
        ohpa = sb("ohpa", [P, 4, 2, NE], F32, att)
        pki = sb("pki", [P, 1], F32, att)
        pka = sb("pka", [P, 4, 2], F32, att)
        sla = sb("sla", [P, 4, 2], F32, att)
        ova = sb("ova", [P, 4, 2], F32, att)
        slia = sb("slia", [P, 4, 2], I32, att)
        selt = sb("selt", [P, 4, NE, 8], F32, att)

        names = """hin_ld hres_ld stat rst xna xnh x16r xtp xte pjd pjh pjl sd mxd exd phd phi pli pll ptd pta ptv pvd
            rid ond ash asl atp ata atv wod h1d st2 l2r l2n l2h l2l x2p x2e rtd dld erd mhd cud cpd sld sldi dspi dsp outd vil vst
            kcp kic lgd init chain pchain""".split()
        S = {n: sem(n) for n in names}
        names = "mchain w1d w2d b2d xld sel gtp gte w1hd w1ld w2hd w2ld f1d gld hhd hld f2d y1d y2d add".split()
        S.update({n: sem("m_" + n) for n in names})

        def load_w1(sp, n, place):
            wait(sp, "w1d", 16 * 4 * n)
            for b, parts in enumerate(KB):
                for r, p0, k in parts:
                    sp.dma_start(stage[p0:p0 + k, place, b * FF:(b + 1) * FF],
                                 w1[bass.ds(n, 1), r:r + k, :].rearrange("o r n -> (o r) n")).then_inc(S["w1d"], 16)

        def w1_hi(a, n, place, b):
            wait(a, "w1d", 16 * 4 * (n + 1))
            wait(a, "f1d", NQ * (n - 1))
            a.activation(w1h[:, place, b, :], stage[:, place, b * FF:(b + 1) * FF], ACT.Copy, scale=WS).then_inc(S["w1hd"], 1)

        def w1_lo(v, n, place, b):
            wait(v, "w1hd", 3 * n + b + 1)
            v.scalar_tensor_tensor(w1l[:, place, b, :], stage[:, place, b * FF:(b + 1) * FF], WS,
                                   w1h[:, place, b, :], ALU.mult, ALU.subtract).then_inc(S["w1ld"], 1)

        def isb(p):
            return not isinstance(p, int) or p >= NPAIR_A

        def wait(eng, name, v):
            if isinstance(v, int) and v <= 0:
                return
            eng.wait_ge(S[name], v)
            if eng is nc.sync and not isinstance(v, int):
                fixed(eng)

        def fixed(eng):
            eng.nop(nofuse=True)

        class Chain:
            def __init__(self, name):
                self.name, self.n = name, 0

            def done(self, ins):
                ins.then_inc(S[self.name], 1)
                self.n = self.n + 1
                return ins

            def here(self, eng):
                eng.wait_ge(S[self.name], self.n)

        SLOTS = 11
        LAG_T, LAG_V = 2, 3
        LO_EARLY = {1: 0, 2: 1, 3: 2, 4: 3, 6: 5, 7: 6, 8: 7, 9: 8}
        LO_LATE = {4: 4, 9: 9}

        SEND = {8: [(0, 0), (0, 1)], 9: [(1, 0)], 10: [(1, 1)]}

        def unit(u):
            return u // 4, u % 4

        def step_pe(pe, s, par, pre, pro, attn, post, place):
            pp, pa, pq = s, s - 1, s - 2
            qpar, apar = par, 1 - par

            def item(k):
                bank = pj[k % 2]
                if k == 0:
                    wait(pe, "xte", pp + 1)
                else:
                    wait(pe, "pjl", 10 * pp + k - 1)
                if k < 6:
                    for t in range(2):
                        c = t * HD + k * P
                        for n, (w, b, e) in enumerate(TERMS):
                            mm = pe.matmul(bank[:, t * 256:(t + 1) * 256], (wqkvh, wqkvl)[w][:, b, c:c + P],
                                           xt[:, qpar, e, :], start=n == 0, stop=n == 4)
                else:
                    j, hf = divmod(k - 6, 2)
                    c = 2 * HD + hf * 384
                    for n, (w, b, e) in enumerate(TERMS):
                        mm = pe.matmul(bank[:, 0:384], xt[:, qpar, e, j * P:(j + 1) * P],
                                       (wqkvh, wqkvl)[w][:, b, c:c + 384], start=n == 0, stop=n == 4)
                mm.then_inc(S["pjd"], 1)

            def transpose_x(p):
                wait(pe, "x16r", p + 1)
                wait(pe, "pjl", 10 * pp + 9)
                for j in range(2):
                    for b in range(3):
                        mm = pe.transpose(pjh[0][:, (3 * j + b) * P:(3 * j + b + 1) * P],
                                          x16[:, apar, j, b * P:(b + 1) * P], ident[:, :])
                mm.then_inc(S["xtp"], 1)

            for k in range(SLOTS):
                if attn and k < UNITS:
                    j, g = unit(k)
                    bank = sps[k % 2]
                    if k == 0:
                        wait(pe, "pjl", 10 * pa + 10)
                        if isb(pa):
                            wait(pe, "kic", 2 * (pa - 2) + 2)
                    wait(pe, "exd", 8 * pa + k - 1)
                    lo, n = (0, SEQ) if isb(pa) else (IT, P)
                    bk = bank[:, 0:3 * SEQ].rearrange("p (r c) -> p r c", r=3)[:, :, lo:SEQ]
                    pe.matmul(bk, identb[:, :], (maskt if isb(pa) else maski)[:, :, :], start=True, stop=False)
                    r0 = 64 * (g % 2)
                    for r in range(3):
                        m = 3 * (g // 2) + r
                        q = [qk[r0:r0 + 64, apar, z, m, 0, j, IT:SEQ] for z in range(2)]
                        kk = [qk[r0:r0 + 64, apar, z, m, 1, j, lo:SEQ] for z in range(2)]
                        o = bank[:, r * SEQ + lo:(r + 1) * SEQ]
                        pe.matmul(o, q[0], kk[0], start=False, stop=False)
                        pe.matmul(o, q[0], kk[1], start=False, stop=False)
                        mm = pe.matmul(o, q[1], kk[0], start=False, stop=r == 2)
                    mm.then_inc(S["sd"], 1)
                if pro and k < 10:
                    item(k)
                if pre and k == 10:
                    transpose_x(s + 1)
                if attn and LAG_T <= k < LAG_T + UNITS:
                    u = k - LAG_T
                    bank = ptp[u % 2]
                    wait(pe, "pll", 8 * pa + u + 1)
                    wait(pe, "pta" if u % 2 else "ptv", 4 * pa + u // 2)
                    for r in range(3):
                        pe.transpose(bank[:, r * P:(r + 1) * P], ph[:, u % 2, r, :], ident[:, :])
                        mm = pe.transpose(bank[:, (3 + r) * P:(4 + r) * P], pl[:, u % 2, r, :], ident[:, :])
                    if isb(pa):
                        mm = pe.transpose(bank[:, 6 * P:7 * P], pi[:, u % 2, :, :, :].rearrange("p r t c -> p (r t c)"),
                                          ident[:, :])
                    mm.then_inc(S["ptd"], 1)
                if place and k == 2:
                    count_pe(pe, s - 3)
                if post:
                    post_pe(pe, k, pq, 1 - apar)
                if attn and LAG_V <= k:
                    u = k - LAG_V
                    j, g = unit(u)
                    wait(pe, "pta" if u % 2 else "ptv", 4 * pa + u // 2 + 1)
                    if u % 2 == 0:
                        wait(pe, "ond", 4 * pa + u // 2)
                    if u == 0 and place:
                        wait(pe, "cpd", s - 2)
                    if u == 0 and isb(pa):
                        wait(pe, "vil", 16 * 12 * (pa - 1))
                    z = u % 2 * 192
                    if isb(pa):
                        for w in range(2):
                            mm = pe.matmul(ops[:, z:z + 192], pt[:, u % 2, 6, :],
                                           vi[:, apar, j, w, g, :, :].rearrange("p r d -> p (r d)"), start=w == 0, stop=False)
                    for r in range(3):
                        o = ops[:, z + r * DH:z + (r + 1) * DH]
                        c = g * 192 + r * DH
                        st = not isb(pa)
                        pe.matmul(o, pt[:, u % 2, r, :], v16[:, apar, j, 0, c:c + DH], start=st, stop=False)
                        pe.matmul(o, pt[:, u % 2, r, :], v16[:, apar, j, 1, c:c + DH], start=False, stop=False)
                        mm = pe.matmul(o, pt[:, u % 2, 3 + r, :], v16[:, apar, j, 0, c:c + DH], start=False,
                                       stop=st or r == 2)
                    mm.then_inc(S["pvd"], 1)

        def post_pe(pe, k, p, par):
            if k < 4:
                j, z = divmod(k, 2)
                if k == 0:
                    wait(pe, "lgd", p)
                else:
                    wait(pe, "atv" if k == 2 else "ata", 2 * p + (k + 1) // 2)
                wait(pe, "asl", 4 * p + 2 * j + 2)
                for c in range(6):
                    mm = pe.transpose(poh[:, c * P:(c + 1) * P], a16[:, par, j, z, c * P:(c + 1) * P], ident[:, :])
                mm.then_inc(S["atp"], 1)
            if k == 4:
                wait(pe, "atv", 2 * p + 2)
                for j in range(2):
                    n = 0
                    for c in range(6):
                        for z, w in ((0, woh), (0, wol), (1, woh)):
                            mm = pe.matmul(po[:, j * D:(j + 1) * D], at[:, j, z, c, :], w[:, c, :], start=n == 0, stop=n == 17)
                            n += 1
                mm.then_inc(S["wod"], 1)
            if k == 8:
                wait(pe, "h1d", p + 1)
                wait(pe, "l2l", p + 1)
                for j in range(2):
                    for b in range(3):
                        mm = pe.transpose(poh[:, (3 * j + b) * P:(3 * j + b + 1) * P], x2_of(p)[:, j, b * P:(b + 1) * P], ident[:, :])
                mm.then_inc(S["x2p"], 1)
            if k == 9:
                wait(pe, "x2e", p + 1)
                for j in range(2):
                    for n, (w, b, e) in enumerate(TERMS):
                        mm = pe.matmul(po[:, j * NE:(j + 1) * NE], x2t[:, e, j * P:(j + 1) * P], (wrh, wrl)[w][:, b, :],
                                       start=n == 0, stop=n == 4)
                mm.then_inc(S["rtd"], 1)

        def count_pe(pe, p):
            wait(pe, "mhd", p + 1)
            wait(pe, "ond", 4 * (min(p + 2, NPAIR) if isinstance(p, int) else p + 2))
            if isb(p):
                cc = ops[:, 0:4 * NE]
                pe.matmul(cc, tri[:, :], ma[:, :, :].rearrange("p a e -> p (a e)"), start=True, stop=False)
                mm = pe.matmul(cc, ones[:, :], mb[:, :, :].rearrange("p a e -> p (a e)"), start=False, stop=True)
            elif p == 0:
                mm = pe.matmul(ops[:, 0:NE], ident[:, :], mimg[:, 0, :], start=True, stop=True)
            else:
                im = mimg[:, :, :].rearrange("p t e -> p (t e)")
                pe.matmul(ops[:, 0:32], tri[:, :], im, start=True, stop=True)
                for q in range(8):
                    mm = pe.matmul(ops[:, 32 * (q + 1):32 * (q + 2)], rowmask[:, q, :], im, start=True, stop=True)
            mm.then_inc(S["cud"], 1)

        def step_dve(v, ch, s, par, pre, pro, attn, post, place):
            pp, pa, pq, pr = s, s - 1, s - 2, s - 3
            apar = 1 - par

            def norm(b):
                j, hb = divmod(b, 2)
                wait(v, "pvd", 8 * pa + 2 * b + 2)
                wait(v, "exd", 8 * pa + 2 * b + 2)
                wait(v, "asl", 4 * pa + b - 1)
                wait(v, "ond", 4 * pa + b)
                v.reciprocal(ri[:, :], rs[:, j, 2 * hb:2 * hb + 2, :].rearrange("p g r -> p (g r)")).then_inc(S["rid"], 1)
                wait(v, "rid", 4 * pa + b + 1)
                v.tensor_tensor(a32[:, b % 2, :, :], ops[:, 0:384].rearrange("p (h d) -> p h d", h=6),
                                ri[:, :].unsqueeze(2).broadcast_to((P, 6, DH)), ALU.mult).then_inc(S["ond"], 1)

            def proj_lo(n):
                wait(v, "pjh", 10 * pp + n + 1)
                bank = pj[n % 2]
                if n < 6:
                    v.scalar_tensor_tensor(qk[:, par, 1, n, :, :, IT:SEQ], bank[:, :].rearrange("p (t j c) -> p t j c", t=2, j=2),
                                           1.0 / WS, qk[:, par, 0, n, :, :, IT:SEQ], ALU.mult, ALU.subtract).then_inc(S["pjl"], 1)
                else:
                    j, hf = divmod(n - 6, 2)
                    v.scalar_tensor_tensor(v16[:, par, j, 1, hf * 384:(hf + 1) * 384], bank[:, 0:384], 1.0 / WS,
                                           v16[:, par, j, 0, hf * 384:(hf + 1) * 384], ALU.mult, ALU.subtract).then_inc(S["pjl"], 1)

            if isinstance(s, int) and s == 2:
                wait(v, "init", 1)
            for k in range(SLOTS + 1):
                if attn and k < UNITS:
                    wait(v, "sd", 8 * pa + k + 1)
                    wait(v, "exd", 8 * pa + k - 1)
                    lo = 0 if isb(pa) else IT
                    v.tensor_reduce(nm[:, k % 2, :], sps[k % 2][:, 0:3 * SEQ].rearrange("p (r c) -> p r c", r=3)[:, :, lo:SEQ],
                                    X, ALU.max, negate=True).then_inc(S["mxd"], 1)
                if attn and k >= 5 and k % 2 == 1:
                    norm((k - 5) // 2)
                if attn and 1 <= k <= UNITS:
                    u = k - 1
                    wait(v, "exd", 8 * pa + u + 1)
                    wait(v, "ptd", 8 * pa + u - 1)
                    v.tensor_copy(ph[:, u % 2, :, :], p32[:, u % 2, :, IT:SEQ]).then_inc(S["phd"], 1)
                    if isb(pa):
                        v.tensor_copy(pi[:, u % 2, 0:3, 0, :], p32[:, u % 2, :, 0:IT]).then_inc(S["phi"], 1)
                if pro and k in LO_EARLY:
                    proj_lo(LO_EARLY[k])
                if attn and LAG_T <= k < LAG_T + UNITS and k % 2 == 0:
                    u = k - LAG_T
                    wait(v, "ptd", 8 * pa + u + 1)
                    wait(v, "pvd", 8 * pa + u - 1)
                    evac_pt(v.tensor_copy, pa, u).then_inc(S["ptv"], 1)
                if pro and not isb(pp) and k == 9:
                    wait(v, "pjl", 10 * pp + 6)
                    for z in range(2):
                        v.tensor_copy(kimg[:, z, :, 256 * pp:256 * (pp + 1)].rearrange("p m (j c) -> p m j c", j=2),
                                      qk[:, par, z, :, 1, :, IT:SEQ]).then_inc(S["kcp"], 1)
                if pre and k == 2:
                    p = s + 1
                    wait(v, "hin_ld", 16 * (p + 1))
                    wait(v, "xna", 2 * p)
                    for j in range(2):
                        ch.done(v.bn_stats(bst[:, j, :], hin[:, (par + 1) % 2, j, :]))
                    ch.here(v)
                    fixed(v)
                    for j in range(2):
                        v.bn_aggr(mv[:, j, :], bst[:, j, :]).then_inc(S["stat"], 1)
                if pre and k == 4:
                    scaled(v, hin[:, (par + 1) % 2], mv, rstd, xn, s + 1, "rst", "x16r", "xna")
                if pro and k in LO_LATE:
                    proj_lo(LO_LATE[k])
                if post:
                    post_dve(v, ch, k, pq)
                if place and k < 8:
                    place_dve(v, ch, pr, k)
                if k == 10 and isinstance(s, int) and s == NPAIR - 1:
                    place_images(v, ch, 0, 3)

        def evac_pt(f, pa, u):
            n = 7 if isb(pa) else 6
            return f(pt[:, u % 2, 0:n, :], ptp[u % 2][:, 0:n * P].rearrange("p (n c) -> p n c", n=n))

        def post_dve(v, ch, k, p):
            if k in (1, 3):
                wait(v, "atp", 4 * p + k + 1)
                v.tensor_copy(at[:, k // 2, 1, :, :], poh[:, 0:6 * P].rearrange("p (c q) -> p c q", c=6)).then_inc(S["atv"], 1)
            if k == 5:
                wait(v, "wod", p + 1)
                wait(v, "hres_ld", 16 * (p + 1))
                wait(v, "outd", 32 * p)
                wait(v, "l2n", 2 * p)
                v.scalar_tensor_tensor(h1[:, :, :], po[:, 0:2 * D].rearrange("p (j n) -> p j n", j=2), 1.0 / WS, hres[:, PAR[0], :, :],
                                       ALU.mult, ALU.add).then_inc(S["h1d"], 1)
                wait(v, "h1d", p + 1)
                for j in range(2):
                    ch.done(v.bn_stats(bst2[:, j, :], h1[:, j, :]))
                ch.here(v)
                fixed(v)
                for j in range(2):
                    v.bn_aggr(mv2[:, j, :], bst2[:, j, :]).then_inc(S["st2"], 1)
            if k == 6:
                scaled(v, h1, mv2, rstd2, xn2, p, "l2r", "l2l", "l2n")
            if k == 9:
                wait(v, "rtd", p + 1)
                v.tensor_scalar(lg[:, :, :], po[:, 0:2 * NE].rearrange("p (j e) -> p j e", j=2), 1.0 / RS, None, ALU.mult).then_inc(S["lgd"], 1)
            if k == 10:
                wait(v, "lgd", p + 1)
                fixed(v)
                for j in range(2):
                    ch.done(v.max(mx[:, j, :], lg[:, j, :]))
            if k == 11:
                ch.here(v)
                fixed(v)
                for j in range(2):
                    ch.done(v.max_index(mi[:, j, :], mx[:, j, :], lg[:, j, :]))
                wait(v, "erd", p)
                v.tensor_tensor(dl[:, :, :], mx[:, :, :], mx[:, :, 0:1].broadcast_to((P, 2, 8)), ALU.subtract).then_inc(S["dld"], 1)

        def place_dve(v, ch, p, k):
            B = isb(p)
            t0 = None if B else 2 * p
            oht = oh[:, :, :, :] if B else ohimg[:, t0:t0 + 2, :, :]
            ixt = ix[:, :, :] if B else iximg[:, t0:t0 + 2, :]
            r_ = rows[:, 1 - PAR[0], :, :] if B else rimg[:, t0:t0 + 2, :]
            ch.here(v)
            if k == 0:
                ch.done(v.tensor_copy(ixt, mi[:, :, 0:2]))
                wait(v, "erd", p + 1)
                ch.done(v.tensor_reduce(sm[:, 0:2], exr[:, :, :], X, ALU.add))
            if k == 1:
                ch.done(v.tensor_tensor(oht, iota8[:, :].unsqueeze(1).unsqueeze(1).broadcast_to((P, 2, 2, NE)),
                                        ixt.unsqueeze(3).broadcast_to((P, 2, 2, NE)), ALU.is_equal))
                ch.done(v.reciprocal(sm[:, 2:4], sm[:, 0:2]))
                ch.here(v)
                if B:
                    wait(v, "cud", p)
                    ch.done(v.tensor_tensor(ma[:, 0:2, :], oht[:, :, 0, :], oht[:, :, 1, :], ALU.add))
                    ch.here(v)
                    ch.done(v.tensor_copy(mb[:, 1:3, :], ma[:, 0:1, :].broadcast_to((P, 2, NE))))
                    v.tensor_tensor(mb[:, 3, :], ma[:, 0, :], ma[:, 1, :], ALU.add).then_inc(S["mhd"], 1)
                else:
                    v.tensor_tensor(mimg[:, t0:t0 + 2, :], oht[:, :, 0, :], oht[:, :, 1, :], ALU.add).then_inc(S["mhd"], 1)
            if k == 2:
                if B:
                    ch.done(v.tensor_tensor(base[:, :, :], ipre[:, bass.ds(2 * (p - 2) * NE, 2 * NE)].rearrange("p (a e) -> p a e", a=2),
                                            tb[:, bass.ds(2 * (p - 2) * NE, NE)].unsqueeze(1).broadcast_to((P, 2, NE)), ALU.add))
                ch.done(v.tensor_tensor(pk[:, :, :], exr[:, :, 0:2], sm[:, 2:4].unsqueeze(2).broadcast_to((P, 2, 2)), ALU.mult))
                wait(v, "cud", p + 1)
                if B:
                    v.tensor_copy(c4[:, :], ops[:, 0:4 * NE]).then_inc(S["cpd"], 1)
                elif p == 0:
                    v.tensor_copy(cimg[:, 0, :], ops[:, 0:NE]).then_inc(S["cpd"], 1)
                else:
                    ch.done(v.tensor_copy(ipre[:, :].rearrange("p (t j e) -> p t j e", t=4, j=8),
                                          ops[:, 32:288].rearrange("p (j t e) -> p t j e", j=8, t=4)))
                    wait(v, "cpd", 1)
                    ch.here(v)
                    v.tensor_copy(cimg[:, :, :], ops[:, 0:32].rearrange("p (t e) -> p t e", t=4)).then_inc(S["cpd"], 1)
            if k == 3:
                ch.done(v.tensor_reduce(sm[:, 4:6], pk[:, :, :], X, ALU.add))
                wait(v, "cpd", p + 1)
                if B:
                    cur = tb[:, bass.ds(2 * (p - 2) * NE, NE)].unsqueeze(1).broadcast_to((P, 2, NE))
                    ch.here(v)
                    cc = c4[:, :].rearrange("p (a e) -> p a e", a=4)
                    ch.done(v.tensor_tensor(pos[:, :, :], cc[:, 0:2, :], base[:, :, :], ALU.add))
                    ch.done(v.tensor_tensor(tb[:, bass.ds((2 * (p - 2) + 1) * NE, 2 * NE)].rearrange("p (a e) -> p a e", a=2),
                                            cc[:, 2:4, :], cur, ALU.add))
            if k == 4:
                ch.done(v.reciprocal(sm[:, 6:8], sm[:, 4:6]))
                if B:
                    ch.done(v.tensor_tensor(ohp[:, :, :, :], oh[:, :, :, :], pos[:, :, :].unsqueeze(2).broadcast_to((P, 2, 2, NE)), ALU.mult))
                ch.here(v)
                if B:
                    wait(v, "dsp", 64 * (p - 3))
                ch.done(v.tensor_tensor(r_[:, :, WC:WC + 2].bitcast(F32), pk[:, :, :], sm[:, 6:8].unsqueeze(2).broadcast_to((P, 2, 2)), ALU.mult))
                ch.done(v.tensor_copy(r_[:, :, EC].bitcast(F32), ixt[:, :, 0]))
                if B:
                    ch.done(v.tensor_copy(r_[:, :, TC], tid[:, :]))
            if k == 5 and B:
                ch.done(v.tensor_reduce(pk2[:, :, :], ohp[:, :, :, :], X, ALU.add))
            if k == 6 and B:
                ch.done(v.tensor_scalar(tid[:, :], tid[:, :], float(2 * SEQ), None, ALU.add))
                ch.done(v.scalar_tensor_tensor(sl[:, :, :], ix[:, :, :], float(CAP), pk2[:, :, :], ALU.mult, ALU.add))
                ch.done(v.tensor_scalar(ov[:, :, :], pk2[:, :, :], float(CAP), 65536.0, ALU.is_ge, ALU.mult))
            if k == 7 and B:
                wait(v, "dsp", 64 * (p - 2))
                v.tensor_tensor(sli[:, :, :], sl[:, :, :], ov[:, :, :], ALU.add).then_inc(S["sld"], 1)
            if k == 6 and not B and p == 1:
                ip = ipre[:, :].rearrange("p (t j e) -> p t j e", t=4, j=8)
                for t in range(1, 4):
                    tot = ipre[:, (8 * t - 1) * NE:8 * t * NE]
                    ch.here(v)
                    ch.done(v.tensor_tensor(cimg[:, t, :], cimg[:, t, :], tot, ALU.add))
                    ch.done(v.tensor_tensor(ip[:, t], ip[:, t], tot.unsqueeze(1).broadcast_to((P, 8, NE)), ALU.add))

        def place_images(v, ch, a, b):
            n, t = b - a, slice(a, b)
            if a == 0:
                ch.done(v.tensor_tensor(ppi[:, :], seli[:, :], iota8[:, :], ALU.mult))
                ch.here(v)
                ch.done(v.tensor_reduce(pki[:, 0:1], ppi[:, :], X, ALU.add))
                ch.here(v)
                ch.done(v.scalar_tensor_tensor(tidi[:, :], pki[:, 0:1].broadcast_to((P, 4)), float(SEQ - IT), ppos[:, :], ALU.mult, ALU.add))
            ch.done(v.tensor_tensor(selt[:, t, :, :], tb[:, 8 * a * NE:8 * b * NE].rearrange("p (t j e) -> p t e j", t=n, j=8),
                                    seli[:, :].unsqueeze(1).unsqueeze(1).broadcast_to((P, n, NE, 8)), ALU.mult))
            ch.here(v)
            ch.done(v.tensor_reduce(posa[:, t, :], selt[:, t, :, :], X, ALU.add))
            ch.done(v.tensor_copy(rimg[:, t, TC], tidi[:, t]))
            ch.here(v)
            ch.done(v.tensor_tensor(posa[:, t, :], posa[:, t, :], cimg[:, t, :], ALU.add))
            ch.here(v)
            ch.done(v.tensor_tensor(ohpa[:, t, :, :], ohimg[:, t, :, :], posa[:, t, :].unsqueeze(2).broadcast_to((P, n, 2, NE)), ALU.mult))
            ch.here(v)
            ch.done(v.tensor_reduce(pka[:, t, :], ohpa[:, t, :, :], X, ALU.add))
            ch.here(v)
            ch.done(v.scalar_tensor_tensor(sla[:, t, :], iximg[:, t, :], float(CAP), pka[:, t, :], ALU.mult, ALU.add))
            ch.done(v.tensor_scalar(ova[:, t, :], pka[:, t, :], float(CAP), 65536.0, ALU.is_ge, ALU.mult))
            ch.here(v)
            v.tensor_tensor(slia[:, t, :], sla[:, t, :], ova[:, t, :], ALU.add).then_inc(S["sldi"], 1)

        def send_image(g, t, kk):
            g.indirect_dma_start(xg_d, bass.IndirectOffsetOnAxis(ap=slia[:, t, kk:kk + 1], axis=0), rimg[:, t, :], None,
                                 bounds_check=NE * CAP - 1, oob_is_err=False).then_inc(S["dspi"], 16)

        PAR = [0]

        def step_act(a, s, par, pre, pro, attn, post, place):
            pp, pa, pq = s, s - 1, s - 2
            for k in range(SLOTS + 1):
                if attn and k < UNITS:
                    j, g = unit(k)
                    wait(a, "mxd", 8 * pa + k + 1)
                    wait(a, "pll", 8 * pa + k - 1)
                    if k % 2 == 0:
                        wait(a, "rid", 4 * (pa - 1) + k // 2 + 1)
                    lo = 0 if isb(pa) else IT
                    for r in range(3):
                        i = a.activation(p32[:, k % 2, r, lo:SEQ], sps[k % 2][:, r * SEQ + lo:(r + 1) * SEQ], ACT.Exp,
                                         bias=nm[:, k % 2, r:r + 1], accum_out=rs[:, j, g, r:r + 1])
                    i.then_inc(S["exd"], 1)
                if pre and isb(s + 1) and k == 9:
                    wait(a, "sd", 8 * s)
                    if isinstance(s, int) and s + 1 == NPAIR_A:
                        wait(a, "kcp", 2 * NPAIR_A)
                    for j in range(2):
                        a.activation(qk[:, 1 - par, :, :, 1, j, 0:IT], kimg[:, :, :, bass.ds((2 * (s + 1 - NPAIR_A) + j) * IT, IT)],
                                     ACT.Copy).then_inc(S["kic"], 1)
                if pre and k == 10:
                    wait(a, "xtp", s + 2)
                    a.activation(xt[:, 1 - par, :, :].rearrange("p b (j c) -> p j b c", j=2),
                                 pjh[0][:, 0:6 * P].rearrange("p (j b c) -> p j b c", j=2, b=3), ACT.Copy).then_inc(S["xte"], 1)
                if pro and k < 10:
                    n = k
                    wait(a, "pjd", 10 * pp + n + 1)
                    bank = pj[k % 2]
                    if k == 0:
                        wait(a, "sd", 8 * (pp - 1))
                        if isinstance(pp, int) and 2 <= pp < 4:
                            wait(a, "kcp", 2 * (pp - 1))
                            wait(a, "vst", 32 * (pp - 1))
                    if k == 6:
                        wait(a, "pvd", 8 * (pp - 1))
                    if k < 6:
                        a.activation(qk[:, par, 0, n, :, :, IT:SEQ], bank[:, :].rearrange("p (t j c) -> p t j c", t=2, j=2),
                                     ACT.Copy, scale=1.0 / WS).then_inc(S["pjh"], 1)
                    else:
                        j, hf = divmod(k - 6, 2)
                        a.activation(v16[:, par, j, 0, hf * 384:(hf + 1) * 384], bank[:, 0:384], ACT.Copy,
                                     scale=1.0 / WS).then_inc(S["pjh"], 1)
                if attn and LAG_T <= k < LAG_T + UNITS and k % 2 == 1:
                    u = k - LAG_T
                    wait(a, "ptd", 8 * pa + u + 1)
                    wait(a, "pvd", 8 * pa + u - 1)
                    evac_pt(lambda o, i: a.activation(o, i, ACT.Copy), pa, u).then_inc(S["pta"], 1)
                if attn and k >= 5 and k % 2 == 1:
                    b = (k - 5) // 2
                    j, hb = divmod(b, 2)
                    wait(a, "ond", 4 * pa + b + 1)
                    if b == 0:
                        wait(a, "atp", 4 * (pa - 1))
                    a.activation(a16[:, 1 - par, j, 0, hb * 384:(hb + 1) * 384].rearrange("p (h d) -> p h d", h=6),
                                 a32[:, b % 2, :, :], ACT.Copy).then_inc(S["ash"], 1)
                if pre and k == 5:
                    wait(a, "xna", 2 * (s + 1) + 2)
                    wait(a, "xtp", s)
                    a.activation(x16[:, 1 - par, :, 0:D], xn[:, :, :], ACT.Copy).then_inc(S["xnh"], 1)
                if post:
                    p = pq
                    if k in (0, 2):
                        wait(a, "atp", 4 * p + k + 1)
                        a.activation(at[:, k // 2, 0, :, :], poh[:, 0:6 * P].rearrange("p (c q) -> p c q", c=6), ACT.Copy).then_inc(S["ata"], 1)
                    if k == 6:
                        wait(a, "l2n", 2 * p + 2)
                        if isb(p):
                            wait(a, "dsp", 64 * (p - 3))
                        a.activation(x2_of(p)[:, :, 0:D], xn2[:, :, :], ACT.Copy).then_inc(S["l2h"], 1)
                    if k == 8:
                        wait(a, "x2p", p + 1)
                        a.activation(x2t[:, :, :].rearrange("p b (j c) -> p j b c", j=2),
                                     poh[:, 0:6 * P].rearrange("p (j b c) -> p j b c", j=2, b=3), ACT.Copy).then_inc(S["x2e"], 1)
                    if k == 11:
                        wait(a, "dld", p + 1)
                        a.activation(exr[:, :, :], dl[:, :, :], ACT.Exp).then_inc(S["erd"], 1)

        def inv_std(g, c, rstd_, mv_, var, name, p):
            wait(g, var, 2 * p + 2)
            fixed(g)
            c.done(g.tensor_scalar(rstd_, mv_[:, :, 1], EPS, None, ALU.add))
            c.here(g)
            g.tensor_tensor(rstd_, rstd_, halfc[:, 0:2], ALU.pow).then_inc(S[name], 1)

        def scaled(v, h_, mv_, rstd_, xn_, p, inv, split, name):
            wait(v, inv, p + 1)
            wait(v, split, p)
            fixed(v)
            for j in range(2):
                v.tensor_scalar(xn_[:, j, :], h_[:, j, :], mv_[:, j, 0:1], rstd_[:, j:j + 1], ALU.subtract, ALU.mult).then_inc(S[name], 1)

        def x2_of(p):
            return (rows[:, PAR[0], :, 0:D] if isb(p) else rimg[:, 2 * p:2 * p + 2, 0:D]).bitcast(F16)

        def step_pool(g, c, s, par, pre, pro, attn, post, place):
            pa, pq, pr = s - 1, s - 2, s - 3
            apar = 1 - par

            if isinstance(s, int) and s == 0:
                c.done(g.memset(vi[:, :, :, :, :, :, :], 0.0))
                c.done(g.memset(pi[:, :, :, :, :], 0.0))
                c.done(g.memset(tb[:, :], 0.0))
                c.done(g.memset(ma[:, :, :], 0.0))
                c.done(g.memset(mb[:, :, :], 0.0))
                c.done(g.iota(tid[:, :], pattern=[[SEQ, 2]], base=IT, channel_multiplier=1, allow_small_or_imprecise_dtypes=True))
                c.done(g.iota(ppos[:, :], pattern=[[8 * SEQ, 4]], base=0, channel_multiplier=1, allow_small_or_imprecise_dtypes=True))
                c.here(g)
                g.memset(ppi[:, :], 0.0).then_inc(S["init"], 1)

            def split_a(b):
                j, hb = divmod(b, 2)
                wait(g, "ash", 4 * pa + b + 1)
                dst = [a16[:, apar, j, z, hb * 384:(hb + 1) * 384].rearrange("p (h d) -> p h d", h=6) for z in range(2)]
                g.tensor_tensor(dst[1], a32[:, b % 2, :, :], dst[0], ALU.subtract).then_inc(S["asl"], 1)

            for k in range(SLOTS + 1):
                if attn and 1 <= k <= UNITS:
                    u = k - 1
                    wait(g, "phd", 8 * pa + u + 1)
                    if isb(pa):
                        wait(g, "phi", 8 * (pa - 2) + u + 1)
                        g.tensor_tensor(pi[:, u % 2, 0:3, 1, :], p32[:, u % 2, :, 0:IT], pi[:, u % 2, 0:3, 0, :], ALU.subtract).then_inc(S["pli"], 1)
                        wait(g, "pli", 8 * (pa - 2) + u + 1)
                    g.tensor_tensor(pl[:, u % 2, :, :], p32[:, u % 2, :, IT:SEQ], ph[:, u % 2, :, :], ALU.subtract).then_inc(S["pll"], 1)
                if isinstance(s, int) and s == NPAIR and 2 <= k < 8:
                    if k == 2:
                        wait(g, "sldi", 1)
                    send_image(g, *divmod(k - 2, 2))
                if pre and k == 8:
                    x_ = x16[:, (par + 1) % 2]
                    wait(g, "xnh", s + 2)
                    g.tensor_tensor(x_[:, :, D:2 * D], xn[:, :, :], x_[:, :, 0:D], ALU.subtract).then_inc(S["x16r"], 1)
                if place and isb(pr) and k in SEND:
                    for j, kk in SEND[k]:
                        if (j, kk) == (0, 0):
                            wait(g, "sld", pr - 1)
                        fixed(g)
                        g.indirect_dma_start(xg_d, bass.IndirectOffsetOnAxis(ap=sli[:, j, kk:kk + 1], axis=0),
                                             rows[:, apar, j, :], None, bounds_check=NE * CAP - 1, oob_is_err=False).then_inc(S["dsp"], 16)
                if attn and k >= 5 and k % 2 == 1:
                    split_a((k - 5) // 2)
                if pre and k == 3:
                    inv_std(g, c, rstd[:, :], mv, "stat", "rst", s + 1)
                if post and k == 5:
                    inv_std(g, c, rstd2[:, :], mv2, "st2", "l2r", pq)
                if post and k == 6:
                    wait(g, "l2h", pq + 1)
                    x_ = x2_of(pq)
                    g.tensor_tensor(x_[:, :, D:2 * D], xn2[:, :, :], x_[:, :, 0:D], ALU.subtract).then_inc(S["l2l"], 1)

        def h_of(p):
            if isb(p):
                return txt[bass.ds(2 * (p - 2), 2)].rearrange("t p n -> p t n")
            return himg_d[256 * p:256 * (p + 1)].rearrange("(t p) n -> p t n", t=2)

        out_i = out[0:TOK, :].rearrange("(b s) n -> b s n", s=SEQ)

        def step_sp(sp, s, par, pre, pro, attn, post, place):
            pp, pq = s, s - 2
            if pre:
                p = s + 1
                wait(sp, "xna", 2 * (p - 1))
                wait(sp, "hin_ld", 16 * p)
                sp.dma_start(hin[:, (par + 1) % 2, :, :], h_of(p)).then_inc(S["hin_ld"], 16)
            if post:
                wait(sp, "h1d", pq - 1)
                wait(sp, "hres_ld", 16 * pq)
                sp.dma_start(hres[:, PAR[0], :, :], h_of(pq)).then_inc(S["hres_ld"], 16)
            if isinstance(s, int) and s == NPAIR - 1:
                load_w1(sp, 0, 0)
            if isinstance(s, int) and s == 2:
                wait(sp, "init", 1)
            if pro and isb(pp):
                wait(sp, "pvd", 8 * (pp - 1))
                wait(sp, "vil", 16 * 12 * (pp - 2))
                for j in range(2):
                    src = vimg_d[bass.ds((2 * (pp - 2) + j) * IT, IT)].rearrange("k z (g r d) -> k z g r d", g=4, r=3)
                    for r in range(3):
                        for t in range(2):
                            p0 = 32 * r + 16 * t
                            sp.dma_start(vi[p0:p0 + 16, par, j, :, :, r, :].rearrange("k z g d -> k (z g) d"),
                                         src[:, :, :, r, :].rearrange("k z g d -> k (z g) d")).then_inc(S["vil"], 16)
            if pro and not isb(pp):
                for j in range(2):
                    wait(sp, "pjl", 10 * pp + 8 + 2 * j)
                    r0 = 256 * pp + P * j
                    sp.dma_start(vimg_d[r0:r0 + P], v16[:, par, j, :, :]).then_inc(S["vst"], 16)
                if pp == 1:
                    sp.wait_ge(S["vst"], 64)
            if post:
                wait(sp, "h1d", pq + 1)
                for j in range(2):
                    if isb(pq):
                        dst = out_i[bass.ds(2 * (pq - 2) + j, 1), IT:SEQ, :].rearrange("o s n -> (o s) n")
                        sp.dma_start(dst, h1[:, j, :]).then_inc(S["outd"], 16)
                    else:
                        b0 = 8 * (2 * pq + j)
                        sp.dma_start(out_i[b0:b0 + 8, 0:IT, :], h1[:, j, :]).then_inc(S["outd"], 16)

        LOOP0, LOOP1 = 7, NPAIR - 1

        def stages(s):
            return dict(pre=0 <= s + 1 < NPAIR, pro=0 <= s < NPAIR, attn=0 <= s - 1 < NPAIR, post=0 <= s - 2 < NPAIR,
                        place=0 <= s - 3 < NPAIR)

        def run(eng, f, chain=None):
            for s in range(-1, LOOP0):
                n0 = chain.n if chain else 0
                PAR[0] = s % 2
                f(s, s % 2, stages(s))
            per = chain.n - n0 if chain else 0
            base = chain.n if chain else 0
            with eng.Fori(0, (LOOP1 - LOOP0) // 2) as i:
                for h in range(2):
                    if chain:
                        chain.n = (i * 2 + h) * per + base
                    PAR[0] = (LOOP0 + h) % 2
                    f(i * 2 + (LOOP0 + h), PAR[0], dict(pre=True, pro=True, attn=True, post=True, place=True))
            if chain:
                chain.n = base + per * (LOOP1 - LOOP0)
            for s in range(LOOP1, NPAIR + 3):
                PAR[0] = s % 2
                f(s, s % 2, stages(s))

        with nc.Block() as block:
            @block.sync
            def _(sp):
                run(sp, lambda s, par, st: step_sp(sp, s, par, **st))
                sp.wait_ge(S["outd"], 32 * NPAIR)

            @block.gpsimd
            def _(g):
                c = Chain("pchain")
                run(g, lambda s, par, st: step_pool(g, c, s, par, **st), c)
                g.wait_ge(S["sldi"], 2)
                for kk in range(2):
                    send_image(g, 3, kk)
                g.wait_ge(S["dsp"], 64 * (NPAIR - NPAIR_A))
                g.wait_ge(S["dspi"], 16 * 8)

            @block.scalar
            def _(a):
                run(a, lambda s, par, st: step_act(a, s, par, **st))
                for b in range(3):
                    w1_hi(a, 0, 0, b)

            @block.vector
            def _(v):
                ch = Chain("chain")
                run(v, lambda s, par, st: step_dve(v, ch, s, par, **st), ch)
                place_images(v, ch, 3, 4)
                for b in range(2):
                    w1_lo(v, 0, 0, b)

            @block.tensor
            def _(pe):
                run(pe, lambda s, par, st: step_pe(pe, s, par, **st))
        att.close()

        xg = sb("xg", [P, 2, NB, ROW], I32)
        xgt = sb("xgt", [P, 2, 3, CAP], F16)
        wsel = sb("wsel", [P, 2, 3, NB], F32)
        tok = sb("tok", [P, 2, NB, 1], I32)
        w2h = sb("w2h", [P, 2, 6, D], F16)
        w2l = sb("w2l", [P, 2, 6, D], F16)
        b2s = sb("b2s", [P, 2, D], F32)
        g32 = sb("g32", [P, 2, HALF], F32)
        h16 = sb("h16", [P, 2, 2, 6, CAP], F16)
        y1 = sb("y1", [P, 4, D], F32)
        y2 = sb("y2", [P, NB, D], F32)
        f1b = [pj[0], pj[1], ops]
        f2b = [po[:, :], ptp[0][:, :].bitcast(F32)]
        xtb = [b[:, :].bitcast(F16) for b in sps]
        NX = (NB + 1) // 2
        F2AT = {0: 0, 2: 1, 4: 2, 6: 3, 8: 4, 9: 5, 11: 6}
        PREP0 = 7

        def m_sp(sp, t, par, prep, one, two):
            if prep:
                n, place = t + 1, 1 - par
                e = bass.ds(n, 1)
                if one:
                    wait(sp, "w1hd", 3 * (n - 1))
                    wait(sp, "w1ld", 2 * (n - 1))
                    load_w1(sp, n, place)
                wait(sp, "xld", 32 * n)
                wait(sp, "gtp", NX * (n - 1))
                wait(sp, "sel", 4 * (n - 1))
                sp.dma_start(xg[:, place, 0:FB, :], xg_d[bass.ds(n * CAP, FB * P), :].rearrange("(b p) n -> p b n", p=P)).then_inc(S["xld"], 16)
                sp.dma_start(xg[0:CAP - FB * P, place, FB, :], xg_d[bass.ds(n * CAP + FB * P, CAP - FB * P), :]).then_inc(S["xld"], 16)
                wait(sp, "w2d", 16 * n)
                wait(sp, "w2hd", 2 * (n - 1))
                wait(sp, "w2ld", 2 * (n - 1))
                sp.dma_start(stage[:, place, 3 * FF:].rearrange("p (c n) -> p c n", n=D),
                             w2[e].rearrange("o (c p) n -> p (o c) n", p=P)).then_inc(S["w2d"], 16)
                wait(sp, "b2d", 16 * n)
                wait(sp, "y1d", NB * (n - 1))
                sp.dma_start(b2s[:, place, :], b2[e].broadcast_to((P, D))).then_inc(S["b2d"], 16)

        def m_pe(pe, t, par, prep, one, two):
            def rows_t(q):
                if q == 0:
                    wait(pe, "xld", 32 * (t + 2))
                wait(pe, "gte", NX * (t + 1) + q - 1)
                for b in range(2 * q, min(2 * q + 2, NB)):
                    for c in range(3):
                        o = xtb[q % 2][:, ((b % 2) * 3 + c) * P:((b % 2) * 3 + c) * P + BLK[b]]
                        mm = pe.transpose(o, xg[0:BLK[b], 1 - par, b, c * DH:(c + 1) * DH].bitcast(F16), ident[0:BLK[b], 0:BLK[b]])
                mm.then_inc(S["gtp"], 1)

            if one:
                wait(pe, "w1hd", 3 * (t + 1))
                wait(pe, "w1ld", 2 * (t + 1))
                wait(pe, "gte", NX * (t + 1))
            for q in range(NQ):
                if one:
                    m, hf = divmod(q, 2)
                    wait(pe, "gld", NQ * t + q - 2)
                    for n, (w, b, e) in enumerate(TERMS):
                        mm = pe.matmul(f1b[q % 3][:, 0:HALF], (w1h, w1l)[w][:, par, b, m * P:(m + 1) * P],
                                       xgt[:, par, e, hf * HALF:(hf + 1) * HALF], start=n == 0, stop=n == 4)
                    mm.then_inc(S["f1d"], 1)
                if two and q in F2AT:
                    u, tt, pr = F2AT[q], t - 1, 1 - par
                    if u == 0:
                        wait(pe, "hld", NQ * (tt + 1))
                        wait(pe, "w2hd", 2 * (tt + 1))
                        wait(pe, "w2ld", 2 * (tt + 1))
                    wait(pe, "y1d", NB * tt + u - (1 if u else 0))
                    n = 0
                    for c in range(6):
                        for z, w in ((0, w2h), (0, w2l), (1, w2h)):
                            mm = pe.matmul(f2b[u % 2][0:BLK[u], 0:D], h16[:, pr, z, c, u * P:u * P + BLK[u]], w[:, pr, c, :],
                                           start=n == 0, stop=n == 17)
                            n += 1
                    mm.then_inc(S["f2d"], 1)
                if prep and PREP0 <= q < PREP0 + NX:
                    rows_t(q - PREP0)

        def m_act(a, t, par, prep, one, two):
            for q in range(NQ):
                if one:
                    m, hf = divmod(q, 2)
                    wait(a, "f1d", NQ * t + q + 1)
                    wait(a, "hld", NQ * t + q - 1)
                    fixed(a)
                    a.activation(g32[:, q % 2, :], f1b[q % 3][:, 0:HALF], ACT.Gelu, bias=b1t[:, bass.ds(t * 6 + m, 1)],
                                 scale=1.0 / WS).then_inc(S["gld"], 1)
                    if q == 0:
                        wait(a, "f2d", NB * (t - 1))
                    wait(a, "gld", NQ * t + q + 1)
                    a.activation(h16[:, par, 0, m, hf * HALF:(hf + 1) * HALF], g32[:, q % 2, :], ACT.Copy).then_inc(S["hhd"], 1)
                if one and q in (1, 2):
                    c = 3 * (q - 1)
                    wait(a, "w2d", 16 * (t + 1))
                    wait(a, "f2d", NB * (t - 1))
                    a.activation(w2h[:, par, c:c + 3, :], stage[:, par, 3 * FF + c * D:3 * FF + (c + 3) * D]
                                 .rearrange("p (c n) -> p c n", n=D), ACT.Copy, scale=WS).then_inc(S["w2hd"], 1)
                if two and not one and q < NB:
                    u, n = q, BLK[q]
                    wait(a, "y1d", NB * (t - 1) + u + 1)
                    if u == 0:
                        wait(a, "sel", 4 * t)
                        wait(a, "add", 16 * NB * (t - 1))
                    a.activation(y2[0:n, u, :], y1[0:n, u % 4, :], ACT.Copy, scale=wsel[0:n, 1 - par, 2, u:u + 1]).then_inc(S["y2d"], 1)
                if prep and one and q in (4, 5, 6):
                    w1_hi(a, t + 1, 1 - par, q - 4)

        def m_dve(v, ch, t, par, prep, one, two):
            def rows_e(q):
                wait(v, "gtp", NX * (t + 1) + q + 1)
                for b in range(2 * q, min(2 * q + 2, NB)):
                    i = v.tensor_copy(xgt[:, 1 - par, :, b * P:b * P + BLK[b]],
                                      xtb[q % 2][:, (b % 2) * 3 * P:((b % 2) * 3 + 3) * P].rearrange("p (c n) -> p c n", c=3)[:, :, 0:BLK[b]])
                i.then_inc(S["gte"], 1)

            def choose():
                wait(v, "xld", 32 * (t + 1))
                wait(v, "add", 16 * NB * (t - 1))
                x_ = xg[:, par]
                wt = [x_[:, :, WC + z].bitcast(F32) for z in range(2)]
                fixed(v)
                parts = [(slice(0, P), slice(0, FB)), (slice(0, CAP - FB * P), slice(FB, NB))]
                for r, b in parts:
                    for z, op in ((0, ALU.is_equal), (1, ALU.not_equal)):
                        ch.done(v.scalar_tensor_tensor(wsel[r, par, z, b], x_[r, b, EC].bitcast(F32), iota8[r, bass.ds(t, 1)],
                                                       wt[z][r, b], op, ALU.mult))
                    v.tensor_copy(tok[r, par, b, 0], x_[r, b, TC]).then_inc(S["sel"], 1)
                ch.here(v)
                for r, b in parts:
                    v.tensor_tensor(wsel[r, par, 2, b], wsel[r, par, 0, b], wsel[r, par, 1, b], ALU.add).then_inc(S["sel"], 1)

            def second(u):
                tt, n = t - 1, BLK[u]
                wait(v, "f2d", NB * tt + u + 1)
                wait(v, "y2d", NB * tt + (u - 3 if u >= 4 else min(u - 2, 0)))
                if u == 0:
                    wait(v, "b2d", 16 * (tt + 1))
                v.scalar_tensor_tensor(y1[0:n, u % 4, :], f2b[u % 2][0:n, 0:D], 1.0 / WS, b2s[0:n, 1 - par, :], ALU.mult,
                                       ALU.add).then_inc(S["y1d"], 1)

            if prep and not one:
                for q in range(NX):
                    rows_e(q)
            for q in range(NQ):
                if one:
                    m, hf = divmod(q, 2)
                    wait(v, "hhd", NQ * t + q + 1)
                    c = slice(hf * HALF, (hf + 1) * HALF)
                    v.tensor_tensor(h16[:, par, 1, m, c], g32[:, q % 2, :], h16[:, par, 0, m, c], ALU.subtract).then_inc(S["hld"], 1)
                if one and q in (2, 3):
                    c = 3 * (q - 2)
                    wait(v, "w2hd", 2 * t + q - 1)
                    v.scalar_tensor_tensor(w2l[:, par, c:c + 3, :], stage[:, par, 3 * FF + c * D:3 * FF + (c + 3) * D]
                                           .rearrange("p (c n) -> p c n", n=D), WS, w2h[:, par, c:c + 3, :], ALU.mult,
                                           ALU.subtract).then_inc(S["w2ld"], 1)
                if prep and one and q in (5, 6):
                    w1_lo(v, t + 1, 1 - par, q - 5)
                if one and q == 4:
                    choose()
                if two and q - 1 in F2AT:
                    second(F2AT[q - 1])
                if prep and one and PREP0 <= q < PREP0 + NX:
                    rows_e(q - PREP0)
            if two:
                second(NB - 1)

        def m_pool(g, t, par, prep, one, two):
            if two:
                tt = t - 1
                for u, n in enumerate(BLK):
                    wait(g, "y1d", NB * tt + u + 1)
                    if u == 0:
                        wait(g, "sel", 4 * (tt + 1))
                        wait(g, "add", 16 * NB * tt)
                    fixed(g)
                    if one:
                        g.tensor_scalar(y2[0:n, u, :], y1[0:n, u % 4, :], wsel[0:n, 1 - par, 2, u:u + 1], None, ALU.mult).then_inc(S["y2d"], 1)
                    wait(g, "y2d", NB * tt + u + 1)
                    fixed(g)
                    g.indirect_dma_start(out, bass.IndirectOffsetOnAxis(ap=tok[0:n, 1 - par, u, :], axis=0),
                                         y2[0:n, u, :], None, compute_op=ALU.add).then_inc(S["add"], 16)

        def steps(eng, f, chain=None):
            f(-1, 1, True, False, False)
            f(0, 0, True, True, False)
            n0 = chain.n if chain else 0
            f(1, 1, True, True, True)
            base = chain.n if chain else 0
            per = base - n0
            with eng.Fori(0, NE // 2 - 2) as i:
                for h in range(2):
                    if chain:
                        chain.n = (i * 2 + h) * per + base
                    f(i * 2 + (2 + h), h, True, True, True)
            if chain:
                chain.n = base + per * (NE - 4)
            f(NE - 2, 0, True, True, True)
            f(NE - 1, 1, False, True, True)
            f(NE, 0, False, False, True)

        with nc.Block() as block:
            @block.sync
            def _(sp):
                steps(sp, lambda *a: m_sp(sp, *a))
                sp.wait_ge(S["add"], 16 * NB * NE)

            @block.gpsimd
            def _(g):
                steps(g, lambda *a: m_pool(g, *a))

            @block.scalar
            def _(a):
                steps(a, lambda *b: m_act(a, *b))

            @block.vector
            def _(v):
                ch = Chain("mchain")
                steps(v, lambda *a: m_dve(v, ch, *a), ch)

            @block.tensor
            def _(pe):
                steps(pe, lambda *a: m_pe(pe, *a))


INS = ["x", "txt", "L0_tok_ln_gamma", "L0_tok_ln_beta", "L0_tok_W", "L0_tok_b", "L0_attn_W_Q", "L0_attn_W_K", "L0_attn_W_V",
       "L0_attn_W_O", "L0_ffn_Wr", "L0_ffn_w1", "L0_ffn_b1", "L0_ffn_w2", "L0_ffn_b2"]


def kernel(**inputs):
    import numpy as np
    import concourse.bacc as bacc
    from concourse.bass_utils import run_bass_kernel_spmd

    nc = bacc.Bacc("TRN2", target_bir_lowering=False, num_devices=1)
    arrays, args = {}, []
    for name in INS:
        a = np.ascontiguousarray(inputs[name])
        arrays[f"in_{name}"] = a
        args.append(nc.dram_tensor(f"in_{name}", a.shape, mybir.dt.from_np(a.dtype), kind="ExternalInput").ap())
    out = nc.dram_tensor("out", (TOK + CAP, D), F32, kind="ExternalOutput").ap()
    build(nc, *args, out)
    r = run_bass_kernel_spmd(nc, [arrays], core_ids=[0])
    return r.results[0]["out"][:TOK].reshape(NI, SEQ, D)
```
